# Optimizing a Trainium2 kernel written in Bass

```python
import numpy as np
import jax
import jax.numpy as jnp

def _softmax(x, axis=-1):
    return jax.nn.softmax(x, axis=axis)

def _gelu(x):
    return jax.nn.gelu(x, approximate=True)

def _silu(x):
    return jax.nn.silu(x)

def _sigmoid(x):
    return jax.nn.sigmoid(x)

def _layernorm(x, axis=-1, eps=1e-05):
    m = jnp.mean(x, axis=axis, keepdims=True)
    v = jnp.var(x, axis=axis, keepdims=True)
    return (x - m) / jnp.sqrt(v + eps)

def _scatter_add(tgt, idx, src, axis=0):
    return tgt.at[idx].add(src)

def _segment_sum(src, seg, n):
    return jax.ops.segment_sum(src, seg, n)
kernel_name = 'mk_gnn_resnorm_d4_gnn_r32_106276'

def setup_inputs(seed: int=0):
    np.random.seed(seed)
    _w = jnp.asarray

    def _rec_inputs():
        import jax
        import jax.numpy as jnp
        _gk = jax.random.key(seed)
        x = -0.000202 + 1 * jax.random.normal(jax.random.fold_in(_gk, 1), (3125, 128), jnp.float32)
        _s = jax.random.randint(jax.random.fold_in(_gk, 2), (25000,), 0, 3125, jnp.int32)
        _d = jax.random.randint(jax.random.fold_in(_gk, 3), (25000,), 0, 3125, jnp.int32)
        _loop = jnp.arange(3125, dtype=jnp.int32)
        src = jnp.concatenate([_s, _d, _loop])
        dst = jnp.concatenate([_d, _s, _loop])
        _o = jnp.argsort(dst, stable=True)
        src = src[_o]
        dst = dst[_o]
        edge_attr_4 = 0.000398945 + 1.00003 * jax.random.normal(jax.random.fold_in(_gk, 12), (53125, 4), jnp.float32)
        edge_type_64 = jax.random.randint(jax.random.fold_in(_gk, 14), (53125,), 0, 64, jnp.int32)
        return (x, src, dst, edge_attr_4, edge_type_64)
    x, src, dst, edge_attr_4, edge_type_64 = _rec_inputs()

    def _L0_gnn_setup():
        import jax, jax.numpy as jnp
        import numpy as np
        N, F_IN, F_OUT, H, E = (50000, 128, 32, 4, 50000)
        key = jax.random.key(seed)
        ks = jax.random.split(key, 8)
        features = jax.random.normal(ks[0], (N, F_IN), dtype=jnp.float32)
        edge_src = jax.random.randint(ks[1], (E,), 0, N, dtype=jnp.int32)
        edge_dst = jax.random.randint(ks[2], (E,), 0, N, dtype=jnp.int32)
        W_w = jax.random.normal(ks[3], (F_IN, F_OUT * H), dtype=jnp.float32) * 0.05
        W_b = jax.random.normal(ks[4], (F_OUT * H,), dtype=jnp.float32) * 0.05
        a_w = jax.random.normal(ks[5], (H, 2 * F_OUT), dtype=jnp.float32) * 0.05
        a_b = jax.random.normal(ks[6], (H,), dtype=jnp.float32) * 0.05
        return {'features': features, 'edge_src': edge_src, 'edge_dst': edge_dst, 'W_w': W_w, 'W_b': W_b, 'a_w': a_w, 'a_b': a_b}
    _L0_gnn_all = _L0_gnn_setup()
    _L0_gnn_in = {k: v for k, v in _L0_gnn_all.items() if k in ('W_w', 'W_b', 'a_w', 'a_b')}
    del _L0_gnn_all

    def _L1_gnn_setup():
        import jax, jax.numpy as jnp
        import numpy as np
        N_NODES = 50000
        key = jax.random.key(seed)
        k1, k2, k3 = jax.random.split(key, 3)
        H = jax.random.normal(k1, (N_NODES, 128), dtype=jnp.float32)
        edge_index = jax.random.randint(k2, (2, 25000), 0, N_NODES, dtype=jnp.int64)
        W = jax.random.normal(k3, (128, 128), dtype=jnp.float32) * jnp.sqrt(2.0 / 128.0)
        return {'H': H, 'edge_index': edge_index, 'W': W}
    _L1_gnn_all = _L1_gnn_setup()
    _L1_gnn_in = {k: v for k, v in _L1_gnn_all.items() if k in ('W',)}
    del _L1_gnn_all

    def _L2_gnn_setup():
        import jax, jax.numpy as jnp
        import numpy as np
        N = 3125
        E = 50000
        IN_DIM = 128
        OUT_DIM = 128
        EDGE_DIM = 4
        LN_EPS = 1e-05
        key = jax.random.key(seed)
        ks = jax.random.split(key, 12)
        s_in = 1.0 / np.sqrt(IN_DIM)
        s_ed = 1.0 / np.sqrt(EDGE_DIM)
        s_out = 1.0 / np.sqrt(OUT_DIM)
        s_cat = 1.0 / np.sqrt(IN_DIM + OUT_DIM)
        return {'x': jax.random.normal(ks[0], (N, IN_DIM), jnp.float32), 'edge_index': jax.random.randint(ks[1], (2, E), 0, N, jnp.int32), 'edge_attr': jax.random.normal(ks[2], (E, EDGE_DIM), jnp.float32), 'agg_W': jax.random.uniform(ks[3], (IN_DIM, OUT_DIM), jnp.float32, -s_in, s_in), 'agg_b': jnp.zeros((OUT_DIM,), jnp.float32), 'edge_W1': jax.random.uniform(ks[4], (EDGE_DIM, OUT_DIM), jnp.float32, -s_ed, s_ed), 'edge_b1': jnp.zeros((OUT_DIM,), jnp.float32), 'edge_W2': jax.random.uniform(ks[5], (OUT_DIM, 1), jnp.float32, -s_out, s_out), 'edge_b2': jnp.zeros((1,), jnp.float32), 'upd_W1': jax.random.uniform(ks[6], (IN_DIM + OUT_DIM, OUT_DIM), jnp.float32, -s_cat, s_cat), 'upd_b1': jnp.zeros((OUT_DIM,), jnp.float32), 'upd_W2': jax.random.uniform(ks[7], (OUT_DIM, OUT_DIM), jnp.float32, -s_out, s_out), 'upd_b2': jnp.zeros((OUT_DIM,), jnp.float32), 'ln_g': jnp.ones((OUT_DIM,), jnp.float32), 'ln_b': jnp.zeros((OUT_DIM,), jnp.float32), 'res_W': jax.random.uniform(ks[8], (IN_DIM, OUT_DIM), jnp.float32, -s_in, s_in)}
    _L2_gnn_all = _L2_gnn_setup()
    _L2_gnn_in = {k: v for k, v in _L2_gnn_all.items() if k in ('agg_W', 'agg_b', 'edge_W1', 'edge_b1', 'edge_W2', 'edge_b2', 'upd_W1', 'upd_b1', 'upd_W2', 'upd_b2', 'ln_g', 'ln_b', 'res_W')}
    del _L2_gnn_all

    def _L3_gnn_setup():
        import jax, jax.numpy as jnp
        import numpy as np
        N_NODES = 3125
        N_EDGES = 18750
        HIDDEN = 128
        NUM_REL = 64
        key = jax.random.key(seed)
        ks = jax.random.split(key, 8)
        node_states = jax.random.normal(ks[0], (N_NODES, HIDDEN), dtype=jnp.float32)
        edge_index = jax.random.randint(ks[1], (2, N_EDGES), 0, N_NODES, dtype=jnp.int64)
        edge_type_ids = jax.random.randint(ks[2], (N_EDGES,), 0, NUM_REL, dtype=jnp.int64)
        s = 1.0 / np.sqrt(HIDDEN)
        W_self = jax.random.uniform(ks[3], (HIDDEN, HIDDEN), jnp.float32, -s, s)
        b_self = jax.random.uniform(ks[4], (HIDDEN,), jnp.float32, -s, s)
        W_msg = jax.random.uniform(ks[5], (HIDDEN, HIDDEN), jnp.float32, -s, s)
        b_msg = jax.random.uniform(ks[6], (HIDDEN,), jnp.float32, -s, s)
        rel_emb = jax.random.normal(ks[7], (NUM_REL, HIDDEN), dtype=jnp.float32)
        return {'node_states': node_states, 'edge_index': edge_index, 'edge_type_ids': edge_type_ids, 'W_self': W_self, 'b_self': b_self, 'W_msg': W_msg, 'b_msg': b_msg, 'rel_emb': rel_emb}
    _L3_gnn_all = _L3_gnn_setup()
    _L3_gnn_in = {k: v for k, v in _L3_gnn_all.items() if k in ('W_self', 'b_self', 'W_msg', 'b_msg', 'rel_emb')}
    del _L3_gnn_all
    return {'x': x, 'src': src, 'dst': dst, 'edge_attr_4': edge_attr_4, 'edge_type_64': edge_type_64, 'L0_gnn_W_w': _L0_gnn_in['W_w'], 'L0_gnn_W_b': _L0_gnn_in['W_b'], 'L0_gnn_a_w': _L0_gnn_in['a_w'], 'L0_gnn_a_b': _L0_gnn_in['a_b'], 'L1_gnn_W': _L1_gnn_in['W'], 'L2_gnn_agg_W': _L2_gnn_in['agg_W'], 'L2_gnn_agg_b': _L2_gnn_in['agg_b'], 'L2_gnn_edge_W1': _L2_gnn_in['edge_W1'], 'L2_gnn_edge_b1': _L2_gnn_in['edge_b1'], 'L2_gnn_edge_W2': _L2_gnn_in['edge_W2'], 'L2_gnn_edge_b2': _L2_gnn_in['edge_b2'], 'L2_gnn_upd_W1': _L2_gnn_in['upd_W1'], 'L2_gnn_upd_b1': _L2_gnn_in['upd_b1'], 'L2_gnn_upd_W2': _L2_gnn_in['upd_W2'], 'L2_gnn_upd_b2': _L2_gnn_in['upd_b2'], 'L2_gnn_ln_g': _L2_gnn_in['ln_g'], 'L2_gnn_ln_b': _L2_gnn_in['ln_b'], 'L2_gnn_res_W': _L2_gnn_in['res_W'], 'L3_gnn_W_self': _L3_gnn_in['W_self'], 'L3_gnn_b_self': _L3_gnn_in['b_self'], 'L3_gnn_W_msg': _L3_gnn_in['W_msg'], 'L3_gnn_b_msg': _L3_gnn_in['b_msg'], 'L3_gnn_rel_emb': _L3_gnn_in['rel_emb']}

def reference(x, src, dst, edge_attr_4, edge_type_64, L0_gnn_W_w, L0_gnn_W_b, L0_gnn_a_w, L0_gnn_a_b, L1_gnn_W, L2_gnn_agg_W, L2_gnn_agg_b, L2_gnn_edge_W1, L2_gnn_edge_b1, L2_gnn_edge_W2, L2_gnn_edge_b2, L2_gnn_upd_W1, L2_gnn_upd_b1, L2_gnn_upd_W2, L2_gnn_upd_b2, L2_gnn_ln_g, L2_gnn_ln_b, L2_gnn_res_W, L3_gnn_W_self, L3_gnn_b_self, L3_gnn_W_msg, L3_gnn_b_msg, L3_gnn_rel_emb):
    import jax
    import jax.numpy as jnp

    def _L0_gnn_ref(features, edge_src, edge_dst, W_w, W_b, a_w, a_b):
        import jax, jax.numpy as jnp
        import numpy as np
        N, F_IN, F_OUT, H, E = (50000, 128, 32, 4, 50000)
        n = features.shape[0]
        h = a_w.shape[0]
        f_out = a_w.shape[1] // 2
        self_idx = jnp.arange(n, dtype=edge_src.dtype)
        src = jnp.concatenate([edge_src, self_idx])
        dst = jnp.concatenate([edge_dst, self_idx])
        key = (features @ W_w + W_b).reshape(n, h, f_out)
        a_dst = a_w[:, :f_out]
        a_src = a_w[:, f_out:]
        s_dst = jnp.einsum('nhf,hf->nh', key, a_dst)
        s_src = jnp.einsum('nhf,hf->nh', key, a_src)
        e = jax.nn.leaky_relu(s_dst[dst] + s_src[src] + a_b, negative_slope=0.2)
        m = jax.ops.segment_max(e, dst, num_segments=n)
        e_exp = jnp.exp(e - m[dst])
        denom = jax.ops.segment_sum(e_exp, dst, num_segments=n)
        alpha = e_exp / denom[dst]
        out = jax.ops.segment_sum(alpha[:, :, None] * key[src], dst, num_segments=n)
        return out.reshape(n, h * f_out)

    def _L1_gnn_ref(H, edge_index, W):
        import jax, jax.numpy as jnp
        import numpy as np
        N_NODES = 50000
        src, dst = (edge_index[0], edge_index[1])
        new_H = jax.ops.segment_sum(H[src], dst, num_segments=H.shape[0])
        out = (H + new_H) @ W
        return jax.nn.relu(out)

    def _L2_gnn_ref(x, edge_index, edge_attr, agg_W, agg_b, edge_W1, edge_b1, edge_W2, edge_b2, upd_W1, upd_b1, upd_W2, upd_b2, ln_g, ln_b, res_W):
        import jax, jax.numpy as jnp
        import numpy as np
        N = 3125
        E = 50000
        IN_DIM = 128
        OUT_DIM = 128
        EDGE_DIM = 4
        LN_EPS = 1e-05
        n = x.shape[0]
        src, dst = (edge_index[0], edge_index[1])
        e_h = jax.nn.silu(edge_attr @ edge_W1 + edge_b1)
        e_w = jax.nn.sigmoid(e_h @ edge_W2 + edge_b2)
        x_agg = jax.nn.silu(x[src] @ agg_W + agg_b) * e_w
        out = jax.ops.segment_sum(x_agg, dst, num_segments=n)
        cnt = jax.ops.segment_sum(jnp.ones((dst.shape[0],), x.dtype), dst, num_segments=n)
        out = out / jnp.maximum(cnt, 1.0)[:, None]
        h = jnp.concatenate([x, out], axis=-1)
        h = jax.nn.silu(h @ upd_W1 + upd_b1) @ upd_W2 + upd_b2
        h = h + x @ res_W
        mu = jnp.mean(h, axis=-1, keepdims=True)
        var = jnp.mean(jnp.square(h - mu), axis=-1, keepdims=True)
        h = (h - mu) * jax.lax.rsqrt(var + LN_EPS) * ln_g + ln_b
        return h

    def _L3_gnn_ref(node_states, edge_index, edge_type_ids, W_self, b_self, W_msg, b_msg, rel_emb):
        import jax, jax.numpy as jnp
        import numpy as np
        N_NODES = 3125
        N_EDGES = 18750
        HIDDEN = 128
        NUM_REL = 64
        src = edge_index[0]
        dst = edge_index[1]
        n_nodes = node_states.shape[0]
        rel_ids = jnp.clip(edge_type_ids, 0, rel_emb.shape[0] - 1)
        rel_vec = rel_emb[rel_ids]
        msg = (node_states[src] + rel_vec) @ W_msg.T + b_msg
        agg = jax.ops.segment_sum(msg, dst, num_segments=n_nodes)
        deg = jax.ops.segment_sum(jnp.ones((dst.shape[0],), node_states.dtype), dst, num_segments=n_nodes)
        agg = agg / jnp.maximum(deg, 1.0)[:, None]
        return node_states @ W_self.T + b_self + agg
    edge_index = jnp.stack([src, dst])
    x = _layernorm(x + _L0_gnn_ref(x, src, dst, L0_gnn_W_w, L0_gnn_W_b, L0_gnn_a_w, L0_gnn_a_b), axis=-1)
    x = _layernorm(x + _L1_gnn_ref(x, edge_index, L1_gnn_W), axis=-1)
    x = _layernorm(x + _L2_gnn_ref(x, edge_index, edge_attr_4, L2_gnn_agg_W, L2_gnn_agg_b, L2_gnn_edge_W1, L2_gnn_edge_b1, L2_gnn_edge_W2, L2_gnn_edge_b2, L2_gnn_upd_W1, L2_gnn_upd_b1, L2_gnn_upd_W2, L2_gnn_upd_b2, L2_gnn_ln_g, L2_gnn_ln_b, L2_gnn_res_W), axis=-1)
    x = _layernorm(x + _L3_gnn_ref(x, edge_index, edge_type_64, L3_gnn_W_self, L3_gnn_b_self, L3_gnn_W_msg, L3_gnn_b_msg, L3_gnn_rel_emb), axis=-1)
    return x

_drawn_inputs = setup_inputs


def setup_inputs(seed=0):
    import zlib

    import numpy as np

    out = dict(_drawn_inputs(seed))
    spreads = {'L2_gnn_agg_b': (0.0, 0.8),
     'L2_gnn_edge_b1': (0.0, 0.8),
     'L2_gnn_upd_b1': (0.0, 0.1),
     'L2_gnn_upd_b2': (0.0, 0.1),
     'L2_gnn_ln_g': (1.0, 0.2),
     'L2_gnn_ln_b': (0.0, 0.1)}
    factors = {'edge_attr_4': 8.0,
     'L0_gnn_a_b': 8.0,
     'L2_gnn_agg_W': 6.701,
     'L2_gnn_edge_W1': 8.0,
     'L2_gnn_edge_W2': 8.0}
    for name, (base, spread) in spreads.items():
        noise = np.random.default_rng([zlib.crc32(name.encode()), seed]).standard_normal(out[name].shape)
        drawn = base * np.exp(spread * noise) if base else spread * noise
        out[name] = jnp.asarray(drawn.astype(out[name].dtype))
    for name, factor in factors.items():
        out[name] = (out[name] * factor).astype(out[name].dtype)
    return out
```

```python
import concourse.bass as bass
from concourse import mybir
from contextlib import ExitStack

fp32 = mybir.dt.float32
bf16 = mybir.dt.bfloat16
i32 = mybir.dt.int32
ALU = mybir.AluOpType
ACT = mybir.ActivationFunctionType
AX = mybir.AxisListType.X
PE_E = mybir.EngineType.PE

P = 128
F = 128
H = 4
FH = F // H
R = 4
U = 4
HALF = 64
ROW0 = F + H
DW = H + 1
NREL = 64
BIG = 1.0e30
PAD_DST = 1000000
SAFE_RANGE = 60.0
LN_EPS = 1e-5
SLOPE = 0.2


def gnn_kernel(nc, ins, out):
    N = ins["x"].shape[0]
    E = ins["src"].shape[0]
    NB = -(-N // P)
    LASTR = N - (NB - 1) * P
    NN = NB * P
    NCH = -(-E // (P * R * U)) * R * U
    NG = NCH // U
    NIT = NG // R
    GE = U * P
    FULLP = E // GE
    REM = E - FULLP * GE
    NWIN = 2 * NB - 1
    BANKS = -(-NB // 4)
    assert BANKS <= 7 and NG <= P and (NB % 4) * P + NWIN * DW <= 512 and NB % 4

    def blocks(i):
        return range(4 * i, min(4 * i + 4, NB))

    def cols(i):
        return slice(blocks(i)[0] * P, (blocks(i)[-1] + 1) * P)

    tab = [nc.dram_tensor("tab0", (NN, ROW0), fp32, kind="Internal").ap()]
    tab += [nc.dram_tensor(f"tab{n}", (NN, F), fp32, kind="Internal").ap() for n in (1, 2, 3)]
    win_d = nc.dram_tensor("win_d", (1, NCH), fp32, kind="Internal").ap()
    dst_d = nc.dram_tensor("dst_d", (1, NCH * P), fp32, kind="Internal").ap()
    typ_d = nc.dram_tensor("typ_d", (1, NCH * P), bf16, kind="Internal").ap()

    ctx = ExitStack()
    with ctx:
        def sb(name, shape, dt=fp32):
            return ctx.enter_context(nc.sbuf_tensor(name, shape, dt))

        def sem(name):
            return ctx.enter_context(nc.semaphore(name))

        X = sb("X", [P, NB, F])
        XT = sb("XT", [P, NN])
        AG = sb("AG", [P, NN])
        T0 = sb("T0", [P, NB, ROW0])
        bias3 = T0[:, :, 0:F]
        T1 = sb("T1", [P, NB, F])
        NX = sb("NX", [P, NB, F])
        T1f = T1[:, :, :].rearrange("p b f -> p (b f)")
        rcB = sb("rcB", [P, NN])
        vals = sb("vals", [P, R * U, ROW0])
        oh = sb("oh", [P, R * U, P])
        ohT = sb("ohT", [P, R * U, P])
        rowB = sb("rowB", [P, R, GE])
        typB = sb("typB", [NREL, R, GE], bf16)
        idx = sb("idx", [P, R * U], i32)
        srcT = sb("srcT", [P, NCH], i32)
        dstT = sb("dstT", [P, NCH])
        relT = sb("relT", [P, NCH])
        nid = sb("nid", [P, NCH])
        winB = sb("winB", [P, NCH])
        winc = sb("winc", [P, NCH])
        winrow = sb("winrow", [1, NCH], i32)
        edge_raw = sb("edge_raw", [P, 3, GE], i32)
        edge_f = sb("edge_f", [P, 3, GE])
        typ_b = sb("typ_b", [P, GE], bf16)
        attr = sb("attr", [P, GE * 4])
        attrE = sb("attrE", [P, NG, U * 4])
        ar = sb("ar", [P, U * 4])
        arT = sb("arT", [U * 4, P])
        hid = sb("hid", [P, GE])
        ew = sb("ew", [P, NCH])
        iota_i = sb("iota_i", [P, P], i32)
        pcol_i = sb("pcol_i", [P, 1], i32)
        iota = sb("iota", [P, P])
        pcol = sb("pcol", [P, 1])
        ident = sb("ident", [P, P])
        ident4 = sb("ident4", [P, 4, P])
        swap = sb("swap", [P, P])
        ones = sb("ones", [P, P])
        zeros = sb("zeros", [1, 512])
        W0 = sb("W0", [F, F])
        W1 = sb("W1", [F, F])
        Wagg = sb("Wagg", [F, F])
        Wu1 = sb("Wu1", [F, 2, F])
        Wu2 = sb("Wu2", [F, F])
        Wres = sb("Wres", [F, F])
        Wmr = sb("Wmr", [F, F])
        Wsr = sb("Wsr", [F, F])
        WmT = sb("WmT", [F, F])
        WsT = sb("WsT", [F, F])
        We1 = sb("We1", [U * 4, U, F])
        We2 = sb("We2", [F, 1])
        rel = sb("rel", [NREL, F])
        b0 = sb("b0", [P, F])
        aw = sb("aw", [P, H, 2 * FH])
        ab = sb("ab", [P, H])
        bagg = sb("bagg", [P, F])
        bu2 = sb("bu2", [P, F])
        lng = sb("lng", [P, F])
        lnb = sb("lnb", [P, F])
        bself = sb("bself", [P, F])
        bmsg = sb("bmsg", [P, F])
        be1 = sb("be1", [F, 1])
        be2 = sb("be2", [P, 1])
        bu1 = sb("bu1", [F, 1])
        sd = sb("sd", [P, NB, H])
        mx = sb("mx", [P, NB, H])
        zz = sb("zz", [P, NB, H])
        nodeE = sb("nodeE", [P, NB, 2 * H])
        nd = sb("nd", [P, NWIN, 2 * H])
        wself = sb("wself", [P, NB, H])
        ext = sb("ext", [P, 2 * H])
        exq = sb("exq", [2 * H, 2 * H])
        exc = sb("exc", [2 * H, 1])
        exB = sb("exB", [P, 2 * H])
        rng = sb("rng", [P, H])
        rng1 = sb("rng1", [P, 1])
        cmin = sb("cmin", [P, U])
        cmax = sb("cmax", [P, U])
        cwin_i = sb("cwin_i", [P, U], i32)
        cwin = sb("cwin", [P, U])
        cspan = sb("cspan", [P, U])
        viol = sb("viol", [P, 1])
        bad = sb("bad", [P, 1])
        gen = sb("gen", [P, 1])
        isfast = sb("isfast", [P, 1])
        npass_f = sb("npass_f", [P, 2])
        npass_i = sb("npass_i", [P, 2], i32)
        pb = sb("pb", [P, 1])
        pstep = sb("pstep", [P, 1])
        z = sb("z", [P, R, U, H])
        lz = sb("lz", [P, R, U, H])
        tt = sb("tt", [P, R, U, H])
        wr = sb("wr", [P, R, U, DW])
        D = sb("D", [P, NWIN, DW])
        den = sb("den", [P, NB, DW])
        rden = sb("rden", [P, NB, H])
        st = sb("st", [P, NB, 6])
        ma = sb("ma", [P, NB])
        mb = sb("mb", [P, NB])
        mean = sb("mean", [P, NB])
        rstd = sb("rstd", [P, NB])
        cnt = sb("cnt", [P, NB])
        rc = sb("rc", [P, NB])
        g_idx = sb("g_idx", [P, 1], i32)
        g_row = sb("g_row", [P, ROW0])
        g_oh = sb("g_oh", [P, P])
        g_ohm = sb("g_ohm", [P, P])
        g_dg = sb("g_dg", [P, H, P])
        g_m = sb("g_m", [P, H])
        g_base = sb("g_base", [P, 1])

        PS = ctx.enter_context(nc.psum_tensor("PS", [P, 4096], fp32))
        DENP = PS[:, NB * P:NB * P + NWIN * DW]
        B7 = PS[:, 3584:4096]

        padded = sem("padded")
        x_in = sem("x_in")
        edges_in = sem("edges_in")
        attr_in = sem("attr_in")
        w_in = sem("w_in")
        we1_in = sem("we1_in")
        iotas = sem("iotas")
        consts = sem("consts")
        lists_out = sem("lists_out")
        lists_in = sem("lists_in")
        lists_ready = sem("lists_ready")
        edge_tr = sem("edge_tr")
        edge_tr_used = sem("edge_tr_used")
        wt_tr = sem("wt_tr")
        wt_used = sem("wt_used")
        ext_ready = sem("ext_ready")
        ext_tr = sem("ext_tr")
        ext_diag = sem("ext_diag")
        ext_bc = sem("ext_bc")
        npass_ready = sem("npass_ready")
        node_ready = sem("node_ready")
        node_sw = sem("node_sw")
        nd_ready = sem("nd_ready")
        dve_order = sem("dve_order")
        xt_tr = [sem(f"xt_tr{n}") for n in range(4)]
        xt_ready = [sem(f"xt_ready{n}") for n in range(4)]
        mm0 = sem("mm0")
        mm0_used = sem("mm0_used")
        mm2 = sem("mm2")
        mm2_used = sem("mm2_used")
        silu2 = sem("silu2")
        rows_ready = [sem(f"rows_ready{n}") for n in range(4)]
        table_ready = [sem(f"table_ready{n}") for n in range(4)]
        x_ready = [sem(f"x_ready{n}") for n in range(5)]
        var_ready = sem("var_ready")
        std_ready = sem("std_ready")
        wself_in = sem("wself_in")
        wself_ready = sem("wself_ready")
        pass_set = [sem(f"pass_set{n}") for n in range(4)]
        slot_free = [sem(f"slot_free{n}") for n in range(4)]
        idx_used = [sem(f"idx_used{n}") for n in range(4)]
        idx_in = [[sem(f"idx_in{n}_{r}") for r in range(R)] for n in range(4)]
        got = [[sem(f"got{n}_{r}") for r in range(R)] for n in range(4)]
        row_in = [[sem(f"row_in{n}_{r}") for r in range(R)] for n in range(2)]
        row_free = [sem(f"row_free{n}") for n in range(2)]
        oh_ready = [sem(f"oh_ready{n}") for n in range(4)]
        ohT_ready = [sem(f"ohT_ready{n}") for n in range(2)]
        bank7_free = [sem(f"bank7_free{n}") for n in range(2)]
        sd_ready = sem("sd_ready")
        z_done = sem("z_done")
        lz_done = sem("lz_done")
        t_ready = sem("t_ready")
        w_ready = sem("w_ready")
        vals_ready = [sem(f"vals_ready{n}") for n in range(2)]
        rel_ready = sem("rel_ready")
        attr_cp = sem("attr_cp")
        attr_tr = sem("attr_tr")
        attr_T = sem("attr_T")
        hid_mm = sem("hid_mm")
        hid_act = sem("hid_act")
        ew_mm = sem("ew_mm")
        ew_cp = sem("ew_cp")
        ew_ready = sem("ew_ready")
        acc_read = [sem(f"acc_read{n}") for n in range(4)]
        den_ready = sem("den_ready")
        den_sw = sem("den_sw")
        back = sem("back")
        post1 = sem("post1")
        rc_diag = sem("rc_diag")
        rc_bc = sem("rc_bc")
        rc_cp = sem("rc_cp")
        up1 = sem("up1")
        up1_act = sem("up1_act")
        up2 = sem("up2")
        post3 = sem("post3")
        out_done = sem("out_done")
        pool_passed = sem("pool_passed")
        pe_passed = sem("pe_passed")
        dve_passed = sem("dve_passed")
        g_ready = sem("g_ready")
        g_idx_ready = sem("g_idx_ready")
        g_got = sem("g_got")
        g_mm = sem("g_mm")

        W_LOADS = 25

        block = ctx.enter_context(nc.Block())

        def passes_of(eng):
            eng.wait_ge(npass_ready, 1)
            n = eng.value_load(npass_i[0:1, 0:1], min_val=1, max_val=NB)
            g = eng.value_load(npass_i[0:1, 1:2], min_val=0, max_val=1)
            return n, g

        @block.sync
        def _(sp):
            sp.wait_ge(padded, 4)
            for k, name in enumerate(("src", "dst", "typ")):
                v = ins[name]
                sp.dma_start(edge_raw[0:FULLP, k, :], v[0:FULLP * GE].rearrange("(p j) -> p j", j=GE)).then_inc(edges_in, 16)
                if REM:
                    sp.dma_start(edge_raw[FULLP:FULLP + 1, k, 0:REM],
                                 v[FULLP * GE:E].rearrange("(p j) -> p j", p=1)).then_inc(edges_in, 16)
            if NB > 1:
                sp.dma_start(X[:, 0:NB - 1, :], ins["x"][0:(NB - 1) * P, :].rearrange("(b p) f -> p b f", p=P)).then_inc(x_in, 16)
            sp.dma_start(X[0:LASTR, NB - 1, :], ins["x"][(NB - 1) * P:N, :]).then_inc(x_in, 16)

            def row(v):
                return v.rearrange("(o f) -> o f", o=1).to_broadcast([P, v.shape[0]])

            def col(v):
                return v.rearrange("(f o) -> f o", o=1)

            loads = [
                (W0[:, :], ins["W_w"]), (b0[:, :], row(ins["W_b"])),
                (aw[:, :, :].rearrange("p h f -> p (h f)"), row(ins["a_w"].rearrange("h f -> (h f)"))),
                (ab[:, :], row(ins["a_b"])), (W1[:, :], ins["W1"]), (Wagg[:, :], ins["agg_W"]),
                (bagg[:, :], row(ins["agg_b"])), (We2[:, :], ins["edge_W2"]), (be1[:, :], col(ins["edge_b1"])),
                (be2[:, :], row(ins["edge_b2"])), (Wu1[:, 0, :], ins["upd_W1"][0:F, :]),
                (Wu1[:, 1, :], ins["upd_W1"][F:2 * F, :]), (bu1[:, :], col(ins["upd_b1"])),
                (Wu2[:, :], ins["upd_W2"]), (bu2[:, :], row(ins["upd_b2"])), (lng[:, :], row(ins["ln_g"])),
                (lnb[:, :], row(ins["ln_b"])), (Wres[:, :], ins["res_W"]), (Wsr[:, :], ins["W_self"]),
                (bself[:, :], row(ins["b_self"])), (Wmr[:, :], ins["W_msg"]), (bmsg[:, :], row(ins["b_msg"])),
                (rel[:, :], ins["rel_emb"]),
            ]
            for dst, src in loads:
                sp.dma_start(dst, src).then_inc(w_in, 16)
            sp.dma_start(attr[0:FULLP, :], ins["attr"][0:FULLP * GE, :].rearrange("(p j) k -> p (j k)", j=GE)).then_inc(attr_in, 16)
            if REM:
                sp.dma_start(attr[FULLP:FULLP + 1, 0:REM * 4],
                             ins["attr"][FULLP * GE:E, :].rearrange("(p j) k -> p (j k)", p=1)).then_inc(attr_in, 16)
            for u in range(U):
                sp.dma_start(We1[4 * u:4 * u + 4, u, :], ins["edge_W1"]).then_inc(we1_in, 16)

            sp.wait_ge(lists_ready, 3)
            sp.dma_start(win_d.rearrange("o (g u) -> (o g) u", u=U), cwin[0:NG, :]).then_inc(lists_out, 16)
            sp.dma_start(dst_d.rearrange("o (g j) -> (o g) j", j=GE), edge_f[0:NG, 1, :]).then_inc(lists_out, 16)
            sp.dma_start(typ_d.rearrange("o (g j) -> (o g) j", j=GE), typ_b[0:NG, :]).then_inc(lists_out, 16)
            sp.wait_ge(lists_out, 48)
            sp.dma_start(winB[:, :], win_d.to_broadcast([P, NCH])).then_inc(lists_in, 16)

            for L in range(4):
                if L == 2:
                    sp.wait_ge(silu2, BANKS)
                else:
                    sp.wait_ge(rows_ready[L], 1)
                rows = {0: T0[:, :, :], 1: X[:, :, :], 2: T1[:, :, :], 3: X[:, :, :]}[L]
                sp.dma_start(tab[L].rearrange("(b p) f -> p b f", p=P), rows).then_inc(table_ready[L], 16)
                if L == 0:
                    npass, _ = passes_of(sp)
                    sp.wait_ge(edge_tr_used, 2)
                with sp.Fori(0, npass) as ps, sp.Fori(0, NIT) as it:
                    turn = sp.snap(ps * NIT + it)
                    for r in range(R):
                        sp.wait_ge(idx_used[L], turn * R + (r + 1))
                        sp.dma_start(idx[:, r * U:(r + 1) * U],
                                     srcT[:, bass.ds(it * (R * U) + r * U, U)]).then_inc(idx_in[L][r], 16)
                        if L == 0:
                            sp.wait_ge(row_free[0], turn * R + (r + 1))
                            sp.dma_start(rowB[:, r, :], dst_d[:, bass.ds(it * (R * GE) + r * GE, GE)].to_broadcast([P, GE])).then_inc(row_in[0][r], 16)
                        if L == 3:
                            sp.wait_ge(row_free[1], turn * R + (r + 1))
                            sp.dma_start(typB[:, r, :], typ_d[:, bass.ds(it * (R * GE) + r * GE, GE)].to_broadcast([NREL, GE])).then_inc(row_in[1][r], 16)

            sp.wait_ge(x_ready[4], 1)
            if NB > 1:
                sp.dma_start(out[0:(NB - 1) * P, :].rearrange("(b p) f -> p b f", p=P), X[:, 0:NB - 1, :]).then_inc(out_done, 16)
            sp.dma_start(out[(NB - 1) * P:N, :], X[0:LASTR, NB - 1, :]).then_inc(out_done, 16)
            sp.wait_ge(out_done, 16 * (1 + (NB > 1)))

        @block.gpsimd
        def _(pool):
            nc.gpsimd.iota(iota_i[:, :], pattern=[[1, P]], base=0, channel_multiplier=0).then_inc(iotas, 1)
            nc.gpsimd.iota(pcol_i[:, :], pattern=[[0, 1]], base=0, channel_multiplier=1).then_inc(iotas, 1)
            for L in range(4):
                pool.sem_inc(idx_used[L], R)
            npass, general = passes_of(pool)
            pool.wait_ge(table_ready[0], 16)
            with pool.If(general == 1):
                with pool.Fori(0, NB * NCH) as n:
                    pool.wait_ge(g_idx_ready, n + 1)
                    pool.sem_inc(pool_passed, 1)
                    nc.gpsimd.indirect_dma_start(g_row[:, :], None, tab[0],
                                                 bass.IndirectOffsetOnAxis(ap=g_idx[:, 0:1], axis=0)).then_inc(g_got, 16)
            for L in range(4):
                pool.wait_ge(table_ready[L], 16)
                width = ROW0 if L == 0 else F
                with pool.Fori(0, npass) as ps, pool.Fori(0, NIT) as it:
                    turn = pool.snap(ps * NIT + it)
                    for r in range(R):
                        pool.wait_ge(slot_free[L], turn * R + (r + 1))
                        pool.wait_ge(idx_in[L][r], turn * 16 + 16)
                        pool.sem_inc(pool_passed, 1)
                        for u in range(U):
                            s = r * U + u
                            nc.gpsimd.indirect_dma_start(
                                vals[:, s, 0:width], None, tab[L],
                                bass.IndirectOffsetOnAxis(ap=idx[:, s:s + 1], axis=0)).then_inc(got[L][r], 16)

        @block.scalar
        def _(act):
            npass, _ = passes_of(act)
            act.wait_ge(wself_in, 1)
            nc.scalar.activation(wself[:, :, :], wself[:, :, :], ACT.Exp).then_inc(wself_ready, 1)
            with act.Fori(0, npass) as ps, act.Fori(0, NIT) as it:
                turn = act.snap(ps * NIT + it)
                for r in range(R):
                    act.wait_ge(t_ready, turn * R + (r + 1))
                    nc.scalar.activation(wr[:, r, :, 0:H], tt[:, r, :, :], ACT.Exp).then_inc(w_ready, 1)

            def sqrt_var(n):
                act.wait_ge(var_ready, n)
                nc.scalar.activation(rstd[:, :], mb[:, :], ACT.Sqrt).then_inc(std_ready, 1)

            sqrt_var(1)
            act.wait_ge(w_in, 16 * 23)
            with act.Fori(0, npass) as ps, act.Fori(0, NIT) as it:
                turn = act.snap(ps * NIT + it)
                for r in range(R):
                    g = turn * R + r
                    nc.scalar.copy(ar[:, :], attrE[:, bass.ds(it * R + r, 1), :].rearrange("p o k -> p (o k)")).then_inc(attr_cp, 1)
                    act.wait_ge(attr_tr, g + 1)
                    nc.scalar.copy(arT[:, :], B7[0:U * 4, 0:P]).then_inc(attr_T, 1)
                    act.wait_ge(hid_mm, g + 1)
                    nc.scalar.activation(hid[:, :], B7, ACT.Silu, bias=be1[:, 0:1]).then_inc(hid_act, 1)
                    act.wait_ge(ew_mm, g + 1)
                    nc.scalar.copy(ew[:, bass.ds(it * (R * U) + r * U, U)], B7[:, 0:U]).then_inc(ew_cp, 1)
            act.wait_ge(ew_cp, npass * (NIT * R))
            nc.scalar.activation(ew[:, :], ew[:, :], ACT.Sigmoid, bias=be2[:, 0:1]).then_inc(ew_ready, 1)
            sqrt_var(2)
            for i in range(BANKS):
                act.wait_ge(mm2_used, i + 1)
                b = blocks(i)
                nc.scalar.activation(T1[:, b[0]:b[-1] + 1, :], NX[:, b[0]:b[-1] + 1, :], ACT.Silu).then_inc(silu2, 1)
            for i in range(BANKS):
                act.wait_ge(up1, i + 1)
                nc.scalar.activation(T1f[:, cols(i)], PS[:, cols(i)], ACT.Silu, bias=bu1[:, 0:1]).then_inc(up1_act, 1)
            sqrt_var(3)
            sqrt_var(4)
            sqrt_var(5)

        @block.vector
        def _(dve):
            done = [0]
            V = nc.vector

            def link(instr):
                done[0] += 1
                instr.then_inc(dve_order, 1)
                dve.wait_ge(dve_order, done[0])

            def loose(instr):
                done[0] += 1
                instr.then_inc(dve_order, 1)

            def settle():
                dve.wait_ge(dve_order, done[0])

            for L in range(2):
                dve.sem_inc(row_free[L], R)
                dve.sem_inc(bank7_free[L], 1)
            V.memset(edge_raw[:, 0, :], 0).then_inc(padded, 1)
            V.memset(edge_raw[:, 1, :], PAD_DST).then_inc(padded, 1)
            V.memset(edge_raw[:, 2, :], 0).then_inc(padded, 1)
            loose(V.memset(attr[:, :], 0.0))
            loose(V.memset(We1[:, :, :], 0.0))
            loose(V.memset(wr[:, :, :, :], 1.0))
            loose(V.memset(ones[:, :], 1.0))
            loose(V.memset(zeros[:, :], 0.0))
            loose(V.memset(pb[:, :], 0.0))
            loose(V.memset(viol[:, :], 0.0))
            loose(V.memset(vals[:, :, :], 0.0))
            loose(V.memset(den[:, :, :], 0.0))
            settle()
            V.memset(X[:, NB - 1, :], 0.0).then_inc(padded, 1)
            dve.wait_ge(iotas, 2)
            loose(V.tensor_copy(iota[:, :], iota_i[:, :]))
            link(V.tensor_copy(pcol[:, :], pcol_i[:, :]))
            link(V.tensor_scalar(ident[:, :], iota[:, :], pcol[:, 0:1], None, ALU.is_equal))
            for k in range(4):
                loose(V.tensor_copy(ident4[:, k, :], ident[:, :]))
            loose(V.tensor_copy(swap[:, 0:HALF], ident[:, HALF:P]))
            loose(V.tensor_copy(swap[:, HALF:P], ident[:, 0:HALF]))
            settle()
            dve.sem_inc(consts, 1)

            dve.wait_ge(edges_in, 16 * 3 * (1 + (REM > 0)))
            link(V.tensor_copy(edge_f[0:NG, :, :], edge_raw[0:NG, :, :]))
            V.tensor_scalar(typ_b[0:NG, :], edge_f[0:NG, 2, :], 0.0, float(NREL - 1), ALU.max, ALU.min).then_inc(lists_ready, 1)
            d4 = edge_f[0:NG, 1, :].rearrange("p (u j) -> p u j", u=U)
            link(V.tensor_reduce(cmin[0:NG, :], d4, AX, ALU.min))
            link(V.tensor_scalar(cmin[0:NG, :], cmin[0:NG, :], float(HALF * (NWIN - 1)), None, ALU.min))
            link(V.tensor_copy(cwin_i[0:NG, :], cmin[0:NG, :]))
            link(V.tensor_single_scalar(cwin_i[0:NG, :], cwin_i[0:NG, :], 6, ALU.arith_shift_right))
            V.tensor_copy(cwin[0:NG, :], cwin_i[0:NG, :]).then_inc(lists_ready, 2)
            dve.wait_ge(lists_ready, 3)
            tmp = T1f[0:NG, 0:GE]
            link(V.scalar_tensor_tensor(tmp, edge_f[0:NG, 1, :], 0.5 * PAD_DST, edge_f[0:NG, 1, :], ALU.is_lt, ALU.mult))
            link(V.tensor_reduce(cmax[0:NG, :], tmp.rearrange("p (u j) -> p u j", u=U), AX, ALU.max))
            link(V.scalar_tensor_tensor(cspan[0:NG, :], cwin[0:NG, :], -float(HALF), cmax[0:NG, :], ALU.mult, ALU.add))
            link(V.tensor_scalar(cspan[0:NG, :], cspan[0:NG, :], float(P), None, ALU.is_ge))
            link(V.tensor_reduce(viol[0:NG, :], cspan[0:NG, :], AX, ALU.max))

            def copy_xt(L):
                for i in range(BANKS):
                    dve.wait_ge(xt_tr[L], i + 1)
                    V.tensor_copy(XT[:, cols(i)], PS[:, cols(i)]).then_inc(xt_ready[L], 1)

            copy_xt(0)
            dve.wait_ge(w_in, 16 * 23)
            for i in range(BANKS):
                dve.wait_ge(mm0, i + 1)
                b = blocks(i)
                V.tensor_tensor(T0[:, b[0]:b[-1] + 1, 0:F], PS[:, cols(i)].rearrange("p (b f) -> p b f", f=F),
                                b0[:, :].unsqueeze(1).to_broadcast([P, len(b), F]), ALU.add).then_inc(mm0_used, 1)
            dve.wait_ge(mm0_used, BANKS)

            def head_sum(dst, half):
                link(V.tensor_tensor(T1[:, :, :].rearrange("p b (h f) -> p b h f", h=H),
                                     T0[:, :, 0:F].rearrange("p b (h f) -> p b h f", h=H),
                                     aw[:, :, half * FH:(half + 1) * FH].unsqueeze(1).to_broadcast([P, NB, H, FH]), ALU.mult))
                return V.tensor_reduce(dst, T1[:, :, :].rearrange("p b (h f) -> p b h f", h=H), AX, ALU.add)

            link(head_sum(T0[:, :, F:ROW0], 1))
            dve.sem_inc(rows_ready[0], 1)
            link(head_sum(sd[:, :, :], 0))
            link(V.tensor_tensor(sd[:, :, :], sd[:, :, :], ab[:, :].unsqueeze(1).to_broadcast([P, NB, H]), ALU.add))
            ss = T0[:, :, F:ROW0]
            link(V.tensor_reduce(ext[:, 0:H], ss.rearrange("p b h -> p h b"), AX, ALU.max))
            link(V.tensor_reduce(ext[:, H:2 * H], ss.rearrange("p b h -> p h b"), AX, ALU.min))
            link(V.tensor_scalar(ext[:, H:2 * H], ext[:, H:2 * H], -1.0, None, ALU.mult))
            dve.sem_inc(ext_ready, 1)
            dve.wait_ge(ext_tr, 1)
            link(V.tensor_reduce(exc[:, :], B7[0:2 * H, 0:P], AX, ALU.max))
            V.tensor_scalar(exq[:, :], ident[0:2 * H, 0:2 * H], exc[:, 0:1], None, ALU.mult).then_inc(ext_diag, 1)
            dve.wait_ge(ext_bc, 1)
            loose(V.tensor_copy(exB[:, :], B7[:, 0:2 * H]))
            link(V.tensor_copy(bad[:, :], B7[:, 8:9]))
            link(V.tensor_tensor(rng[:, :], exB[:, 0:H], exB[:, H:2 * H], ALU.add))
            link(V.tensor_reduce(rng1[:, :], rng[:, :], AX, ALU.max))
            link(V.tensor_scalar(rng1[:, :], rng1[:, :], SAFE_RANGE, None, ALU.is_le))
            link(V.tensor_scalar(bad[:, :], bad[:, :], 0.5, None, ALU.is_lt))
            link(V.tensor_tensor(isfast[:, :], bad[:, :], rng1[:, :], ALU.mult))
            link(V.tensor_scalar(gen[:, :], isfast[:, :], -1.0, 1.0, ALU.mult, ALU.add))
            loose(V.tensor_scalar(npass_f[:, 0:1], gen[:, :], float(NB - 1), 1.0, ALU.mult, ALU.add))
            loose(V.tensor_copy(npass_f[:, 1:2], gen[:, :]))
            loose(V.tensor_scalar(pstep[:, :], gen[:, :], 2.0, None, ALU.mult))
            link(V.tensor_copy(mx[:, :, :], exB[:, 0:H].unsqueeze(1).to_broadcast([P, NB, H])))
            V.tensor_copy(npass_i[:, :], npass_f[:, :]).then_inc(npass_ready, 1)

            for k, dstn in ((0, srcT), (1, dstT)):
                dve.wait_ge(edge_tr, k + 1)
                V.tensor_copy(dstn[:, :].rearrange("p (g u) -> p u g", u=U),
                              PS[:, k * 512:k * 512 + U * P].rearrange("p (u g) -> p u g", u=U)[:, :, 0:NG]).then_inc(edge_tr_used, 1)
            dve.wait_ge(edge_tr_used, 2)
            for k in range(4):
                dve.wait_ge(edge_tr, 3 + k)
                V.tensor_copy(attrE[:, :, :].rearrange("p g (u k) -> p k u g", k=4)[:, k, :, :],
                              PS[:, (2 + k) * 512:(2 + k) * 512 + U * P].rearrange("p (u g) -> p u g", u=U)[:, :, 0:NG]).then_inc(edge_tr_used, 1)
            dve.wait_ge(wt_tr, 1)
            loose(V.tensor_copy(WmT[:, :], B7[:, 0:P]))
            V.tensor_copy(WsT[:, :], B7[:, P:2 * P]).then_inc(wt_used, 1)

            npass, general = passes_of(dve)
            with dve.If(general == 1):
                V.tensor_copy(mx[:, :, :], ss).then_inc(g_ready, 1)
                V.memset(g_base[:, :], 0.0).then_inc(g_ready, 1)
                dve.wait_ge(g_ready, 2)
                mxf = mx[:, :, :].rearrange("p b h -> p (b h)")
                with dve.Fori(0, NB) as w:
                    with dve.Fori(0, NCH) as c:
                        n = dve.snap(w * NCH + c)
                        V.tensor_copy(g_idx[:, :], srcT[:, bass.ds(c, 1)]).then_inc(g_idx_ready, 1)
                        V.tensor_scalar(g_oh[:, :], iota[:, :], g_base[:, 0:1], dstT[:, bass.ds(c, 1)], ALU.add, ALU.is_equal).then_inc(g_ready, 1)
                        dve.wait_ge(g_ready, n * 8 + w + 3)
                        V.tensor_scalar(g_ohm[:, :], g_oh[:, :], BIG, -BIG, ALU.mult, ALU.add).then_inc(g_ready, 1)
                        dve.wait_ge(g_got, n * 16 + 16)
                        for h in range(H):
                            V.tensor_scalar(g_dg[:, h, :], ident[:, :], g_row[:, F + h:F + h + 1], None, ALU.mult).then_inc(g_ready, 1)
                        dve.wait_ge(g_mm, n + 1)
                        V.tensor_reduce(g_m[:, :], B7.rearrange("p (h e) -> p h e", h=H), AX, ALU.max).then_inc(g_ready, 1)
                        dve.wait_ge(g_ready, n * 8 + w + 9)
                        V.tensor_tensor(mxf[:, bass.ds(w * H, H)], mxf[:, bass.ds(w * H, H)], g_m[:, :], ALU.max).then_inc(g_ready, 1)
                        dve.wait_ge(g_ready, n * 8 + w + 10)
                    V.tensor_scalar(g_base[:, :], g_base[:, :], float(P), None, ALU.add).then_inc(g_ready, 1)
                    dve.wait_ge(g_ready, w * (NCH * 8 + 1) + (NCH * 8 + 3))

            def leaky(dst, src):
                link(V.scalar_tensor_tensor(dst, src, SLOPE, src, ALU.mult, ALU.max))

            link(V.tensor_tensor(zz[:, :, :], sd[:, :, :], mx[:, :, :], ALU.add))
            leaky(nodeE[:, :, H:2 * H], zz[:, :, :])
            link(V.tensor_copy(nodeE[:, :, 0:H], sd[:, :, :]))
            dve.sem_inc(node_ready, 1)
            link(V.tensor_tensor(zz[:, :, :], sd[:, :, :], ss, ALU.add))
            leaky(wself[:, :, :], zz[:, :, :])
            V.tensor_tensor(wself[:, :, :], wself[:, :, :], nodeE[:, :, H:2 * H], ALU.subtract).then_inc(wself_in, 1)
            dve.wait_ge(node_sw, 1)
            sw = B7[:, 0:NB * 2 * H].rearrange("p (b k) -> p b k", k=2 * H)
            loose(V.tensor_copy(nd[:, 0:NWIN:2, :], nodeE[:, :, :]))
            if NB > 1:
                loose(V.tensor_copy(nd[0:HALF, 1:NWIN:2, :], sw[0:HALF, 0:NB - 1, :]))
                loose(V.tensor_copy(nd[HALF:P, 1:NWIN:2, :], sw[HALF:P, 1:NB, :]))
            settle()
            dve.sem_inc(nd_ready, 1)
            dve.wait_ge(lists_in, 16)

            def set_pass(L, ps, chain, total):
                V.tensor_scalar(winc[:, :], winB[:, :], isfast[:, 0:1], pb[:, 0:1], ALU.mult, ALU.add).then_inc(chain, 1)
                dve.wait_ge(chain, ps * 6 + 1)
                V.scalar_tensor_tensor(relT[:, :], winc[:, :], -float(HALF), dstT[:, :], ALU.mult, ALU.add).then_inc(chain, 1)
                V.tensor_scalar(nid[:, :], winc[:, :], float(HALF), pcol[:, 0:1], ALU.mult, ALU.add).then_inc(chain, 1)
                V.tensor_copy(winrow[:, :], winc[0:1, :]).then_inc(chain, 1)
                V.tensor_tensor(pb[:, :], pb[:, :], pstep[:, :], ALU.add).then_inc(chain, 1)
                dve.wait_ge(chain, ps * 6 + 5)
                V.tensor_scalar(pb[:, :], pb[:, :], 1.0, None, ALU.mult).then_inc(chain, 1)
                dve.wait_ge(chain, ps * 6 + 6)
                dve.sem_inc(dve_passed, 1)

            def one_hot(L, it, r, weighted=False):
                for u in range(U):
                    c = it * (R * U) + (r * U + u)
                    o = V.tensor_scalar(oh[:, r * U + u, :], iota[:, :], relT[:, bass.ds(c, 1)],
                                        ew[:, bass.ds(c, 1)] if weighted else None,
                                        ALU.is_equal, *([ALU.mult] if weighted else []))
                o.then_inc(oh_ready[L], 1)

            with dve.Fori(0, npass) as ps:
                dve.wait_ge(slot_free[0], ps * (NIT * R) + R)
                set_pass(0, ps, pass_set[0], None)
                with dve.Fori(0, NIT) as it:
                    turn = dve.snap(ps * NIT + it)

                    def masks(r):
                        dve.wait_ge(slot_free[0], turn * R + (r + 1))
                        dve.wait_ge(row_in[0][r], turn * 16 + 16)
                        for u in range(U):
                            c = it * (R * U) + (r * U + u)
                            o = V.tensor_scalar(ohT[:, r * U + u, :], rowB[:, r, u * P:(u + 1) * P], nid[:, bass.ds(c, 1)], None, ALU.is_equal)
                        o.then_inc(ohT_ready[0], 1)
                        one_hot(0, it, r)
                        dve.wait_ge(ohT_ready[0], turn * R + (r + 1))
                        dve.sem_inc(row_free[0], 1)

                    def exponents(r):
                        g = turn * R + r
                        dve.wait_ge(got[0][r], turn * (16 * U) + 16 * U)
                        dve.sem_inc(idx_used[0], 1)
                        dve.wait_ge(sd_ready, g + 1)
                        sp_ = B7[:, 0:U * 2 * H].rearrange("p (u k) -> p u k", u=U)
                        V.tensor_tensor(z[:, r, :, :], sp_[:, :, 0:H], vals[:, r * U:(r + 1) * U, F:ROW0], ALU.add).then_inc(z_done, 1)
                        dve.wait_ge(z_done, g + 1)
                        V.scalar_tensor_tensor(lz[:, r, :, :], z[:, r, :, :], SLOPE, z[:, r, :, :], ALU.mult, ALU.max).then_inc(lz_done, 1)
                        dve.wait_ge(lz_done, g + 1)
                        V.tensor_tensor(tt[:, r, :, :], lz[:, r, :, :], sp_[:, :, H:2 * H], ALU.subtract).then_inc(t_ready, 1)
                        dve.wait_ge(t_ready, g + 1)
                        dve.sem_inc(bank7_free[0], 1)

                    def weigh(r):
                        dve.wait_ge(w_ready, turn * R + (r + 1))
                        v = vals[:, r * U:(r + 1) * U, 0:F].rearrange("p u (h f) -> p u h f", h=H)
                        V.tensor_tensor(v, v, wr[:, r, :, 0:H].unsqueeze(3).to_broadcast([P, U, H, FH]), ALU.mult).then_inc(vals_ready[0], 1)

                    masks(0)
                    masks(1)
                    exponents(0)
                    weigh(0)
                    exponents(1)
                    masks(2)
                    weigh(1)
                    exponents(2)
                    masks(3)
                    weigh(2)
                    exponents(3)
                    weigh(3)

            dve.wait_ge(slot_free[0], npass * (NIT * R) + R)
            dve.wait_ge(wself_ready, 1)
            V.tensor_copy(D[:, :, :].rearrange("p w k -> p (w k)"), DENP).then_inc(den_ready, 1)
            for i in range(BANKS):
                V.tensor_copy(AG[:, cols(i)], PS[:, cols(i)]).then_inc(acc_read[0], 1)
            wk = T1[:, :, :].rearrange("p b (h f) -> p b h f", h=H)
            link(V.tensor_tensor(wk, T0[:, :, 0:F].rearrange("p b (h f) -> p b h f", h=H),
                                 wself[:, :, :].unsqueeze(3).to_broadcast([P, NB, H, FH]), ALU.mult))
            dve.wait_ge(den_sw, 1)
            sdn = B7[:, 0:NWIN * DW].rearrange("p (w k) -> p w k", k=DW)
            link(V.tensor_copy(den[:, :, :], D[:, 0:NWIN:2, :]))
            if NB > 1:
                loose(V.tensor_tensor(den[0:HALF, 1:NB, :], den[0:HALF, 1:NB, :], sdn[0:HALF, 1:NWIN:2, :], ALU.add))
                loose(V.tensor_tensor(den[HALF:P, 0:NB - 1, :], den[HALF:P, 0:NB - 1, :], sdn[HALF:P, 1:NWIN:2, :], ALU.add))
            settle()
            link(V.tensor_tensor(rden[:, :, :], den[:, :, 0:H], wself[:, :, :], ALU.add))
            link(V.reciprocal(rden[:, :, :], rden[:, :, :]))
            link(V.tensor_scalar(rc[:, :], den[:, :, H], 1.0, None, ALU.max))
            loose(V.tensor_scalar(cnt[:, :], den[:, :, H], 1.0, None, ALU.min))
            link(V.reciprocal(rc[:, :], rc[:, :]))

            def psum4(i):
                return PS[:, cols(i)].rearrange("p (b f) -> p b f", f=F)

            for i in range(BANKS):
                b = blocks(i)
                s = slice(b[0], b[-1] + 1)
                dve.wait_ge(back, i + 1)
                link(V.tensor_tensor(NX[:, s, :], psum4(i), T1[:, s, :], ALU.add))
                h4 = NX[:, s, :].rearrange("p b (h f) -> p b h f", h=H)
                link(V.tensor_tensor(h4, h4, rden[:, s, :].unsqueeze(3).to_broadcast([P, len(b), H, FH]), ALU.mult))
                link(V.tensor_tensor(NX[:, s, :], NX[:, s, :], X[:, s, :], ALU.add))

            norms = [0]

            def normalise(dst, src):
                for b in range(NB):
                    loose(V.bn_stats(st[:, b, :], src[:, b, :]))
                settle()
                loose(V.tensor_tensor(ma[:, :], st[:, :, 1], st[:, :, 4], ALU.subtract))
                loose(V.tensor_tensor(mean[:, :], st[:, :, 1], st[:, :, 4], ALU.add))
                loose(V.tensor_tensor(mb[:, :], st[:, :, 2], st[:, :, 5], ALU.add))
                settle()
                loose(V.tensor_scalar(mean[:, :], mean[:, :], 0.5, None, ALU.mult))
                link(V.tensor_tensor(ma[:, :], ma[:, :], ma[:, :], ALU.mult))
                link(V.scalar_tensor_tensor(mb[:, :], ma[:, :], 0.25 * F, mb[:, :], ALU.mult, ALU.add))
                norms[0] += 1
                V.tensor_scalar(mb[:, :], mb[:, :], 1.0 / F, LN_EPS, ALU.mult, ALU.add).then_inc(var_ready, 1)
                dve.wait_ge(std_ready, norms[0])
                link(V.reciprocal(rstd[:, :], rstd[:, :]))
                for b in range(NB):
                    loose(V.tensor_scalar(dst[:, b, :], src[:, b, :], mean[:, b:b + 1], rstd[:, b:b + 1], ALU.subtract, ALU.mult))
                settle()

            normalise(X, NX)
            dve.sem_inc(rows_ready[1], 1)
            dve.sem_inc(x_ready[1], 1)

            copy_xt(1)
            for i in range(BANKS):
                b = blocks(i)
                for k, n in enumerate(b):
                    loose(V.tensor_scalar(T1[:, n, :], ident[:, :], rc[:, n:n + 1], None, ALU.mult))
            settle()
            dve.sem_inc(rc_diag, 1)
            for i in range(BANKS):
                dve.wait_ge(rc_bc, i + 1)
                V.tensor_copy(rcB[:, cols(i)], PS[:, cols(i)]).then_inc(rc_cp, 1)
            link(V.tensor_tensor(bias3[:, :, :], cnt[:, :].unsqueeze(2).to_broadcast([P, NB, F]),
                                 bmsg[:, :].unsqueeze(1).to_broadcast([P, NB, F]), ALU.mult))
            link(V.tensor_tensor(bias3[:, :, :], bias3[:, :, :], bself[:, :].unsqueeze(1).to_broadcast([P, NB, F]), ALU.add))

            def plain_loop(L):
                with dve.Fori(0, npass) as ps:
                    dve.wait_ge(slot_free[L], ps * (NIT * R) + R)
                    set_pass(L, ps, pass_set[L], None)
                    with dve.Fori(0, NIT) as it:
                        turn = dve.snap(ps * NIT + it)
                        for r in range(R):
                            dve.wait_ge(slot_free[L], turn * R + (r + 1))
                            one_hot(L, it, r, weighted=L == 2)

            def reset_pass():
                link(V.memset(pb[:, :], 0.0))

            reset_pass()
            plain_loop(1)
            dve.wait_ge(slot_free[1], npass * (NIT * R) + R)
            for i in range(BANKS):
                V.tensor_tensor(AG[:, cols(i)], PS[:, cols(i)], XT[:, cols(i)], ALU.add).then_inc(acc_read[1], 1)
            for i in range(BANKS):
                b = blocks(i)
                s = slice(b[0], b[-1] + 1)
                dve.wait_ge(post1, i + 1)
                loose(V.scalar_tensor_tensor(NX[:, s, :], psum4(i), 0.0, X[:, s, :], ALU.max, ALU.add))
            settle()
            normalise(X, NX)
            dve.sem_inc(x_ready[2], 1)

            copy_xt(2)
            for i in range(BANKS):
                b = blocks(i)
                s = slice(b[0], b[-1] + 1)
                dve.wait_ge(mm2, i + 1)
                V.tensor_tensor(NX[:, s, :], psum4(i), bagg[:, :].unsqueeze(1).to_broadcast([P, len(b), F]), ALU.add).then_inc(mm2_used, 1)
            dve.wait_ge(ew_ready, 1)
            reset_pass()
            plain_loop(2)
            dve.wait_ge(slot_free[2], npass * (NIT * R) + R)
            for i in range(BANKS):
                V.tensor_tensor(AG[:, cols(i)], PS[:, cols(i)], rcB[:, cols(i)], ALU.mult).then_inc(acc_read[2], 1)
            for i in range(BANKS):
                b = blocks(i)
                s = slice(b[0], b[-1] + 1)
                dve.wait_ge(up2, i + 1)
                loose(V.tensor_tensor(NX[:, s, :], psum4(i), bu2[:, :].unsqueeze(1).to_broadcast([P, len(b), F]), ALU.add))
            settle()
            normalise(T1, NX)
            link(V.tensor_tensor(T1[:, :, :], T1[:, :, :], lng[:, :].unsqueeze(1).to_broadcast([P, NB, F]), ALU.mult))
            link(V.tensor_tensor(T1[:, :, :], T1[:, :, :], lnb[:, :].unsqueeze(1).to_broadcast([P, NB, F]), ALU.add))
            link(V.tensor_tensor(NX[:, :, :], T1[:, :, :], X[:, :, :], ALU.add))
            normalise(X, NX)
            dve.sem_inc(rows_ready[3], 1)
            dve.sem_inc(x_ready[3], 1)

            copy_xt(3)
            reset_pass()
            with dve.Fori(0, npass) as ps:
                dve.wait_ge(slot_free[3], ps * (NIT * R) + R)
                set_pass(3, ps, pass_set[3], None)
                with dve.Fori(0, NIT) as it:
                    turn = dve.snap(ps * NIT + it)

                    def masks3(r):
                        dve.wait_ge(slot_free[3], turn * R + (r + 1))
                        dve.wait_ge(row_in[1][r], turn * 16 + 16)
                        V.tensor_scalar(ohT[0:NREL, r * U:(r + 1) * U, :].rearrange("p u e -> p (u e)"), typB[:, r, :],
                                        pcol[0:NREL, 0:1], None, ALU.is_equal).then_inc(ohT_ready[1], 1)
                        one_hot(3, it, r)
                        dve.wait_ge(ohT_ready[1], turn * R + (r + 1))
                        dve.sem_inc(row_free[1], 1)

                    def add_rel(r):
                        dve.wait_ge(got[3][r], turn * (16 * U) + 16 * U)
                        dve.sem_inc(idx_used[3], 1)
                        dve.wait_ge(rel_ready, turn * R + (r + 1))
                        v = vals[:, r * U:(r + 1) * U, 0:F]
                        V.tensor_tensor(v, v, B7.rearrange("p (u f) -> p u f", u=U), ALU.add).then_inc(vals_ready[1], 1)

                    masks3(0)
                    for r in range(R):
                        if r + 1 < R:
                            masks3(r + 1)
                        add_rel(r)
            dve.wait_ge(slot_free[3], npass * (NIT * R) + R)
            for i in range(BANKS):
                V.tensor_tensor(AG[:, cols(i)], PS[:, cols(i)], rcB[:, cols(i)], ALU.mult).then_inc(acc_read[3], 1)
            link(V.tensor_tensor(bias3[:, :, :], bias3[:, :, :], X[:, :, :], ALU.add))
            for i in range(BANKS):
                b = blocks(i)
                s = slice(b[0], b[-1] + 1)
                dve.wait_ge(post3, i + 1)
                loose(V.tensor_tensor(NX[:, s, :], psum4(i), bias3[:, s, :], ALU.add))
            settle()
            normalise(X, NX)
            dve.sem_inc(x_ready[4], 1)

        @block.tensor
        def _(pe):
            T = nc.tensor
            for L in range(4):
                pe.sem_inc(slot_free[L], R)
            pe.wait_ge(consts, 1)
            pe.wait_ge(x_in, 16 * (1 + (NB > 1)))

            def x_transposed(L):
                for i in range(BANKS):
                    for b in blocks(i):
                        o = T.transpose(PS[:, b * P:(b + 1) * P], X[:, b, :], ident[:, :])
                    o.then_inc(xt_tr[L], 1)

            def dense(dst_sem, ready, terms):
                for i in range(BANKS):
                    for s, base in ready:
                        pe.wait_ge(s, base + i + 1)
                    for b in blocks(i):
                        for k, (lhs, rhs) in enumerate(terms):
                            o = T.matmul(PS[:, b * P:(b + 1) * P], lhs[:, b * P:(b + 1) * P], rhs,
                                         start=k == 0, stop=k == len(terms) - 1)
                    o.then_inc(dst_sem, 1)

            def zero_banks():
                for i in range(BANKS):
                    T.matmul(PS[:, i * 512:(i + 1) * 512], zeros[0:1, 0:P], zeros[0:1, :], start=True, stop=False, skip_group_check=True)

            x_transposed(0)
            pe.wait_ge(w_in, 16 * 23)
            pe.wait_ge(lists_ready, 3)
            dense(mm0, [(xt_ready[0], 0)], [(XT, W0[:, :])])
            pe.wait_ge(ext_ready, 1)
            T.transpose(B7[0:2 * H, 0:P], ext[:, :], ident[:, :]).then_inc(ext_tr, 1)
            pe.wait_ge(ext_diag, 1)
            T.matmul(B7[:, 0:2 * H], ones[0:2 * H, :], exq[:, :], start=True, stop=True)
            T.matmul(B7[:, 2 * H:2 * H + 1], ones[:, :], viol[:, :], start=True, stop=True).then_inc(ext_bc, 1)
            pe.wait_ge(mm0_used, BANKS)
            for k in range(2):
                for u in range(U):
                    o = T.transpose(PS[:, k * 512 + u * P:k * 512 + u * P + NG], edge_f[0:NG, k, u * P:(u + 1) * P], ident[0:NG, 0:NG])
                o.then_inc(edge_tr, 1)
            pe.wait_ge(attr_in, 16 * (1 + (REM > 0)))
            av = attr[:, :].rearrange("p (u j k) -> p u k j", u=U, k=4)
            for k in range(4):
                for u in range(U):
                    o = T.transpose(PS[:, (2 + k) * 512 + u * P:(2 + k) * 512 + u * P + NG], av[0:NG, u, k, :], ident[0:NG, 0:NG])
                o.then_inc(edge_tr, 1)
            pe.wait_ge(npass_ready, 1)
            T.transpose(B7[:, 0:P], Wmr[:, :], ident[:, :])
            T.transpose(B7[:, P:2 * P], Wsr[:, :], ident[:, :]).then_inc(wt_tr, 1)
            pe.wait_ge(wt_used, 1)
            npass, general = passes_of(pe)
            with pe.If(general == 1):
                with pe.Fori(0, NB) as w, pe.Fori(0, NCH) as c:
                    n = pe.snap(w * NCH + c)
                    pe.wait_ge(g_ready, n * 8 + w + 8)
                    T.matmul(B7, g_oh[:, :], g_dg[:, :, :].rearrange("p h e -> p (h e)"), start=True, stop=False)
                    T.matmul(B7, g_ohm[:, :], ident4[:, :, :].rearrange("p h e -> p (h e)"), start=False, stop=True).then_inc(g_mm, 1)
            pe.wait_ge(node_ready, 1)
            T.matmul(B7[:, 0:NB * 2 * H], swap[:, :], nodeE[:, :, :].rearrange("p b k -> p (b k)"), start=True, stop=True).then_inc(node_sw, 1)
            pe.wait_ge(edge_tr_used, 6)
            zero_banks()
            pe.wait_ge(nd_ready, 1)
            ndf = nd[:, :, :].rearrange("p w k -> p (w k)")

            def windows(it, r):
                c = it * (R * U) + r * U
                return [pe.value_load(winrow[0:1, bass.ds(c + u, 1)], min_val=0, max_val=NWIN - 1) for u in range(U)]

            def scatter(L, r, u, w):
                s = r * U + u
                for half in range(2):
                    o = T.matmul(PS[:, bass.ds(w * HALF + half * HALF, HALF)], vals[:, s, 0:F],
                                 oh[:, s, half * HALF:(half + 1) * HALF], start=False, stop=False, skip_group_check=True)
                return o

            with pe.Fori(0, npass) as ps:
                pe.wait_ge(pass_set[0], ps * 6 + 6)
                pe.sem_inc(pe_passed, 1)
                with pe.Fori(0, NIT) as it:
                    turn = pe.snap(ps * NIT + it)
                    wins = {}

                    def fetch(r):
                        g = turn * R + r
                        wins[r] = windows(it, r)
                        pe.wait_ge(ohT_ready[0], g + 1)
                        pe.wait_ge(bank7_free[0], g + 1)
                        for u in range(U):
                            o = T.matmul(B7[:, u * 2 * H:(u + 1) * 2 * H], ohT[:, r * U + u, :],
                                         ndf[:, bass.ds(wins[r][u] * (2 * H), 2 * H)], start=True, stop=True)
                        o.then_inc(sd_ready, 1)

                    def sums(r):
                        g = turn * R + r
                        pe.wait_ge(oh_ready[0], g + 1)
                        pe.wait_ge(vals_ready[0], g + 1)
                        for u in range(U):
                            w = wins[r][u]
                            scatter(0, r, u, w)
                            o = T.matmul(DENP[:, bass.ds(w * DW, DW)], oh[:, r * U + u, :], wr[:, r, u, :],
                                         start=False, stop=False, skip_group_check=True)
                        o.then_inc(slot_free[0], 1)

                    fetch(0)
                    for r in range(R):
                        if r + 1 < R:
                            fetch(r + 1)
                        sums(r)
            pe.wait_ge(den_ready, 1)
            pe.wait_ge(t_ready, npass * (NIT * R))
            T.matmul(B7[:, 0:NWIN * DW], swap[:, :], D[:, :, :].rearrange("p w k -> p (w k)"), start=True, stop=True).then_inc(den_sw, 1)
            for i in range(BANKS):
                pe.wait_ge(acc_read[0], i + 1)
                for b in blocks(i):
                    o = T.transpose(PS[:, b * P:(b + 1) * P], AG[:, b * P:(b + 1) * P], ident[:, :])
                o.then_inc(back, 1)

            pe.wait_ge(x_ready[1], 1)
            x_transposed(1)
            pe.wait_ge(rc_diag, 1)
            pe.wait_ge(xt_ready[1], BANKS)
            for i in range(BANKS):
                for b in blocks(i):
                    o = T.matmul(PS[:, b * P:(b + 1) * P], ones[:, :], T1[:, b, :], start=True, stop=True)
                o.then_inc(rc_bc, 1)
            pe.wait_ge(rc_cp, BANKS)
            zero_banks()
            pe.wait_ge(we1_in, 16 * U)
            with pe.Fori(0, npass) as ps:
                pe.wait_ge(pass_set[1], ps * 6 + 6)
                pe.sem_inc(pe_passed, 1)
                with pe.Fori(0, NIT) as it:
                    turn = pe.snap(ps * NIT + it)
                    for r in range(R):
                        g = turn * R + r
                        wins = windows(it, r)
                        pe.wait_ge(oh_ready[1], g + 1)

                        def sum_of(u):
                            return scatter(1, r, u, wins[u])

                        pe.wait_ge(attr_cp, g + 1)
                        T.transpose(B7[0:U * 4, 0:P], ar[:, :], ident[:, :]).then_inc(attr_tr, 1)
                        pe.wait_ge(got[1][r], turn * (16 * U) + 16 * U)
                        pe.sem_inc(idx_used[1], 1)
                        sum_of(0)
                        pe.wait_ge(attr_T, g + 1)
                        for u in range(U):
                            o = T.matmul(B7[:, u * P:(u + 1) * P], We1[:, u, :], arT[:, :], start=True, stop=True)
                        o.then_inc(hid_mm, 1)
                        sum_of(1)
                        sum_of(2)
                        pe.wait_ge(hid_act, g + 1)
                        for u in range(U):
                            o = T.matmul(B7[:, u:u + 1], hid[:, u * P:(u + 1) * P], We2[:, :], start=True, stop=True)
                        o.then_inc(ew_mm, 1)
                        sum_of(3).then_inc(slot_free[1], 1)
            dense(post1, [(acc_read[1], 0)], [(AG, W1[:, :])])

            pe.wait_ge(x_ready[2], 1)
            x_transposed(2)
            dense(mm2, [(xt_ready[2], 0)], [(XT, Wagg[:, :])])
            pe.wait_ge(mm2_used, BANKS)
            zero_banks()

            with pe.Fori(0, npass) as ps:
                pe.wait_ge(pass_set[2], ps * 6 + 6)
                pe.sem_inc(pe_passed, 1)
                with pe.Fori(0, NIT) as it:
                    turn = pe.snap(ps * NIT + it)
                    for r in range(R):
                        wins = windows(it, r)
                        pe.wait_ge(oh_ready[2], turn * R + (r + 1))
                        pe.wait_ge(got[2][r], turn * (16 * U) + 16 * U)
                        pe.sem_inc(idx_used[2], 1)
                        for u in range(U):
                            o = scatter(2, r, u, wins[u])
                        o.then_inc(slot_free[2], 1)
            for i in range(BANKS):
                pe.wait_ge(acc_read[2], i + 1)
                T.matmul(PS[:, cols(i)], Wu1[:, 0, :], XT[:, cols(i)], start=True, stop=False)
                T.matmul(PS[:, cols(i)], Wu1[:, 1, :], AG[:, cols(i)], start=False, stop=True).then_inc(up1, 1)
            dense(up2, [(up1_act, 0)], [(T1f, Wu2[:, :]), (XT, Wres[:, :])])

            pe.wait_ge(x_ready[3], 1)
            x_transposed(3)
            pe.wait_ge(xt_ready[3], BANKS)
            zero_banks()
            pe.wait_ge(ew_ready, 1)
            pe.sem_inc(pe_passed, 1)
            with pe.Fori(0, npass) as ps:
                pe.wait_ge(pass_set[3], ps * 6 + 6)
                pe.sem_inc(pe_passed, 1)
                with pe.Fori(0, NIT) as it:
                    turn = pe.snap(ps * NIT + it)

                    def relations(r):
                        pe.wait_ge(ohT_ready[1], turn * R + (r + 1))
                        pe.wait_ge(bank7_free[1], 1)
                        if r:
                            pe.wait_ge(vals_ready[1], turn * R + r)
                        for u in range(U):
                            o = T.matmul(B7[:, u * F:(u + 1) * F], ohT[0:NREL, r * U + u, :], rel[:, :], start=True, stop=True)
                        o.then_inc(rel_ready, 1)

                    relations(0)
                    for r in range(R):
                        wins = windows(it, r)
                        pe.wait_ge(vals_ready[1], turn * R + (r + 1))
                        if r + 1 < R:
                            relations(r + 1)
                        pe.wait_ge(oh_ready[3], turn * R + (r + 1))
                        for u in range(U):
                            o = scatter(3, r, u, wins[u])
                        o.then_inc(slot_free[3], 1)
            dense(post3, [(acc_read[3], 0)], [(XT, WsT[:, :]), (AG, WmT[:, :])])


_INS = {'x': 'x', 'src': 'src', 'dst': 'dst', 'attr': 'edge_attr_4', 'typ': 'edge_type_64',
        'W_w': 'L0_gnn_W_w', 'W_b': 'L0_gnn_W_b', 'a_w': 'L0_gnn_a_w', 'a_b': 'L0_gnn_a_b', 'W1': 'L1_gnn_W',
        'agg_W': 'L2_gnn_agg_W', 'agg_b': 'L2_gnn_agg_b', 'edge_W1': 'L2_gnn_edge_W1', 'edge_b1': 'L2_gnn_edge_b1',
        'edge_W2': 'L2_gnn_edge_W2', 'edge_b2': 'L2_gnn_edge_b2', 'upd_W1': 'L2_gnn_upd_W1',
        'upd_b1': 'L2_gnn_upd_b1', 'upd_W2': 'L2_gnn_upd_W2', 'upd_b2': 'L2_gnn_upd_b2', 'ln_g': 'L2_gnn_ln_g',
        'ln_b': 'L2_gnn_ln_b', 'res_W': 'L2_gnn_res_W', 'W_self': 'L3_gnn_W_self', 'b_self': 'L3_gnn_b_self',
        'W_msg': 'L3_gnn_W_msg', 'b_msg': 'L3_gnn_b_msg', 'rel_emb': 'L3_gnn_rel_emb'}


def kernel(**inputs):
    import numpy as _np
    import concourse.bacc as _bacc
    from concourse import mybir as _mybir
    from concourse.bass_utils import run_bass_kernel_spmd as _run

    nc = _bacc.Bacc("TRN2", target_bir_lowering=False, num_devices=1)
    arrays, args = {}, {}
    for short, name in _INS.items():
        a = _np.ascontiguousarray(inputs[name])
        arrays[f"in_{name}"] = a
        args[short] = nc.dram_tensor(f"in_{name}", a.shape, _mybir.dt.from_np(a.dtype), kind="ExternalInput").ap()
    shape = inputs["x"].shape
    out = nc.dram_tensor("out", shape, _mybir.dt.float32, kind="ExternalOutput").ap()
    gnn_kernel(nc, args, out)
    return _run(nc, [arrays], core_ids=[0]).results[0]["out"]
```

```python
import concourse.bass as bass
from concourse import mybir
from contextlib import ExitStack

fp32 = mybir.dt.float32
bf16 = mybir.dt.bfloat16
i32 = mybir.dt.int32
ALU = mybir.AluOpType
ACT = mybir.ActivationFunctionType
AX = mybir.AxisListType.X
PE_E = mybir.EngineType.PE

P = 128
F = 128
H = 4
FH = F // H
R = 4
U = 4
HALF = 64
STRIDE = 448
SHARED = 512 - STRIDE
NDP = 3 * 2 * H
ATT = 96
ATK = ATT + 3
ROW0 = F + H
DW = H + 1
NREL = 64
BIG = 1.0e30
PAD_DST = 1000000
SAFE_RANGE = 60.0
LN_EPS = 1e-5
SLOPE = 0.2


def gnn_kernel(nc, ins, out):
    N = ins["x"].shape[0]
    E = ins["src"].shape[0]
    NB = -(-N // P)
    LASTR = N - (NB - 1) * P
    NN = NB * P
    NCH = -(-E // (P * R * U)) * R * U
    NG = NCH // U
    NIT = NG // R
    GE = U * P
    FULLP = E // GE
    REM = E - FULLP * GE
    NWIN = 2 * NB - 1
    BANKS = -(-NB // 4)
    ABANKS = (NWIN - 1) // 7 + 1
    NSLOT = NWIN + ABANKS - 1
    assert BANKS <= 7 and ABANKS <= 7 and NG <= P and NWIN * 37 < 7 * 256 + 37 and NB > 1

    def blocks(i):
        return range(4 * i, min(4 * i + 4, NB))

    def cols(i):
        return slice(blocks(i)[0] * P, (blocks(i)[-1] + 1) * P)

    tab = [nc.dram_tensor("tab0", (NN, ROW0), fp32, kind="Internal").ap()]
    tab += [nc.dram_tensor(f"tab{n}", (NN, F), fp32, kind="Internal").ap() for n in (1, 2, 3)]
    win_d = nc.dram_tensor("win_d", (1, NCH), fp32, kind="Internal").ap()
    rel_d = nc.dram_tensor("rel_d", (1, NCH * P), bf16, kind="Internal").ap()
    typ_d = nc.dram_tensor("typ_d", (1, NCH * P), bf16, kind="Internal").ap()

    ctx = ExitStack()
    with ctx:
        def sb(name, shape, dt=fp32):
            return ctx.enter_context(nc.sbuf_tensor(name, shape, dt))

        def sem(name):
            return ctx.enter_context(nc.semaphore(name))

        X = sb("X", [P, NB, F])
        XT = sb("XT", [P, NN])
        ag = sb("ag", [P, max(NN, 3 * GE)])
        AG = ag[:, 0:NN]
        edge_raw = ag[:, 0:3 * GE].bitcast(i32).rearrange("p (k j) -> p k j", k=3)
        T0 = sb("T0", [P, NB, ROW0])
        bias3 = T0[:, :, 0:F]
        T1 = sb("T1", [P, NB, F])
        nx = sb("nx", [P, max(NB * F, GE * 4)])
        NX = nx[:, 0:NB * F].rearrange("p (b f) -> p b f", f=F)
        attr = nx[:, 0:GE * 4]
        T1f = T1[:, :, :].rearrange("p b f -> p (b f)")
        rcB = sb("rcB", [P, NN])
        vals = sb("vals", [P, R * U, ROW0])
        oh = sb("oh", [P, R * U, P])
        ohT = sb("ohT", [P, R, GE], bf16)
        rowB = sb("rowB", [P, R, GE], bf16)
        idx = sb("idx", [P, R * U], i32)
        srcT = sb("srcT", [P, NCH], i32)
        dstT = sb("dstT", [P, NCH])
        relT = sb("relT", [P, NCH])
        relc = sb("relc", [P, GE], bf16)
        cwinc = sb("cwinc", [P, U])
        winB = sb("winB", [P, NCH])
        winc = sb("winc", [P, NCH])
        win_i = sb("win_i", [1, NCH], i32)
        slot_i = sb("slot_i", [1, NCH], i32)
        edge_f = sb("edge_f", [P, 3, GE])
        typ_b = sb("typ_b", [P, GE], bf16)
        attrE = sb("attrE", [P, NG, U * 4])
        attrS = sb("attrS", [P, NG, ATT], bf16)
        ar = sb("ar", [P, P], bf16)
        arT = sb("arT", [P, P], bf16)
        hid = sb("hid", [P, U, F])
        ew = sb("ew", [P, NCH])
        iota_i = sb("iota_i", [P, P], i32)
        pcol_i = sb("pcol_i", [P, 1], i32)
        iota = sb("iota", [P, P])
        pcol = sb("pcol", [P, 1])
        ident = sb("ident", [P, P])
        identb = sb("identb", [P, P], bf16)
        pmod = sb("pmod", [P, 1])
        psel = sb("psel", [P, 3])
        ptmp = sb("ptmp", [P, 1])
        ident4 = sb("ident4", [P, 4, P])
        swap = sb("swap", [P, P])
        ones = sb("ones", [P, P])
        zeros = sb("zeros", [1, 512])
        W0 = sb("W0", [F, F])
        W1 = sb("W1", [F, F])
        Wagg = sb("Wagg", [F, F])
        Wu1 = sb("Wu1", [F, 2, F])
        Wu2 = sb("Wu2", [F, F])
        Wres = sb("Wres", [F, F])
        Wmr = sb("Wmr", [F, F])
        Wsr = sb("Wsr", [F, F])
        WmT = sb("WmT", [F, F])
        WsT = sb("WsT", [F, F])
        We1 = oh[:, 0:U, :].rearrange("p a f -> p (a f)")
        We1b = sb("We1b", [P, U * F], bf16)
        We2 = sb("We2", [P, F])
        rel = sb("rel", [P, F])
        relb = sb("relb", [P, 2, F], bf16)
        b0 = sb("b0", [P, F])
        aw = sb("aw", [P, H, 2 * FH])
        ab = sb("ab", [P, H])
        bagg = sb("bagg", [P, F])
        bu2 = sb("bu2", [P, F])
        lng = sb("lng", [P, F])
        lnb = sb("lnb", [P, F])
        bself = sb("bself", [P, F])
        bmsg = sb("bmsg", [P, F])
        be2 = sb("be2", [P, 1])
        bu1 = sb("bu1", [F, 1])
        sd = sb("sd", [P, NB, H])
        mx = sb("mx", [P, NB, H])
        zz = sb("zz", [P, NB, H])
        nodeE = sb("nodeE", [P, NB, 2 * H])
        nd = sb("nd", [P, NSLOT, 2 * H])
        ndr = sb("ndr", [P, NSLOT, 2 * H])
        nd3 = sb("nd3", [P, NSLOT, 3, 2 * H], bf16)
        wself = sb("wself", [P, NB, H])
        ext = sb("ext", [P, 2 * H])
        exq = sb("exq", [2 * H, 2 * H])
        exc = sb("exc", [2 * H, 1])
        exB = sb("exB", [P, 2 * H])
        rng = sb("rng", [P, H])
        rng1 = sb("rng1", [P, 1])
        cmin = sb("cmin", [P, U])
        cmax = sb("cmax", [P, U])
        cwin_i = sb("cwin_i", [P, U], i32)
        cwin = sb("cwin", [P, U])
        cspan = sb("cspan", [P, U])
        viol = sb("viol", [P, 1])
        bad = sb("bad", [P, 1])
        gen = sb("gen", [P, 1])
        isfast = sb("isfast", [P, 1])
        npass_f = sb("npass_f", [P, 2])
        npass_i = sb("npass_i", [P, 2], i32)
        pb = sb("pb", [P, 1])
        pstep = sb("pstep", [P, 1])
        dn = sb("dn", [P, R, U, 2 * H])
        z = sb("z", [P, R, U, H])
        lz = sb("lz", [P, R, U, H])
        tt = sb("tt", [P, R, U, H])
        wr = sb("wr", [P, R, U, DW])
        D = sb("D", [P, NSLOT, DW])
        shared = sb("shared", [P, ABANKS, SHARED])
        den = sb("den", [P, NB, DW])
        rden = sb("rden", [P, NB, H])
        st = sb("st", [P, NB, 6])
        ma = sb("ma", [P, NB])
        mb = sb("mb", [P, NB])
        mean = sb("mean", [P, NB])
        rstd = sb("rstd", [P, NB])
        cnt = sb("cnt", [P, NB])
        rc = sb("rc", [P, NB])
        g_idx = sb("g_idx", [P, 1], i32)
        g_row = sb("g_row", [P, ROW0])
        g_oh = sb("g_oh", [P, P])
        g_ohm = sb("g_ohm", [P, P])
        g_dg = sb("g_dg", [P, H, P])
        g_m = sb("g_m", [P, H])
        g_base = sb("g_base", [P, 1])

        PS = ctx.enter_context(nc.psum_tensor("PS", [P, 4096], fp32))
        B7 = PS[:, 3584:4096]
        DENP = B7[:, 0:NSLOT * DW]
        NDP0 = 512 - U * NDP

        padded = sem("padded")
        x_in = sem("x_in")
        edges_in = sem("edges_in")
        attr_in = sem("attr_in")
        w_in = sem("w_in")
        we1_in = sem("we1_in")
        iotas = sem("iotas")
        consts = sem("consts")
        lists_out = sem("lists_out")
        lists_in = sem("lists_in")
        lists_ready = sem("lists_ready")
        edge_tr = sem("edge_tr")
        edge_tr_used = sem("edge_tr_used")
        wt_tr = sem("wt_tr")
        wt_used = sem("wt_used")
        ext_ready = sem("ext_ready")
        ext_tr = sem("ext_tr")
        ext_diag = sem("ext_diag")
        ext_bc = sem("ext_bc")
        npass_ready = sem("npass_ready")
        node_ready = sem("node_ready")
        node_sw = sem("node_sw")
        nd_ready = sem("nd_ready")
        dve_order = sem("dve_order")
        xt_tr = [sem(f"xt_tr{n}") for n in range(4)]
        xt_ready = [sem(f"xt_ready{n}") for n in range(4)]
        mm0 = sem("mm0")
        mm0_used = sem("mm0_used")
        mm2 = sem("mm2")
        mm2_used = sem("mm2_used")
        silu2 = sem("silu2")
        rows_ready = [sem(f"rows_ready{n}") for n in range(4)]
        table_ready = [sem(f"table_ready{n}") for n in range(4)]
        x_ready = [sem(f"x_ready{n}") for n in range(5)]
        var_ready = sem("var_ready")
        std_ready = sem("std_ready")
        wself_in = sem("wself_in")
        wself_ready = sem("wself_ready")
        pass_set = [sem(f"pass_set{n}") for n in range(4)]
        slot_free = [sem(f"slot_free{n}") for n in range(4)]
        idx_used = [sem(f"idx_used{n}") for n in range(4)]
        idx_in = [sem(f"idx_in{r}") for r in range(R)]
        got = [[sem(f"got{n}_{r}") for r in range(R)] for n in range(4)]
        row_in = [[sem(f"row_in{n}_{r}") for r in range(R)] for n in range(2)]
        row_free = [sem(f"row_free{n}") for n in range(2)]
        oh_ready = [sem(f"oh_ready{n}") for n in range(4)]
        ohT_ready = [sem(f"ohT_ready{n}") for n in range(2)]
        bank7_free = [sem(f"bank7_free{n}") for n in range(2)]
        sd_ready = sem("sd_ready")
        z_done = sem("z_done")
        parts_ready = sem("parts_ready")
        t_sub = sem("t_sub")
        lz_done = sem("lz_done")
        t_ready = sem("t_ready")
        w_ready = sem("w_ready")
        vals_ready = [sem(f"vals_ready{n}") for n in range(2)]
        rel_ready = sem("rel_ready")
        relc_ready = sem("relc_ready")
        rel_out = sem("rel_out")
        dn_done = sem("dn_done")
        split_done = sem("split_done")
        hid_free = sem("hid_free")
        prod_done = sem("prod_done")
        attr_cp = sem("attr_cp")
        attr_tr = sem("attr_tr")
        attr_T = sem("attr_T")
        hid_mm = sem("hid_mm")
        hid_act = sem("hid_act")
        ew_ready = sem("ew_ready")
        acc_read = [sem(f"acc_read{n}") for n in range(4)]
        den_ready = sem("den_ready")
        den_sw = sem("den_sw")
        back = sem("back")
        post1 = sem("post1")
        rc_diag = sem("rc_diag")
        rc_bc = sem("rc_bc")
        rc_cp = sem("rc_cp")
        up1 = sem("up1")
        up1_act = sem("up1_act")
        up2 = sem("up2")
        post3 = sem("post3")
        out_done = sem("out_done")
        passed = sem("passed")
        g_ready = sem("g_ready")
        g_idx_ready = sem("g_idx_ready")
        g_got = sem("g_got")
        g_mm = sem("g_mm")

        W_LOADS = 25

        block = ctx.enter_context(nc.Block())

        def passes_of(eng):
            eng.wait_ge(npass_ready, 1)
            n = eng.value_load(npass_i[0:1, 0:1], min_val=1, max_val=NB)
            g = eng.value_load(npass_i[0:1, 1:2], min_val=0, max_val=1)
            return n, g

        @block.sync
        def _(sp):
            sp.wait_ge(padded, 4)
            for k, name in enumerate(("src", "dst", "typ")):
                v = ins[name]
                sp.dma_start(edge_raw[0:FULLP, k, :], v[0:FULLP * GE].rearrange("(p j) -> p j", j=GE)).then_inc(edges_in, 16)
                if REM:
                    sp.dma_start(edge_raw[FULLP:FULLP + 1, k, 0:REM],
                                 v[FULLP * GE:E].rearrange("(p j) -> p j", p=1)).then_inc(edges_in, 16)
            if NB > 1:
                sp.dma_start(X[:, 0:NB - 1, :], ins["x"][0:(NB - 1) * P, :].rearrange("(b p) f -> p b f", p=P)).then_inc(x_in, 16)
            sp.dma_start(X[0:LASTR, NB - 1, :], ins["x"][(NB - 1) * P:N, :]).then_inc(x_in, 16)

            def row(v):
                return v.rearrange("(o f) -> o f", o=1).to_broadcast([P, v.shape[0]])

            def col(v):
                return v.rearrange("(f o) -> f o", o=1)

            loads = [
                (W0[:, :], ins["W_w"]), (b0[:, :], row(ins["W_b"])),
                (aw[:, :, :].rearrange("p h f -> p (h f)"), row(ins["a_w"].rearrange("h f -> (h f)"))),
                (ab[:, :], row(ins["a_b"])), (W1[:, :], ins["W1"]), (Wagg[:, :], ins["agg_W"]),
                (bagg[:, :], row(ins["agg_b"])), (We2[:, :], row(ins["edge_W2"].rearrange("f o -> (f o)"))),
                (be2[:, :], row(ins["edge_b2"])), (Wu1[:, 0, :], ins["upd_W1"][0:F, :]),
                (Wu1[:, 1, :], ins["upd_W1"][F:2 * F, :]), (bu1[:, :], col(ins["upd_b1"])),
                (Wu2[:, :], ins["upd_W2"]), (bu2[:, :], row(ins["upd_b2"])), (lng[:, :], row(ins["ln_g"])),
                (lnb[:, :], row(ins["ln_b"])), (Wres[:, :], ins["res_W"]), (Wsr[:, :], ins["W_self"]),
                (bself[:, :], row(ins["b_self"])), (Wmr[:, :], ins["W_msg"]), (bmsg[:, :], row(ins["b_msg"])),
                (rel[0:NREL, :], ins["rel_emb"]), (rel[NREL:2 * NREL, :], ins["rel_emb"]),
            ]
            for dst, src in loads:
                sp.dma_start(dst, src).then_inc(w_in, 16)
            sp.dma_start(attr[0:FULLP, :], ins["attr"][0:FULLP * GE, :].rearrange("(p j) k -> p (j k)", j=GE)).then_inc(attr_in, 16)
            if REM:
                sp.dma_start(attr[FULLP:FULLP + 1, 0:REM * 4],
                             ins["attr"][FULLP * GE:E, :].rearrange("(p j) k -> p (j k)", p=1)).then_inc(attr_in, 16)
            for u in range(U):
                for c in range(ATT // 16):
                    sp.dma_start(We1[16 * c + 4 * u:16 * c + 4 * u + 4, u * F:(u + 1) * F], ins["edge_W1"]).then_inc(we1_in, 16)
                sp.dma_start(We1[ATT:ATK, u * F:(u + 1) * F], ins["edge_b1"].rearrange("(o f) -> o f", o=1).to_broadcast([3, F])).then_inc(we1_in, 16)

            sp.wait_ge(lists_ready, 3)
            sp.dma_start(win_d.rearrange("o (g u) -> (o g) u", u=U), cwin[0:NG, :]).then_inc(lists_out, 16)
            sp.dma_start(typ_d.rearrange("o (g j) -> (o g) j", j=GE), typ_b[0:NG, :]).then_inc(lists_out, 16)
            sp.wait_ge(lists_out, 32)
            sp.dma_start(winB[:, :], win_d.to_broadcast([P, NCH])).then_inc(lists_in, 16)

            for L in range(4):
                if L == 2:
                    sp.wait_ge(silu2, BANKS)
                else:
                    sp.wait_ge(rows_ready[L], 1)
                rows = {0: T0[:, :, :], 1: X[:, :, :], 2: T1[:, :, :], 3: X[:, :, :]}[L]
                sp.dma_start(tab[L].rearrange("(b p) f -> p b f", p=P), rows).then_inc(table_ready[L], 16)
                if L == 0:
                    npass, _ = passes_of(sp)
                    sp.wait_ge(edge_tr_used, 2)
                with sp.Fori(0, npass) as ps:
                    if L == 0:
                        sp.wait_ge(relc_ready, ps + 1)
                        sp.dma_start(rel_d.rearrange("o (g j) -> (o g) j", j=GE), relc[0:NG, :]).then_inc(rel_out, 16)
                        sp.wait_ge(rel_out, ps * 16 + 16)
                        sp.sem_inc(passed, 1)
                    with sp.Fori(0, NIT) as it:
                        turn = sp.snap(ps * NIT + it)
                        for r in range(R):
                            sp.wait_ge(idx_used[L], turn * R + (r + 1))
                            sp.dma_start(idx[:, r * U:(r + 1) * U],
                                         srcT[:, bass.ds(it * (R * U) + r * U, U)]).then_inc(idx_in[r], 16)
                            if L in (0, 3):
                                k = L // 3
                                sp.wait_ge(row_free[k], turn * R + (r + 1))
                                sp.dma_start(rowB[:, r, :], (rel_d, typ_d)[k][:, bass.ds(it * (R * GE) + r * GE, GE)].to_broadcast([P, GE])).then_inc(row_in[k][r], 16)

            sp.wait_ge(x_ready[4], 1)
            if NB > 1:
                sp.dma_start(out[0:(NB - 1) * P, :].rearrange("(b p) f -> p b f", p=P), X[:, 0:NB - 1, :]).then_inc(out_done, 16)
            sp.dma_start(out[(NB - 1) * P:N, :], X[0:LASTR, NB - 1, :]).then_inc(out_done, 16)
            sp.wait_ge(out_done, 16 * (1 + (NB > 1)))

        @block.gpsimd
        def _(pool):
            nc.gpsimd.iota(iota_i[:, :], pattern=[[1, P]], base=0, channel_multiplier=0).then_inc(iotas, 1)
            nc.gpsimd.iota(pcol_i[:, :], pattern=[[0, 1]], base=0, channel_multiplier=1).then_inc(iotas, 1)
            for L in range(4):
                pool.sem_inc(idx_used[L], R)
            npass, general = passes_of(pool)
            pool.wait_ge(table_ready[0], 16)
            with pool.If(general == 1):
                with pool.Fori(0, NB * NCH) as n:
                    pool.wait_ge(g_idx_ready, n + 1)
                    pool.sem_inc(passed, 1)
                    nc.gpsimd.indirect_dma_start(g_row[:, :], None, tab[0],
                                                 bass.IndirectOffsetOnAxis(ap=g_idx[:, 0:1], axis=0)).then_inc(g_got, 16)
            for L in range(4):
                if L == 1:
                    n = [0]

                    def step(instr):
                        n[0] += 1
                        instr.then_inc(split_done, 1)
                        pool.wait_ge(split_done, n[0])

                    G = nc.gpsimd
                    pool.wait_ge(edge_tr_used, 6)
                    step(G.tensor_copy(attrS[:, :, 0:16], attrE[:, :, :]))
                    step(G.tensor_tensor(attrE[:, :, :], attrE[:, :, :], attrS[:, :, 0:16], ALU.subtract))
                    step(G.tensor_copy(attrS[:, :, 16:32], attrE[:, :, :]))
                    step(G.tensor_tensor(attrE[:, :, :], attrE[:, :, :], attrS[:, :, 16:32], ALU.subtract))
                    step(G.tensor_copy(attrS[:, :, 32:48], attrE[:, :, :]))
                    step(G.tensor_copy(attrS[:, :, 48:80], attrS[:, :, 0:32]))
                    step(G.tensor_copy(attrS[:, :, 80:96], attrS[:, :, 0:16]))
                pool.wait_ge(table_ready[L], 16)
                width = ROW0 if L == 0 else F
                with pool.Fori(0, npass) as ps, pool.Fori(0, NIT) as it:
                    turn = pool.snap(ps * NIT + it)
                    loads = pool.snap(npass * (L * NIT) + turn)
                    for r in range(R):
                        pool.wait_ge(slot_free[L], turn * R + (r + 1))
                        pool.wait_ge(idx_in[r], loads * 16 + 16)
                        pool.sem_inc(passed, 1)
                        for u in range(U):
                            s = r * U + u
                            nc.gpsimd.indirect_dma_start(
                                vals[:, s, 0:width], None, tab[L],
                                bass.IndirectOffsetOnAxis(ap=idx[:, s:s + 1], axis=0)).then_inc(got[L][r], 16)

        @block.scalar
        def _(act):
            npass, _ = passes_of(act)
            act.wait_ge(wself_in, 1)
            nc.scalar.activation(wself[:, :, :], wself[:, :, :], ACT.Exp).then_inc(wself_ready, 1)
            with act.Fori(0, npass) as ps, act.Fori(0, NIT) as it:
                turn = act.snap(ps * NIT + it)
                for r in range(R):
                    act.wait_ge(t_ready, turn * R + (r + 1))
                    nc.scalar.activation(wr[:, r, :, 0:H], tt[:, r, :, :], ACT.Exp).then_inc(w_ready, 1)

            def sqrt_var(n):
                act.wait_ge(var_ready, n)
                nc.scalar.activation(rstd[:, :], mb[:, :], ACT.Sqrt).then_inc(std_ready, 1)

            sqrt_var(1)
            act.wait_ge(split_done, 7)
            act.sem_inc(passed, 1)
            with act.Fori(0, npass) as ps, act.Fori(0, NIT) as it:
                turn = act.snap(ps * NIT + it)
                for r in range(R):
                    g = turn * R + r
                    nc.scalar.copy(ar[:, 0:ATT], attrS[:, bass.ds(it * R + r, 1), :].rearrange("p o k -> p (o k)")).then_inc(attr_cp, 1)
                    act.wait_ge(attr_tr, g + 1)
                    nc.scalar.copy(arT[0:ATK, :], B7[0:ATK, 0:HALF].bitcast(bf16)).then_inc(attr_T, 1)
                    act.wait_ge(hid_mm, g + 1)
                    act.wait_ge(hid_free, g + 1)
                    nc.scalar.activation(hid[:, :, :].rearrange("p u f -> p (u f)"), B7, ACT.Silu).then_inc(hid_act, 1)
            act.wait_ge(hid_free, npass * (NIT * R) + 1)
            nc.scalar.activation(ew[:, :], ew[:, :], ACT.Sigmoid, bias=be2[:, 0:1]).then_inc(ew_ready, 1)
            sqrt_var(2)
            for i in range(BANKS):
                act.wait_ge(mm2_used, i + 1)
                b = blocks(i)
                nc.scalar.activation(T1[:, b[0]:b[-1] + 1, :], NX[:, b[0]:b[-1] + 1, :], ACT.Silu).then_inc(silu2, 1)
            for i in range(BANKS):
                act.wait_ge(up1, i + 1)
                nc.scalar.activation(T1f[:, cols(i)], PS[:, cols(i)], ACT.Silu, bias=bu1[:, 0:1]).then_inc(up1_act, 1)
            sqrt_var(3)
            sqrt_var(4)
            sqrt_var(5)

        @block.vector
        def _(dve):
            done = [0]
            V = nc.vector

            def link(instr):
                done[0] += 1
                instr.then_inc(dve_order, 1)
                dve.wait_ge(dve_order, done[0])

            def loose(instr):
                done[0] += 1
                instr.then_inc(dve_order, 1)

            def settle():
                dve.wait_ge(dve_order, done[0])

            for L in range(2):
                dve.sem_inc(row_free[L], R)
                dve.sem_inc(bank7_free[L], 1)
            dve.sem_inc(hid_free, 1)
            V.memset(edge_raw[:, 0, :], 0).then_inc(padded, 1)
            V.memset(edge_raw[:, 1, :], PAD_DST).then_inc(padded, 1)
            V.memset(edge_raw[:, 2, :], 0).then_inc(padded, 1)
            loose(V.memset(attr[:, :], 0.0))
            loose(V.memset(We1, 0.0))
            loose(V.memset(ar[:, :], 1.0))
            loose(V.memset(nd[:, :, :], 0.0))
            loose(V.memset(wr[:, :, :, :], 1.0))
            loose(V.memset(ones[:, :], 1.0))
            loose(V.memset(zeros[:, :], 0.0))
            loose(V.memset(pb[:, :], 0.0))
            loose(V.memset(viol[:, :], 0.0))
            loose(V.memset(vals[:, :, :], 0.0))
            loose(V.memset(den[:, :, :], 0.0))
            settle()
            V.memset(X[:, NB - 1, :], 0.0).then_inc(padded, 1)
            dve.wait_ge(iotas, 2)
            loose(V.tensor_copy(iota[:, :], iota_i[:, :]))
            link(V.tensor_copy(pcol[:, :], pcol_i[:, :]))
            link(V.tensor_scalar(ident[:, :], iota[:, :], pcol[:, 0:1], None, ALU.is_equal))
            for k in range(4):
                loose(V.tensor_copy(ident4[:, k, :], ident[:, :]))
            loose(V.tensor_copy(swap[:, 0:HALF], ident[:, HALF:P]))
            loose(V.tensor_copy(swap[:, HALF:P], ident[:, 0:HALF]))
            loose(V.tensor_copy(identb[:, :], ident[:, :]))
            link(V.tensor_scalar(ptmp[:, :], pcol[:, :], float(NREL), None, ALU.is_ge))
            loose(V.scalar_tensor_tensor(pmod[:, :], ptmp[:, :], -float(NREL), pcol[:, :], ALU.mult, ALU.add))
            settle()
            dve.sem_inc(consts, 1)

            dve.wait_ge(edges_in, 16 * 3 * (1 + (REM > 0)))
            link(V.tensor_copy(edge_f[0:NG, :, :], edge_raw[0:NG, :, :]))
            V.tensor_scalar(typ_b[0:NG, :], edge_f[0:NG, 2, :], 0.0, float(NREL - 1), ALU.max, ALU.min).then_inc(lists_ready, 1)
            d4 = edge_f[0:NG, 1, :].rearrange("p (u j) -> p u j", u=U)
            link(V.tensor_reduce(cmin[0:NG, :], d4, AX, ALU.min))
            link(V.tensor_scalar(cmin[0:NG, :], cmin[0:NG, :], float(HALF * (NWIN - 1)), None, ALU.min))
            link(V.tensor_copy(cwin_i[0:NG, :], cmin[0:NG, :]))
            link(V.tensor_single_scalar(cwin_i[0:NG, :], cwin_i[0:NG, :], 6, ALU.arith_shift_right))
            V.tensor_copy(cwin[0:NG, :], cwin_i[0:NG, :]).then_inc(lists_ready, 2)
            dve.wait_ge(lists_ready, 3)
            tmp = T1f[0:NG, 0:GE]
            link(V.scalar_tensor_tensor(tmp, edge_f[0:NG, 1, :], 0.5 * PAD_DST, edge_f[0:NG, 1, :], ALU.is_lt, ALU.mult))
            link(V.tensor_reduce(cmax[0:NG, :], tmp.rearrange("p (u j) -> p u j", u=U), AX, ALU.max))
            link(V.scalar_tensor_tensor(cspan[0:NG, :], cwin[0:NG, :], -float(HALF), cmax[0:NG, :], ALU.mult, ALU.add))
            link(V.tensor_scalar(cspan[0:NG, :], cspan[0:NG, :], float(P), None, ALU.is_ge))
            link(V.tensor_reduce(viol[0:NG, :], cspan[0:NG, :], AX, ALU.max))

            def copy_xt(L):
                for i in range(BANKS):
                    dve.wait_ge(xt_tr[L], i + 1)
                    V.tensor_copy(XT[:, cols(i)], PS[:, cols(i)]).then_inc(xt_ready[L], 1)

            copy_xt(0)
            dve.wait_ge(w_in, 16 * 23)
            for i in range(BANKS):
                dve.wait_ge(mm0, i + 1)
                b = blocks(i)
                V.tensor_tensor(T0[:, b[0]:b[-1] + 1, 0:F], PS[:, cols(i)].rearrange("p (b f) -> p b f", f=F),
                                b0[:, :].unsqueeze(1).to_broadcast([P, len(b), F]), ALU.add).then_inc(mm0_used, 1)
            dve.wait_ge(mm0_used, BANKS)

            def head_sum(dst, half):
                link(V.tensor_tensor(T1[:, :, :].rearrange("p b (h f) -> p b h f", h=H),
                                     T0[:, :, 0:F].rearrange("p b (h f) -> p b h f", h=H),
                                     aw[:, :, half * FH:(half + 1) * FH].unsqueeze(1).to_broadcast([P, NB, H, FH]), ALU.mult))
                return V.tensor_reduce(dst, T1[:, :, :].rearrange("p b (h f) -> p b h f", h=H), AX, ALU.add)

            link(head_sum(T0[:, :, F:ROW0], 1))
            dve.sem_inc(rows_ready[0], 1)
            link(head_sum(sd[:, :, :], 0))
            link(V.tensor_tensor(sd[:, :, :], sd[:, :, :], ab[:, :].unsqueeze(1).to_broadcast([P, NB, H]), ALU.add))
            ss = T0[:, :, F:ROW0]
            link(V.tensor_reduce(ext[:, 0:H], ss.rearrange("p b h -> p h b"), AX, ALU.max))
            link(V.tensor_reduce(ext[:, H:2 * H], ss.rearrange("p b h -> p h b"), AX, ALU.min))
            link(V.tensor_scalar(ext[:, H:2 * H], ext[:, H:2 * H], -1.0, None, ALU.mult))
            dve.sem_inc(ext_ready, 1)
            dve.wait_ge(ext_tr, 1)
            link(V.tensor_reduce(exc[:, :], B7[0:2 * H, 0:P], AX, ALU.max))
            V.tensor_scalar(exq[:, :], ident[0:2 * H, 0:2 * H], exc[:, 0:1], None, ALU.mult).then_inc(ext_diag, 1)
            dve.wait_ge(ext_bc, 1)
            loose(V.tensor_copy(exB[:, :], B7[:, 0:2 * H]))
            link(V.tensor_copy(bad[:, :], B7[:, 8:9]))
            link(V.tensor_tensor(rng[:, :], exB[:, 0:H], exB[:, H:2 * H], ALU.add))
            link(V.tensor_reduce(rng1[:, :], rng[:, :], AX, ALU.max))
            link(V.tensor_scalar(rng1[:, :], rng1[:, :], SAFE_RANGE, None, ALU.is_le))
            link(V.tensor_scalar(bad[:, :], bad[:, :], 0.5, None, ALU.is_lt))
            link(V.tensor_tensor(isfast[:, :], bad[:, :], rng1[:, :], ALU.mult))
            link(V.tensor_scalar(gen[:, :], isfast[:, :], -1.0, 1.0, ALU.mult, ALU.add))
            loose(V.tensor_scalar(npass_f[:, 0:1], gen[:, :], float(NB - 1), 1.0, ALU.mult, ALU.add))
            loose(V.tensor_copy(npass_f[:, 1:2], gen[:, :]))
            loose(V.tensor_scalar(pstep[:, :], gen[:, :], 2.0, None, ALU.mult))
            link(V.tensor_copy(mx[:, :, :], exB[:, 0:H].unsqueeze(1).to_broadcast([P, NB, H])))
            V.tensor_copy(npass_i[:, :], npass_f[:, :]).then_inc(npass_ready, 1)

            for k, dstn in ((0, srcT), (1, dstT)):
                dve.wait_ge(edge_tr, k + 1)
                V.tensor_copy(dstn[:, :].rearrange("p (g u) -> p u g", u=U),
                              PS[:, k * 512:k * 512 + U * P].rearrange("p (u g) -> p u g", u=U)[:, :, 0:NG]).then_inc(edge_tr_used, 1)
            dve.wait_ge(edge_tr_used, 2)
            for k in range(4):
                dve.wait_ge(edge_tr, 3 + k)
                V.tensor_copy(attrE[:, :, :].rearrange("p g (u k) -> p k u g", k=4)[:, k, :, :],
                              PS[:, (2 + k) * 512:(2 + k) * 512 + U * P].rearrange("p (u g) -> p u g", u=U)[:, :, 0:NG]).then_inc(edge_tr_used, 1)
            dve.wait_ge(wt_tr, 1)
            loose(V.tensor_copy(WmT[:, :], B7[:, 0:P]))
            V.tensor_copy(WsT[:, :], B7[:, P:2 * P]).then_inc(wt_used, 1)

            dve.wait_ge(we1_in, 16 * U * (ATT // 16 + 1))
            for k, n in enumerate((48, 80, 96)):
                loose(V.tensor_scalar(psel[:, k:k + 1], pcol[:, :], float(n), None, ALU.is_lt))
            settle()
            link(V.tensor_tensor(psel[:, 2:3], psel[:, 2:3], psel[:, 1:2], ALU.subtract))
            link(V.tensor_tensor(psel[:, 1:2], psel[:, 1:2], psel[:, 0:1], ALU.subtract))
            for k in range(3):
                loose(V.scalar_tensor_tensor(psel[:, k:k + 1], pcol[:, :], float(ATT + k), psel[:, k:k + 1], ALU.is_equal, ALU.add))

            def two_parts(src, p1, p2):
                link(V.tensor_copy(p1, src))
                link(V.tensor_tensor(src, src, p1, ALU.subtract))
                link(V.tensor_copy(p2, src))
                link(V.tensor_tensor(src, src, p2, ALU.subtract))

            two_parts(We1, ohT[:, 0, :], ohT[:, 1, :])
            link(V.tensor_scalar(We1b[:, :], ohT[:, 0, :], psel[:, 0:1], None, ALU.mult))
            link(V.scalar_tensor_tensor(We1b[:, :], ohT[:, 1, :], psel[:, 1:2], We1b[:, :], ALU.mult, ALU.add))
            link(V.scalar_tensor_tensor(We1b[:, :], We1, psel[:, 2:3], We1b[:, :], ALU.mult, ALU.add))
            two_parts(rel[:, :], ohT[:, 0, 0:F], ohT[:, 1, 0:F])
            loose(V.memset(relb[NREL:P, 1, :], 0.0))
            loose(V.tensor_copy(relb[0:NREL, 0, :], ohT[0:NREL, 0, 0:F]))
            loose(V.tensor_copy(relb[NREL:P, 0, :], ohT[NREL:P, 1, 0:F]))
            link(V.tensor_copy(relb[0:NREL, 1, :], rel[0:NREL, :]))
            dve.sem_inc(parts_ready, 1)

            npass, general = passes_of(dve)
            with dve.If(general == 1):
                V.tensor_copy(mx[:, :, :], ss).then_inc(g_ready, 1)
                V.memset(g_base[:, :], 0.0).then_inc(g_ready, 1)
                dve.wait_ge(g_ready, 2)
                mxf = mx[:, :, :].rearrange("p b h -> p (b h)")
                with dve.Fori(0, NB) as w:
                    with dve.Fori(0, NCH) as c:
                        n = dve.snap(w * NCH + c)
                        V.tensor_copy(g_idx[:, :], srcT[:, bass.ds(c, 1)]).then_inc(g_idx_ready, 1)
                        V.tensor_scalar(g_oh[:, :], iota[:, :], g_base[:, 0:1], dstT[:, bass.ds(c, 1)], ALU.add, ALU.is_equal).then_inc(g_ready, 1)
                        dve.wait_ge(g_ready, n * 8 + w + 3)
                        V.tensor_scalar(g_ohm[:, :], g_oh[:, :], BIG, -BIG, ALU.mult, ALU.add).then_inc(g_ready, 1)
                        dve.wait_ge(g_got, n * 16 + 16)
                        for h in range(H):
                            V.tensor_scalar(g_dg[:, h, :], ident[:, :], g_row[:, F + h:F + h + 1], None, ALU.mult).then_inc(g_ready, 1)
                        dve.wait_ge(g_mm, n + 1)
                        V.tensor_reduce(g_m[:, :], B7.rearrange("p (h e) -> p h e", h=H), AX, ALU.max).then_inc(g_ready, 1)
                        dve.wait_ge(g_ready, n * 8 + w + 9)
                        V.tensor_tensor(mxf[:, bass.ds(w * H, H)], mxf[:, bass.ds(w * H, H)], g_m[:, :], ALU.max).then_inc(g_ready, 1)
                        dve.wait_ge(g_ready, n * 8 + w + 10)
                    V.tensor_scalar(g_base[:, :], g_base[:, :], float(P), None, ALU.add).then_inc(g_ready, 1)
                    dve.wait_ge(g_ready, w * (NCH * 8 + 1) + (NCH * 8 + 3))

            def leaky(dst, src):
                link(V.scalar_tensor_tensor(dst, src, SLOPE, src, ALU.mult, ALU.max))

            link(V.tensor_tensor(zz[:, :, :], sd[:, :, :], mx[:, :, :], ALU.add))
            leaky(nodeE[:, :, H:2 * H], zz[:, :, :])
            link(V.tensor_copy(nodeE[:, :, 0:H], sd[:, :, :]))
            dve.sem_inc(node_ready, 1)
            link(V.tensor_tensor(zz[:, :, :], sd[:, :, :], ss, ALU.add))
            leaky(wself[:, :, :], zz[:, :, :])
            V.tensor_tensor(wself[:, :, :], wself[:, :, :], nodeE[:, :, H:2 * H], ALU.subtract).then_inc(wself_in, 1)
            dve.wait_ge(node_sw, 1)
            sw = B7[:, 0:NB * 2 * H].rearrange("p (b k) -> p b k", k=2 * H)
            for k in range(ABANKS):
                for odd in range(2):
                    a0 = 7 * k + (k + odd) % 2
                    a1 = min(7 * k + 7, NWIN)
                    n = len(range(a0, a1, 2))
                    if not n:
                        continue
                    to = nd[:, a0 + k:a0 + k + 2 * n - 1:2, :]
                    if a0 % 2 == 0:
                        loose(V.tensor_copy(to, nodeE[:, a0 // 2:a0 // 2 + n, :]))
                    else:
                        loose(V.tensor_copy(to[0:HALF], sw[0:HALF, a0 // 2:a0 // 2 + n, :]))
                        loose(V.tensor_copy(to[HALF:P], sw[HALF:P, a0 // 2 + 1:a0 // 2 + 1 + n, :]))
            settle()
            link(V.tensor_copy(nd3[:, :, 0, :], nd[:, :, :]))
            link(V.tensor_tensor(ndr[:, :, :], nd[:, :, :], nd3[:, :, 0, :], ALU.subtract))
            link(V.tensor_copy(nd3[:, :, 1, :], ndr[:, :, :]))
            link(V.tensor_tensor(nd3[:, :, 2, :], ndr[:, :, :], nd3[:, :, 1, :], ALU.subtract))
            dve.sem_inc(nd_ready, 1)
            dve.wait_ge(lists_in, 16)

            def set_pass(L, ps):
                base = ps * 9
                chain = pass_set[L]
                V.tensor_scalar(winc[:, :], winB[:, :], isfast[:, 0:1], pb[:, 0:1], ALU.mult, ALU.add).then_inc(chain, 1)
                V.tensor_scalar(cwinc[0:NG, :], cwin[0:NG, :], isfast[0:NG, 0:1], pb[0:NG, 0:1], ALU.mult, ALU.add).then_inc(chain, 1)
                dve.wait_ge(chain, base + 2)
                V.scalar_tensor_tensor(relT[:, :], winc[:, :], -float(HALF), dstT[:, :], ALU.mult, ALU.add).then_inc(chain, 1)
                V.tensor_copy(win_i[:, :], winc[0:1, :]).then_inc(chain, 1)
                V.tensor_tensor(pb[:, :], pb[:, :], pstep[:, :], ALU.add).then_inc(chain, 1)
                dve.wait_ge(chain, base + 5)
                V.tensor_scalar(slot_i[:, :], win_i[:, :], 37.0, None, ALU.mult).then_inc(chain, 1)
                dve.wait_ge(chain, base + 6)
                V.tensor_single_scalar(slot_i[:, :], slot_i[:, :], 8, ALU.arith_shift_right).then_inc(chain, 1)
                dve.wait_ge(chain, base + 7)
                V.tensor_tensor(slot_i[:, :], slot_i[:, :], winc[0:1, :], ALU.add).then_inc(chain, 1)
                dve.wait_ge(chain, base + 8)
                if L == 0:
                    r3 = T1f[0:NG, 0:GE].rearrange("p (u j) -> p u j", u=U)
                    V.scalar_tensor_tensor(r3, cwinc[0:NG, :].unsqueeze(2).to_broadcast([NG, U, P]), -float(HALF),
                                           edge_f[0:NG, 1, :].rearrange("p (u j) -> p u j", u=U), ALU.mult, ALU.add).then_inc(chain, 1)
                    dve.wait_ge(chain, base + 9)
                    V.tensor_scalar(relc[0:NG, :], T1f[0:NG, 0:GE], -1.0, float(P), ALU.max, ALU.min).then_inc(relc_ready, 1)
                    dve.wait_ge(relc_ready, ps + 1)
                else:
                    dve.sem_inc(chain, 1)
                dve.sem_inc(passed, 1)

            def one_hot(L, it, r, weighted=False):
                for u in range(U):
                    c = it * (R * U) + (r * U + u)
                    o = V.tensor_scalar(oh[:, r * U + u, :], iota[:, :], relT[:, bass.ds(c, 1)],
                                        ew[:, bass.ds(c, 1)] if weighted else None,
                                        ALU.is_equal, *([ALU.mult] if weighted else []))
                o.then_inc(oh_ready[L], 1)

            with dve.Fori(0, npass) as ps:
                dve.wait_ge(slot_free[0], ps * (NIT * R) + R)
                set_pass(0, ps)
                def masks(it, r):
                    turn = ps * NIT + it
                    dve.wait_ge(slot_free[0], turn * R + (r + 1))
                    dve.wait_ge(row_in[0][r], turn * 16 + 16)
                    V.tensor_scalar(ohT[:, r, :], rowB[:, r, :], pcol[:, 0:1], None, ALU.is_equal).then_inc(ohT_ready[0], 1)
                    one_hot(0, it, r)
                    dve.wait_ge(ohT_ready[0], turn * R + (r + 1))
                    dve.sem_inc(row_free[0], 1)

                def iteration(it, last):
                    turn = ps * NIT + it
                    for r in range(R):
                        g = turn * R + r
                        dve.wait_ge(got[0][r], turn * (16 * U) + 16 * U)
                        dve.sem_inc(idx_used[0], 1)
                        dve.wait_ge(sd_ready, g + 1)
                        sp_ = B7[:, NDP0:512].rearrange("p (u t k) -> p u k t", u=U, t=3)
                        V.tensor_reduce(dn[:, r, :, :], sp_, AX, ALU.add).then_inc(dn_done, 1)
                        dve.wait_ge(dn_done, g + 1)
                        V.memset(B7[:, NDP0:512], 0.0).then_inc(bank7_free[0], 1)
                        V.tensor_tensor(z[:, r, :, :], dn[:, r, :, 0:H], vals[:, r * U:(r + 1) * U, F:ROW0], ALU.add).then_inc(z_done, 1)
                        dve.wait_ge(z_done, g + 1)
                        V.scalar_tensor_tensor(lz[:, r, :, :], z[:, r, :, :], SLOPE, z[:, r, :, :], ALU.mult, ALU.max).then_inc(lz_done, 1)
                        dve.wait_ge(lz_done, g + 1)
                        V.tensor_tensor(lz[:, r, :, :], lz[:, r, :, :], dn[:, r, :, H:2 * H], ALU.subtract).then_inc(t_sub, 1)
                        dve.wait_ge(t_sub, g + 1)
                        V.tensor_scalar(tt[:, r, :, :], lz[:, r, :, :], 1.0, None, ALU.min).then_inc(t_ready, 1)
                        if r + 1 < R:
                            masks(it, r + 1)
                        elif not last:
                            masks(it + 1, 0)
                        dve.wait_ge(w_ready, g + 1)
                        v = vals[:, r * U:(r + 1) * U, 0:F].rearrange("p u (h f) -> p u h f", h=H)
                        V.tensor_tensor(v, v, wr[:, r, :, 0:H].unsqueeze(3).to_broadcast([P, U, H, FH]), ALU.mult).then_inc(vals_ready[0], 1)

                masks(0, 0)
                with dve.Fori(0, NIT - 1) as it:
                    iteration(it, False)
                iteration(NIT - 1, True)

            dve.wait_ge(slot_free[0], npass * (NIT * R) + R)
            dve.wait_ge(wself_ready, 1)
            V.tensor_copy(D[:, :, :].rearrange("p w k -> p (w k)"), DENP).then_inc(den_ready, 1)

            def read_sums(L, op, other):
                if ABANKS > 1:
                    hi = PS[:, 0:512 * ABANKS].rearrange("p (k n) -> p k n", n=512)
                    link(V.tensor_copy(shared[:, 1:ABANKS, :], hi[:, 1:ABANKS, 0:SHARED]))
                    link(V.tensor_tensor(hi[:, 0:ABANKS - 1, STRIDE:512], hi[:, 0:ABANKS - 1, STRIDE:512], shared[:, 1:ABANKS, :], ALU.add))
                for k in range(ABANKS):
                    n0 = STRIDE * k + (SHARED if k else 0)
                    n1 = min(STRIDE * k + 512, NN)
                    c = PS[:, n0 + SHARED * k:n1 + SHARED * k]
                    if op is None:
                        o = V.tensor_copy(AG[:, n0:n1], c)
                    else:
                        o = V.tensor_tensor(AG[:, n0:n1], c, other[:, n0:n1], op)
                    o.then_inc(acc_read[L], 1)

            read_sums(0, None, None)
            wk = T1[:, :, :].rearrange("p b (h f) -> p b h f", h=H)
            link(V.tensor_tensor(wk, T0[:, :, 0:F].rearrange("p b (h f) -> p b h f", h=H),
                                 wself[:, :, :].unsqueeze(3).to_broadcast([P, NB, H, FH]), ALU.mult))
            dve.wait_ge(den_sw, 1)
            sdn = B7[:, 0:NSLOT * DW].rearrange("p (w k) -> p w k", k=DW)
            for k in range(ABANKS):
                a0 = 7 * k + k % 2
                n = len(range(a0, min(7 * k + 7, NWIN), 2))
                if n:
                    loose(V.tensor_copy(den[:, a0 // 2:a0 // 2 + n, :], D[:, a0 + k:a0 + k + 2 * n - 1:2, :]))
            settle()
            for k in range(ABANKS):
                a0 = 7 * k + 1 - k % 2
                n = len(range(a0, min(7 * k + 7, NWIN), 2))
                if n:
                    b0_ = a0 // 2
                    f = sdn[:, a0 + k:a0 + k + 2 * n - 1:2, :]
                    lo, hi = den[0:HALF, b0_ + 1:b0_ + 1 + n, :], den[HALF:P, b0_:b0_ + n, :]
                    loose(V.tensor_tensor(lo, lo, f[0:HALF], ALU.add))
                    loose(V.tensor_tensor(hi, hi, f[HALF:P], ALU.add))
            settle()
            link(V.tensor_tensor(rden[:, :, :], den[:, :, 0:H], wself[:, :, :], ALU.add))
            link(V.reciprocal(rden[:, :, :], rden[:, :, :]))
            link(V.tensor_scalar(rc[:, :], den[:, :, H], 1.0, None, ALU.max))
            loose(V.tensor_scalar(cnt[:, :], den[:, :, H], 1.0, None, ALU.min))
            link(V.reciprocal(rc[:, :], rc[:, :]))

            def psum4(i):
                return PS[:, cols(i)].rearrange("p (b f) -> p b f", f=F)

            for i in range(BANKS):
                b = blocks(i)
                s = slice(b[0], b[-1] + 1)
                dve.wait_ge(back, i + 1)
                link(V.tensor_tensor(NX[:, s, :], psum4(i), T1[:, s, :], ALU.add))
                h4 = NX[:, s, :].rearrange("p b (h f) -> p b h f", h=H)
                link(V.tensor_tensor(h4, h4, rden[:, s, :].unsqueeze(3).to_broadcast([P, len(b), H, FH]), ALU.mult))
                link(V.tensor_tensor(NX[:, s, :], NX[:, s, :], X[:, s, :], ALU.add))

            norms = [0]

            def normalise(dst, src):
                for b in range(NB):
                    loose(V.bn_stats(st[:, b, :], src[:, b, :]))
                settle()
                loose(V.tensor_tensor(ma[:, :], st[:, :, 1], st[:, :, 4], ALU.subtract))
                loose(V.tensor_tensor(mean[:, :], st[:, :, 1], st[:, :, 4], ALU.add))
                loose(V.tensor_tensor(mb[:, :], st[:, :, 2], st[:, :, 5], ALU.add))
                settle()
                loose(V.tensor_scalar(mean[:, :], mean[:, :], 0.5, None, ALU.mult))
                link(V.tensor_tensor(ma[:, :], ma[:, :], ma[:, :], ALU.mult))
                link(V.scalar_tensor_tensor(mb[:, :], ma[:, :], 0.25 * F, mb[:, :], ALU.mult, ALU.add))
                norms[0] += 1
                V.tensor_scalar(mb[:, :], mb[:, :], 1.0 / F, LN_EPS, ALU.mult, ALU.add).then_inc(var_ready, 1)
                dve.wait_ge(std_ready, norms[0])
                link(V.reciprocal(rstd[:, :], rstd[:, :]))
                for b in range(NB):
                    loose(V.tensor_scalar(dst[:, b, :], src[:, b, :], mean[:, b:b + 1], rstd[:, b:b + 1], ALU.subtract, ALU.mult))
                settle()

            normalise(X, NX)
            dve.sem_inc(rows_ready[1], 1)
            dve.sem_inc(x_ready[1], 1)

            copy_xt(1)
            for i in range(BANKS):
                b = blocks(i)
                for k, n in enumerate(b):
                    loose(V.tensor_scalar(T1[:, n, :], ident[:, :], rc[:, n:n + 1], None, ALU.mult))
            settle()
            dve.sem_inc(rc_diag, 1)
            for i in range(BANKS):
                dve.wait_ge(rc_bc, i + 1)
                V.tensor_copy(rcB[:, cols(i)], PS[:, cols(i)]).then_inc(rc_cp, 1)
            link(V.tensor_tensor(bias3[:, :, :], cnt[:, :].unsqueeze(2).to_broadcast([P, NB, F]),
                                 bmsg[:, :].unsqueeze(1).to_broadcast([P, NB, F]), ALU.mult))
            link(V.tensor_tensor(bias3[:, :, :], bias3[:, :, :], bself[:, :].unsqueeze(1).to_broadcast([P, NB, F]), ALU.add))

            def plain_loop(L):
                with dve.Fori(0, npass) as ps:
                    dve.wait_ge(slot_free[L], ps * (NIT * R) + R)
                    set_pass(L, ps)
                    with dve.Fori(0, NIT) as it:
                        turn = dve.snap(ps * NIT + it)
                        for r in range(R):
                            dve.wait_ge(slot_free[L], turn * R + (r + 1))
                            one_hot(L, it, r, weighted=L == 2)

            def reset_pass():
                link(V.memset(pb[:, :], 0.0))

            reset_pass()
            with dve.Fori(0, npass) as ps:
                dve.wait_ge(slot_free[1], ps * (NIT * R) + R)
                set_pass(1, ps)

                def masks1(it, r):
                    dve.wait_ge(slot_free[1], (ps * NIT + it) * R + (r + 1))
                    one_hot(1, it, r)

                def iteration1(it, last):
                    for r in range(R):
                        g = (ps * NIT + it) * R + r
                        if r + 1 < R:
                            masks1(it, r + 1)
                        elif not last:
                            masks1(it + 1, 0)
                        dve.wait_ge(hid_act, g + 1)
                        V.tensor_tensor(hid[:, :, :], hid[:, :, :], We2[:, :].unsqueeze(1).to_broadcast([P, U, F]), ALU.mult).then_inc(prod_done, 1)
                        dve.wait_ge(prod_done, g + 1)
                        V.tensor_reduce(ew[:, bass.ds(it * (R * U) + r * U, U)], hid[:, :, :], AX, ALU.add).then_inc(hid_free, 1)

                masks1(0, 0)
                with dve.Fori(0, NIT - 1) as it:
                    iteration1(it, False)
                iteration1(NIT - 1, True)
            dve.wait_ge(slot_free[1], npass * (NIT * R) + R)
            read_sums(1, ALU.add, XT)
            for i in range(BANKS):
                b = blocks(i)
                s = slice(b[0], b[-1] + 1)
                dve.wait_ge(post1, i + 1)
                loose(V.scalar_tensor_tensor(NX[:, s, :], psum4(i), 0.0, X[:, s, :], ALU.max, ALU.add))
            settle()
            normalise(X, NX)
            dve.sem_inc(x_ready[2], 1)

            copy_xt(2)
            for i in range(BANKS):
                b = blocks(i)
                s = slice(b[0], b[-1] + 1)
                dve.wait_ge(mm2, i + 1)
                V.tensor_tensor(NX[:, s, :], psum4(i), bagg[:, :].unsqueeze(1).to_broadcast([P, len(b), F]), ALU.add).then_inc(mm2_used, 1)
            dve.wait_ge(ew_ready, 1)
            reset_pass()
            plain_loop(2)
            dve.wait_ge(slot_free[2], npass * (NIT * R) + R)
            read_sums(2, ALU.mult, rcB)
            for i in range(BANKS):
                b = blocks(i)
                s = slice(b[0], b[-1] + 1)
                dve.wait_ge(up2, i + 1)
                loose(V.tensor_tensor(NX[:, s, :], psum4(i), bu2[:, :].unsqueeze(1).to_broadcast([P, len(b), F]), ALU.add))
            settle()
            normalise(T1, NX)
            link(V.tensor_tensor(T1[:, :, :], T1[:, :, :], lng[:, :].unsqueeze(1).to_broadcast([P, NB, F]), ALU.mult))
            link(V.tensor_tensor(T1[:, :, :], T1[:, :, :], lnb[:, :].unsqueeze(1).to_broadcast([P, NB, F]), ALU.add))
            link(V.tensor_tensor(NX[:, :, :], T1[:, :, :], X[:, :, :], ALU.add))
            normalise(X, NX)
            dve.sem_inc(rows_ready[3], 1)
            dve.sem_inc(x_ready[3], 1)

            copy_xt(3)
            reset_pass()
            with dve.Fori(0, npass) as ps:
                dve.wait_ge(slot_free[3], ps * (NIT * R) + R)
                set_pass(3, ps)
                def masks3(it, r):
                    turn = ps * NIT + it
                    dve.wait_ge(slot_free[3], turn * R + (r + 1))
                    dve.wait_ge(row_in[1][r], turn * 16 + 16)
                    V.tensor_scalar(ohT[:, r, :], rowB[:, r, :], pmod[:, 0:1], None, ALU.is_equal).then_inc(ohT_ready[1], 1)
                    one_hot(3, it, r)
                    dve.wait_ge(ohT_ready[1], turn * R + (r + 1))
                    dve.sem_inc(row_free[1], 1)

                def iteration3(it, last):
                    turn = ps * NIT + it
                    for r in range(R):
                        if r + 1 < R:
                            masks3(it, r + 1)
                        elif not last:
                            masks3(it + 1, 0)
                        dve.wait_ge(got[3][r], turn * (16 * U) + 16 * U)
                        dve.sem_inc(idx_used[3], 1)
                        dve.wait_ge(rel_ready, turn * R + (r + 1))
                        v = vals[:, r * U:(r + 1) * U, 0:F]
                        V.tensor_tensor(v, v, B7.rearrange("p (u f) -> p u f", u=U), ALU.add).then_inc(vals_ready[1], 1)

                masks3(0, 0)
                with dve.Fori(0, NIT - 1) as it:
                    iteration3(it, False)
                iteration3(NIT - 1, True)
            dve.wait_ge(slot_free[3], npass * (NIT * R) + R)
            read_sums(3, ALU.mult, rcB)
            link(V.tensor_tensor(bias3[:, :, :], bias3[:, :, :], X[:, :, :], ALU.add))
            for i in range(BANKS):
                b = blocks(i)
                s = slice(b[0], b[-1] + 1)
                dve.wait_ge(post3, i + 1)
                loose(V.tensor_tensor(NX[:, s, :], psum4(i), bias3[:, s, :], ALU.add))
            settle()
            normalise(X, NX)
            dve.sem_inc(x_ready[4], 1)

        @block.tensor
        def _(pe):
            T = nc.tensor
            for L in range(4):
                pe.sem_inc(slot_free[L], R)
            pe.wait_ge(consts, 1)
            pe.wait_ge(x_in, 16 * (1 + (NB > 1)))

            def x_transposed(L):
                for i in range(BANKS):
                    for b in blocks(i):
                        o = T.transpose(PS[:, b * P:(b + 1) * P], X[:, b, :], ident[:, :])
                    o.then_inc(xt_tr[L], 1)

            def dense(dst_sem, ready, terms):
                for i in range(BANKS):
                    for s, ahead, most in ready:
                        pe.wait_ge(s, min(i + 1 + ahead, most))
                    for b in blocks(i):
                        for k, (lhs, rhs) in enumerate(terms):
                            o = T.matmul(PS[:, b * P:(b + 1) * P], lhs[:, b * P:(b + 1) * P], rhs,
                                         start=k == 0, stop=k == len(terms) - 1)
                    o.then_inc(dst_sem, 1)

            def zero_banks(n=7):
                for i in range(n):
                    T.matmul(PS[:, i * 512:(i + 1) * 512], zeros[0:1, 0:P], zeros[0:1, :], start=True, stop=False, skip_group_check=True)

            x_transposed(0)
            pe.wait_ge(w_in, 16 * 23)
            pe.wait_ge(lists_ready, 3)
            dense(mm0, [(xt_ready[0], 0, BANKS)], [(XT, W0[:, :])])
            pe.wait_ge(ext_ready, 1)
            T.transpose(B7[0:2 * H, 0:P], ext[:, :], ident[:, :]).then_inc(ext_tr, 1)
            pe.wait_ge(ext_diag, 1)
            T.matmul(B7[:, 0:2 * H], ones[0:2 * H, :], exq[:, :], start=True, stop=True)
            T.matmul(B7[:, 2 * H:2 * H + 1], ones[:, :], viol[:, :], start=True, stop=True).then_inc(ext_bc, 1)
            pe.wait_ge(mm0_used, BANKS)
            for k in range(2):
                for u in range(U):
                    o = T.transpose(PS[:, k * 512 + u * P:k * 512 + u * P + NG], edge_f[0:NG, k, u * P:(u + 1) * P], ident[0:NG, 0:NG])
                o.then_inc(edge_tr, 1)
            pe.wait_ge(attr_in, 16 * (1 + (REM > 0)))
            av = attr[:, :].rearrange("p (u j k) -> p u k j", u=U, k=4)
            for k in range(4):
                for u in range(U):
                    o = T.transpose(PS[:, (2 + k) * 512 + u * P:(2 + k) * 512 + u * P + NG], av[0:NG, u, k, :], ident[0:NG, 0:NG])
                o.then_inc(edge_tr, 1)
            pe.wait_ge(npass_ready, 1)
            T.transpose(B7[:, 0:P], Wmr[:, :], ident[:, :])
            T.transpose(B7[:, P:2 * P], Wsr[:, :], ident[:, :]).then_inc(wt_tr, 1)
            pe.wait_ge(wt_used, 1)
            npass, general = passes_of(pe)
            with pe.If(general == 1):
                with pe.Fori(0, NB) as w, pe.Fori(0, NCH) as c:
                    n = pe.snap(w * NCH + c)
                    pe.wait_ge(g_ready, n * 8 + w + 8)
                    T.matmul(B7, g_oh[:, :], g_dg[:, :, :].rearrange("p h e -> p (h e)"), start=True, stop=False)
                    T.matmul(B7, g_ohm[:, :], ident4[:, :, :].rearrange("p h e -> p (h e)"), start=False, stop=True).then_inc(g_mm, 1)
            pe.wait_ge(node_ready, 1)
            T.matmul(B7[:, 0:NB * 2 * H], swap[:, :], nodeE[:, :, :].rearrange("p b k -> p (b k)"), start=True, stop=True).then_inc(node_sw, 1)
            pe.wait_ge(edge_tr_used, 6)
            pe.wait_ge(nd_ready, 1)
            zero_banks(8)
            ndf = nd3[:, :, :, :].rearrange("p w t k -> p (w t k)")

            def slots(it):
                _, v = nc.values_load_multi_w_load_instructions(
                    slot_i[0:1, bass.ds(it * (R * U), R * U)], engines=[mybir.EngineType.PE], min_val=0, max_val=NSLOT - 1,
                    skip_runtime_bounds_check_because="set_pass() bounds them")
                return [v[r * U:(r + 1) * U] for r in range(R)]

            def scatter(r, u, w):
                s = r * U + u
                return T.matmul(PS[:, bass.ds(w * HALF, P)], vals[:, s, 0:F], oh[:, s, :],
                                start=False, stop=False, skip_group_check=True)

            with pe.Fori(0, npass) as ps:
                pe.wait_ge(pass_set[0], ps * 9 + 9)
                pe.sem_inc(passed, 1)

                def fetch(it, r, wins):
                    g = (ps * NIT + it) * R + r
                    pe.wait_ge(ohT_ready[0], g + 1)
                    pe.wait_ge(bank7_free[0], g + 1)
                    for u in range(U):
                        o = T.matmul(B7[:, NDP0 + u * NDP:NDP0 + (u + 1) * NDP], ohT[:, r, u * P:(u + 1) * P],
                                     ndf[:, bass.ds(wins[r][u] * NDP, NDP)], start=False, stop=False, skip_group_check=True)
                    o.then_inc(sd_ready, 1)

                def iteration(it, last):
                    wins = slots(it)
                    fetch(it, 0, wins)
                    for r in range(R):
                        g = (ps * NIT + it) * R + r
                        if r + 1 < R:
                            fetch(it, r + 1, wins)
                        pe.wait_ge(oh_ready[0], g + 1)
                        pe.wait_ge(vals_ready[0], g + 1)
                        for u in range(U):
                            scatter(r, u, wins[r][u])
                        pe.wait_ge(bank7_free[0], g + (3 if r + 1 < R else 2))
                        for u in range(U):
                            o = T.matmul(DENP[:, bass.ds(wins[r][u] * DW, DW)], oh[:, r * U + u, :], wr[:, r, u, :],
                                         start=False, stop=False, skip_group_check=True)
                        o.then_inc(slot_free[0], 1)

                with pe.Fori(0, NIT) as it:
                    iteration(it, False)
            pe.wait_ge(den_ready, 1)
            pe.wait_ge(t_ready, npass * (NIT * R))
            T.matmul(B7[:, 0:NSLOT * DW], swap[:, :], D[:, :, :].rearrange("p w k -> p (w k)"), start=True, stop=True).then_inc(den_sw, 1)
            for i in range(BANKS):
                pe.wait_ge(acc_read[0], min(i + 2, ABANKS))
                for b in blocks(i):
                    o = T.transpose(PS[:, b * P:(b + 1) * P], AG[:, b * P:(b + 1) * P], ident[:, :])
                o.then_inc(back, 1)

            pe.wait_ge(x_ready[1], 1)
            x_transposed(1)
            pe.wait_ge(rc_diag, 1)
            pe.wait_ge(xt_ready[1], BANKS)
            for i in range(BANKS):
                for b in blocks(i):
                    o = T.matmul(PS[:, b * P:(b + 1) * P], ones[:, :], T1[:, b, :], start=True, stop=True)
                o.then_inc(rc_bc, 1)
            pe.wait_ge(rc_cp, BANKS)
            zero_banks()
            pe.wait_ge(parts_ready, 1)
            with pe.Fori(0, npass) as ps:
                pe.wait_ge(pass_set[1], ps * 9 + 9)
                pe.sem_inc(passed, 1)
                with pe.Fori(0, NIT) as it:
                    turn = pe.snap(ps * NIT + it)
                    wins = slots(it)
                    for r in range(R):
                        g = turn * R + r
                        pe.wait_ge(attr_cp, g + 1)
                        T.transpose(B7[:, 0:HALF].bitcast(bf16), ar[:, :], identb[:, :]).then_inc(attr_tr, 1)
                        pe.wait_ge(oh_ready[1], g + 1)
                        pe.wait_ge(got[1][r], turn * (16 * U) + 16 * U)
                        pe.sem_inc(idx_used[1], 1)
                        scatter(r, 0, wins[r][0])
                        pe.wait_ge(attr_T, g + 1)
                        T.matmul(B7, arT[0:ATK, :], We1b[0:ATK, :], start=True, stop=True).then_inc(hid_mm, 1)
                        for u in range(1, U):
                            o = scatter(r, u, wins[r][u])
                        o.then_inc(slot_free[1], 1)
            dense(post1, [(acc_read[1], 1, ABANKS)], [(AG, W1[:, :])])

            pe.wait_ge(x_ready[2], 1)
            x_transposed(2)
            dense(mm2, [(xt_ready[2], 0, BANKS)], [(XT, Wagg[:, :])])
            pe.wait_ge(mm2_used, BANKS)
            zero_banks()

            with pe.Fori(0, npass) as ps:
                pe.wait_ge(pass_set[2], ps * 9 + 9)
                pe.sem_inc(passed, 1)
                with pe.Fori(0, NIT) as it:
                    turn = pe.snap(ps * NIT + it)
                    wins = slots(it)
                    for r in range(R):
                        pe.wait_ge(oh_ready[2], turn * R + (r + 1))
                        pe.wait_ge(got[2][r], turn * (16 * U) + 16 * U)
                        pe.sem_inc(idx_used[2], 1)
                        for u in range(U):
                            o = scatter(r, u, wins[r][u])
                        o.then_inc(slot_free[2], 1)
            for i in range(BANKS):
                pe.wait_ge(acc_read[2], min(i + 2, ABANKS))
                T.matmul(PS[:, cols(i)], Wu1[:, 0, :], XT[:, cols(i)], start=True, stop=False)
                T.matmul(PS[:, cols(i)], Wu1[:, 1, :], AG[:, cols(i)], start=False, stop=True).then_inc(up1, 1)
            dense(up2, [(up1_act, 0, BANKS)], [(T1f, Wu2[:, :]), (XT, Wres[:, :])])

            pe.wait_ge(x_ready[3], 1)
            x_transposed(3)
            pe.wait_ge(xt_ready[3], BANKS)
            zero_banks()
            pe.wait_ge(ew_ready, 1)
            pe.sem_inc(passed, 1)
            with pe.Fori(0, npass) as ps:
                pe.wait_ge(pass_set[3], ps * 9 + 9)
                pe.sem_inc(passed, 1)
                with pe.Fori(0, NIT) as it:
                    turn = pe.snap(ps * NIT + it)
                    wins = slots(it)

                    def relations(r):
                        pe.wait_ge(ohT_ready[1], turn * R + (r + 1))
                        pe.wait_ge(bank7_free[1], 1)
                        if r:
                            pe.wait_ge(vals_ready[1], turn * R + r)
                        for u in range(U):
                            for k in range(2):
                                o = T.matmul(B7[:, u * F:(u + 1) * F], ohT[:, r, u * P:(u + 1) * P], relb[:, k, :], start=k == 0, stop=k == 1)
                        o.then_inc(rel_ready, 1)

                    relations(0)
                    for r in range(R):
                        pe.wait_ge(vals_ready[1], turn * R + (r + 1))
                        if r + 1 < R:
                            relations(r + 1)
                        pe.wait_ge(oh_ready[3], turn * R + (r + 1))
                        for u in range(U):
                            o = scatter(r, u, wins[r][u])
                        o.then_inc(slot_free[3], 1)
            dense(post3, [(acc_read[3], 1, ABANKS)], [(XT, WsT[:, :]), (AG, WmT[:, :])])


_INS = {'x': 'x', 'src': 'src', 'dst': 'dst', 'attr': 'edge_attr_4', 'typ': 'edge_type_64',
        'W_w': 'L0_gnn_W_w', 'W_b': 'L0_gnn_W_b', 'a_w': 'L0_gnn_a_w', 'a_b': 'L0_gnn_a_b', 'W1': 'L1_gnn_W',
        'agg_W': 'L2_gnn_agg_W', 'agg_b': 'L2_gnn_agg_b', 'edge_W1': 'L2_gnn_edge_W1', 'edge_b1': 'L2_gnn_edge_b1',
        'edge_W2': 'L2_gnn_edge_W2', 'edge_b2': 'L2_gnn_edge_b2', 'upd_W1': 'L2_gnn_upd_W1',
        'upd_b1': 'L2_gnn_upd_b1', 'upd_W2': 'L2_gnn_upd_W2', 'upd_b2': 'L2_gnn_upd_b2', 'ln_g': 'L2_gnn_ln_g',
        'ln_b': 'L2_gnn_ln_b', 'res_W': 'L2_gnn_res_W', 'W_self': 'L3_gnn_W_self', 'b_self': 'L3_gnn_b_self',
        'W_msg': 'L3_gnn_W_msg', 'b_msg': 'L3_gnn_b_msg', 'rel_emb': 'L3_gnn_rel_emb'}


def kernel(**inputs):
    import numpy as _np
    import concourse.bacc as _bacc
    from concourse import mybir as _mybir
    from concourse.bass_utils import run_bass_kernel_spmd as _run

    nc = _bacc.Bacc("TRN2", target_bir_lowering=False, num_devices=1)
    arrays, args = {}, {}
    for short, name in _INS.items():
        a = _np.ascontiguousarray(inputs[name])
        arrays[f"in_{name}"] = a
        args[short] = nc.dram_tensor(f"in_{name}", a.shape, _mybir.dt.from_np(a.dtype), kind="ExternalInput").ap()
    shape = inputs["x"].shape
    out = nc.dram_tensor("out", shape, _mybir.dt.float32, kind="ExternalOutput").ap()
    gnn_kernel(nc, args, out)
    return _run(nc, [arrays], core_ids=[0]).results[0]["out"]
```

```python
import concourse.bass as bass
from concourse import mybir
from contextlib import ExitStack

fp32 = mybir.dt.float32
bf16 = mybir.dt.bfloat16
i32 = mybir.dt.int32
ALU = mybir.AluOpType
ACT = mybir.ActivationFunctionType
AX = mybir.AxisListType.X

P = 128
F = 128
H = 4
FH = F // H
R = 4
U = 4
AHEAD = R - 1
HALF = 64
STRIDE = 448
SHARED = 512 - STRIDE
NDP = 3 * 2 * H
ATT = 96
ATK = ATT + 3
ROW0 = F + H
KW = F + 2 * H
KB = 3
DW = H + 1
NREL = 64
BIG = 1.0e30
PAD_DST = 1000000
SAFE_RANGE = 60.0
LN_EPS = 1e-5
SLOPE = 0.2


def gnn_kernel(nc, ins, out):
    N = ins["x"].shape[0]
    E = ins["src"].shape[0]
    NB = -(-N // P)
    LASTR = N - (NB - 1) * P
    NN = NB * P
    NCH = -(-E // (P * R * U)) * R * U
    NG = NCH // U
    NIT = NG // R
    GE = U * P
    FULLP = E // GE
    REM = E - FULLP * GE
    NWIN = 2 * NB - 1
    BANKS = -(-NB // 4)
    ABANKS = (NWIN - 1) // 7 + 1
    NSLOT = NWIN + ABANKS - 1
    assert BANKS <= 7 and ABANKS <= 7 and NG <= P and NWIN * 37 < 7 * 256 + 37 
    assert NIT > 1 and NB > 1

    HBANK = (BANKS + 1) // 2
    HNB = 4 * HBANK
    QBANK = HBANK // 2
    QNB = 4 * QBANK
    PIECES = [(0, QNB), (QNB, HNB), (HNB, NB)]
    ACT1 = range(0, HNB - 4)
    ACT2 = range(NB - (NB - HNB) // 2, NB)
    assert QNB and QNB <= ACT1[-1] and HNB < ACT2[0]
    KGROUPS = -(-NB // KB)

    def blocks(i):
        return range(4 * i, min(4 * i + 4, NB))

    def bank_nodes(k):
        n0 = STRIDE * k + (SHARED if k else 0)
        n1 = min(STRIDE * k + 512, NN)
        return slice(n0, n1), slice(n0 + SHARED * k, n1 + SHARED * k)

    def nodes(i):
        return slice(blocks(i)[0], blocks(i)[-1] + 1)

    def piece_of(i):
        return 0 if i < QBANK else 1 if i < HBANK else 2

    def cols(i):
        return slice(blocks(i)[0] * P, (blocks(i)[-1] + 1) * P)

    tab = [nc.dram_tensor("tab0", (NN, ROW0), fp32, kind="Internal").ap()]
    tab += [nc.dram_tensor(f"tab{n}", (NN, F), fp32, kind="Internal").ap() for n in (1, 2, 3)]
    win_d = nc.dram_tensor("win_d", (1, NCH), fp32, kind="Internal").ap()
    rel_d = nc.dram_tensor("rel_d", (1, NCH * P), bf16, kind="Internal").ap()
    typ_d = nc.dram_tensor("typ_d", (1, NCH * P), bf16, kind="Internal").ap()

    ctx = ExitStack()
    with ctx:
        def sb(name, shape, dt=fp32):
            return ctx.enter_context(nc.sbuf_tensor(name, shape, dt))

        def sem(name):
            return ctx.enter_context(nc.semaphore(name))

        X = sb("X", [P, NB, F])
        XT = sb("XT", [P, NN])
        ag = sb("ag", [P, max(NN, 3 * GE)])
        AG = ag[:, 0:NN]
        edge_raw = ag[:, 0:3 * GE].bitcast(i32).rearrange("p (k j) -> p k j", k=3)
        T0 = sb("T0", [P, NB, ROW0])
        bias3 = T0[:, :, 0:F]
        T1 = sb("T1", [P, NB, F])
        nx = sb("nx", [P, max(NB * F, GE * 4)])
        NX = nx[:, 0:NB * F].rearrange("p (b f) -> p b f", f=F)
        attr = nx[:, 0:GE * 4]
        T1f = T1[:, :, :].rearrange("p b f -> p (b f)")
        rcB = sb("rcB", [P, NN])
        vals = sb("vals", [P, R * U, ROW0])
        oh = sb("oh", [P, R * U, P])
        ohT = sb("ohT", [P, R, GE], bf16)
        rowB = sb("rowB", [P, R, GE], bf16)
        idx = sb("idx", [P, R * U], i32)
        srcT = sb("srcT", [P, NCH + R * U], i32)
        dstT = sb("dstT", [P, NCH])
        relT = sb("relT", [P, NCH])
        relc = sb("relc", [P, GE], bf16)
        cwinc = sb("cwinc", [P, U])
        winB = sb("winB", [P, NCH])
        winc = sb("winc", [P, NCH])
        win_i = sb("win_i", [1, NCH], i32)
        slot_i = sb("slot_i", [1, NCH], i32)
        edge_f = sb("edge_f", [P, 3, GE])
        typ_b = sb("typ_b", [P, GE], bf16)
        attrE = sb("attrE", [P, NG, U * 4])
        attrS = sb("attrS", [P, NG, ATT], bf16)
        ar = sb("ar", [P, P], bf16)
        arT = sb("arT", [P, P], bf16)
        hid = sb("hid", [P, U, F])
        hv = hid
        W0T = oh[:, 0, :]
        ew = sb("ew", [P, NCH])
        iota_i = sb("iota_i", [P, P], i32)
        pcol_i = sb("pcol_i", [P, 1], i32)
        iota = sb("iota", [P, P])
        pcol = sb("pcol", [P, 1])
        ident = sb("ident", [P, P])
        identb = sb("identb", [P, P], bf16)
        pmod = sb("pmod", [P, 1])
        psel = sb("psel", [P, 3])
        ptmp = sb("ptmp", [P, 1])
        ident4 = sb("ident4", [P, 4, P])
        swap = sb("swap", [P, P])
        ones = sb("ones", [P, P])
        zeros = sb("zeros", [1, 512], bf16)
        W0 = sb("W0", [F, KW])
        W1 = sb("W1", [F, F])
        Wagg = sb("Wagg", [F, F])
        Wu1 = sb("Wu1", [F, 2, F])
        Wu2 = sb("Wu2", [F, F])
        Wres = sb("Wres", [F, F])
        Wmr = sb("Wmr", [F, F])
        Wsr = sb("Wsr", [F, F])
        WmT = sb("WmT", [F, F])
        WsT = sb("WsT", [F, F])
        We1 = oh[:, 0:U, :].rearrange("p a f -> p (a f)")
        We1b = sb("We1b", [P, U * F], bf16)
        We2 = sb("We2", [P, F])
        rel = sb("rel", [P, F])
        relb = sb("relb", [P, 2, F], bf16)
        b0 = sb("b0", [P, KW])
        aw = sb("aw", [P, H, 2, FH])
        eW1 = sb("eW1", [4, F])
        eb1 = sb("eb1", [1, F])
        m16_i = sb("m16_i", [4, P], i32)
        m16 = sb("m16", [4, P])
        S = sb("S", [4, U, P])
        S1 = sb("S1", [1, P])
        A = sb("A", [F, 2 * H])
        left = sb("left", [P, U * 4])
        ab = sb("ab", [P, H])
        bagg = sb("bagg", [P, F])
        bu2 = sb("bu2", [P, F])
        lng = sb("lng", [P, F])
        lnb = sb("lnb", [P, F])
        bself = sb("bself", [P, F])
        bmsg = sb("bmsg", [P, F])
        be2 = sb("be2", [P, 1])
        bu1 = sb("bu1", [F, 1])
        sd = sb("sd", [P, NB, H])
        mx = sb("mx", [P, NB, H])
        zz = sb("zz", [P, NB, H])
        nodeE = sb("nodeE", [P, NB, 2 * H])
        nd = sb("nd", [P, NSLOT, 2 * H])
        ndr = sb("ndr", [P, NSLOT, 2 * H])
        nd3 = sb("nd3", [P, NSLOT, 3, 2 * H], bf16)
        wself = sb("wself", [P, NB, H])
        ext = sb("ext", [P, 2 * H])
        exq = sb("exq", [2 * H, 2 * H])
        exc = sb("exc", [2 * H, 1])
        exB = sb("exB", [P, 2 * H])
        rng = sb("rng", [P, H])
        rng1 = sb("rng1", [P, 1])
        cmin = sb("cmin", [P, U])
        cmax = sb("cmax", [P, U])
        cwin_i = sb("cwin_i", [P, U], i32)
        cwin = sb("cwin", [P, U])
        cspan = sb("cspan", [P, U])
        viol = sb("viol", [P, 1])
        inside = sb("inside", [P, 1])
        isfast = sb("isfast", [P, 1])
        npass_f = sb("npass_f", [P, 2])
        npass_i = sb("npass_i", [P, 2], i32)
        pb = sb("pb", [P, 1])
        pstep = sb("pstep", [P, 1])
        dn = sb("dn", [P, R, U, 2 * H])
        z = sb("z", [P, R, U, H])
        lz = sb("lz", [P, R, U, H])
        tt = sb("tt", [P, R, U, H])
        wr = sb("wr", [P, R, U, DW])
        D = sb("D", [P, NSLOT, DW])
        shared = sb("shared", [P, ABANKS, SHARED])
        den = sb("den", [P, NB, DW])
        rden = sb("rden", [P, NB, H])
        st = sb("st", [P, NB, 6])
        ma = sb("ma", [P, NB])
        mb = sb("mb", [P, NB])
        mean2 = sb("mean2", [P, NB])
        eps = sb("eps", [P, 1])
        rstd = sb("rstd", [P, NB])
        shift = sb("shift", [P, NB])
        cnt = sb("cnt", [P, NB])
        rc = sb("rc", [P, NB])
        g_idx = sb("g_idx", [P, 1], i32)
        g_row = sb("g_row", [P, ROW0])
        g_oh = sb("g_oh", [P, P])
        g_ohm = sb("g_ohm", [P, P])
        g_dg = sb("g_dg", [P, H, P])
        g_m = sb("g_m", [P, H])
        g_base = sb("g_base", [P, 1])

        PS = ctx.enter_context(nc.psum_tensor("PS", [P, 4096], fp32))
        B7 = PS[:, 3584:4096]
        DENP = B7[:, 0:NSLOT * DW]
        NDP0 = 512 - U * NDP

        padded = sem("padded")
        pool_pads = sem("pool_pads")
        w0_in = sem("w0_in")
        w0_tr = sem("w0_tr")
        w0_cp = sem("w0_cp")
        heads_ready = sem("heads_ready")
        sel_ready = sem("sel_ready")
        we1_mm = sem("we1_mm")
        part_act = sem("part_act")
        edge_cast = sem("edge_cast")
        place_step = sem("place_step")
        dst_cp = sem("dst_cp")
        attr_cols = sem("attr_cols")
        part_dve = sem("part_dve")
        dup_done = sem("dup_done")
        x_first = sem("x_first")
        x_in = sem("x_in")
        edges_in = sem("edges_in")
        attr_in = sem("attr_in")
        w_in = sem("w_in")
        iotas = sem("iotas")
        consts = sem("consts")
        lists_out = sem("lists_out")
        lists_in = sem("lists_in")
        lists_ready = sem("lists_ready")
        edge_tr = sem("edge_tr")
        edge_tr_used = sem("edge_tr_used")
        wt_tr = sem("wt_tr")
        wt_used = sem("wt_used")
        ext_ready = sem("ext_ready")
        ext_tr = sem("ext_tr")
        ext_diag = sem("ext_diag")
        ext_bc = sem("ext_bc")
        npass_ready = sem("npass_ready")
        node_ready = sem("node_ready")
        node_sw = sem("node_sw")
        nd_ready = sem("nd_ready")
        even_ready = sem("even_ready")
        dve_order = sem("dve_order")
        xt_tr = sem("xt_tr")
        xt_ready = sem("xt_ready")
        xt_rest = sem("xt_rest")
        mm0 = sem("mm0")
        mm0_used = sem("mm0_used")
        mm2 = sem("mm2")
        mm2_used = sem("mm2_used")
        silu2 = sem("silu2")
        table_ready = sem("table_ready")
        norm_act = sem("norm_act")
        norm_dve = sem("norm_dve")
        scale_ready = sem("scale_ready")
        wk_ready = sem("wk_ready")
        joined = sem("joined")
        div_done = sem("div_done")
        x_added = sem("x_added")
        g_done = sem("g_done")
        cnt_ready = sem("cnt_ready")
        bias3_step = sem("bias3_step")
        xr = sem("xr")
        xr_used = sem("xr_used")
        upx = sem("upx")
        upx_used = sem("upx_used")
        up1_sum = sem("up1_sum")
        var_ready = sem("var_ready")
        std_ready = sem("std_ready")
        wself_in = sem("wself_in")
        wself_ready = sem("wself_ready")
        pass_set = [sem(f"pass_set{n}") for n in range(4)]
        slot_free = [sem(f"slot_free{n}") for n in range(4)]
        idx_used = [sem(f"idx_used{n}") for n in range(4)]
        idx_in = [sem(f"idx_in{r}") for r in range(R)]
        got = [[sem(f"got{n}_{r}") for r in range(R)] for n in range(4)]
        row_in = [[sem(f"row_in{n}_{r}") for r in range(R)] for n in range(2)]
        row_free = [sem(f"row_free{n}") for n in range(2)]
        oh_ready = [sem(f"oh_ready{n}") for n in range(4)]
        ohT_ready = [sem(f"ohT_ready{n}") for n in range(2)]
        bank7_free = sem("bank7_free")
        sd_ready = sem("sd_ready")
        z_done = sem("z_done")
        parts_ready = sem("parts_ready")
        t_sub = sem("t_sub")
        lz_done = sem("lz_done")
        t_ready = sem("t_ready")
        w_ready = sem("w_ready")
        vals_ready = [sem(f"vals_ready{n}") for n in range(2)]
        rel_ready = sem("rel_ready")
        relc_ready = sem("relc_ready")
        rel_out = sem("rel_out")
        dn_done = sem("dn_done")
        hid_free = sem("hid_free")
        prod_done = sem("prod_done")
        attr_cp = sem("attr_cp")
        attr_tr = sem("attr_tr")
        attr_T = sem("attr_T")
        hid_mm = sem("hid_mm")
        hid_act = sem("hid_act")
        ew_ready = sem("ew_ready")
        acc_read = sem("acc_read")
        den_ready = sem("den_ready")
        den_sw = sem("den_sw")
        back = sem("back")
        post1 = sem("post1")
        rc_diag = sem("rc_diag")
        rc_bc = sem("rc_bc")
        rc_cp = sem("rc_cp")
        up1 = sem("up1")
        up1_act = sem("up1_act")
        up2 = sem("up2")
        post3 = sem("post3")
        out_done = sem("out_done")
        passed = sem("passed")
        g_ready = sem("g_ready")
        g_idx_ready = sem("g_idx_ready")
        g_got = sem("g_got")
        g_mm = sem("g_mm")

        block = ctx.enter_context(nc.Block())

        PASS_STEPS = 7
        W_LOADS = 21
        W0_LOADS = 4

        def row(v):
            return v.rearrange("(o f) -> o f", o=1).to_broadcast([P, v.shape[0]])

        def col(v):
            return v.rearrange("(f o) -> f o", o=1)

        def norm_wait(eng, n, piece=2):
            eng.wait_ge(norm_act, 3 * n - 2 + piece)
            if piece:
                eng.wait_ge(norm_dve, 2 * n - 2 + piece)

        def xt_wait(eng, L, i):
            if L == 0:
                eng.wait_ge(xt_ready, i + 1)
            elif i < HBANK:
                eng.wait_ge(xt_ready, BANKS + (L - 1) * HBANK + i + 1)
            else:
                eng.wait_ge(xt_rest, (L - 1) * (BANKS - HBANK) + i - HBANK + 1)

        def passes_of(eng):
            eng.wait_ge(npass_ready, 1)
            n = eng.value_load(npass_i[0:1, 0:1], min_val=1, max_val=NB)
            g = eng.value_load(npass_i[0:1, 1:2], min_val=0, max_val=1)
            return n, g

        @block.sync
        def _(sp):
            sp.wait_ge(padded, 1)

            def x_load(b0_, b1_):
                return sp.dma_start(X[:, b0_:b1_, :], ins["x"][b0_ * P:b1_ * P, :].rearrange("(b p) f -> p b f", p=P))

            x_load(0, HNB).then_inc(x_first, 16)
            for dst, src in [(W0[:, 0:F], ins["W_w"]), (aw[:, :, :, :].rearrange("p h t f -> p (h t f)"), row(ins["a_w"].rearrange("h f -> (h f)"))),
                             (b0[:, 0:F], row(ins["W_b"])), (ab[:, :], row(ins["a_b"]))]:
                sp.dma_start(dst, src).then_inc(w0_in, 16)
            sp.wait_ge(padded, 3)
            for k, name in enumerate(("src", "dst", "typ")):
                v = ins[name]
                sp.dma_start(edge_raw[0:FULLP, k, :], v[0:FULLP * GE].rearrange("(p j) -> p j", j=GE)).then_inc(edges_in, 16)
                if REM:
                    sp.dma_start(edge_raw[FULLP:FULLP + 1, k, 0:REM],
                                 v[FULLP * GE:E].rearrange("(p j) -> p j", p=1)).then_inc(edges_in, 16)
            x_load(HNB, NB - 1).then_inc(x_in, 16)
            sp.dma_start(X[0:LASTR, NB - 1, :], ins["x"][(NB - 1) * P:N, :]).then_inc(x_in, 16)
            sp.wait_ge(pool_pads, 1)
            sp.dma_start(attr[0:FULLP, :], ins["attr"][0:FULLP * GE, :].rearrange("(p j) k -> p (j k)", j=GE)).then_inc(attr_in, 16)
            if REM:
                sp.dma_start(attr[FULLP:FULLP + 1, 0:REM * 4],
                             ins["attr"][FULLP * GE:E, :].rearrange("(p j) k -> p (j k)", p=1)).then_inc(attr_in, 16)
            loads = [
                (Wsr[:, :], ins["W_self"]), (Wmr[:, :], ins["W_msg"]),
                (W1[:, :], ins["W1"]), (Wagg[:, :], ins["agg_W"]),
                (bagg[:, :], row(ins["agg_b"])), (We2[:, :], row(ins["edge_W2"].rearrange("f o -> (f o)"))),
                (be2[:, :], row(ins["edge_b2"])), (Wu1[:, 0, :], ins["upd_W1"][0:F, :]),
                (Wu1[:, 1, :], ins["upd_W1"][F:2 * F, :]), (bu1[:, :], col(ins["upd_b1"])),
                (Wu2[:, :], ins["upd_W2"]), (bu2[:, :], row(ins["upd_b2"])), (lng[:, :], row(ins["ln_g"])),
                (lnb[:, :], row(ins["ln_b"])), (Wres[:, :], ins["res_W"]),
                (bself[:, :], row(ins["b_self"])), (bmsg[:, :], row(ins["b_msg"])),
                (eW1[:, :], ins["edge_W1"]), (eb1[:, :], ins["edge_b1"].rearrange("(o f) -> o f", o=1)),
                (rel[0:NREL, :], ins["rel_emb"]), (rel[NREL:2 * NREL, :], ins["rel_emb"]),
            ]
            assert len(loads) == W_LOADS
            for dst, src in loads:
                sp.dma_start(dst, src).then_inc(w_in, 16)

            sp.wait_ge(lists_ready, 3)
            sp.dma_start(win_d.rearrange("o (g u) -> (o g) u", u=U), cwin[0:NG, :]).then_inc(lists_out, 16)
            sp.dma_start(typ_d.rearrange("o (g j) -> (o g) j", j=GE), typ_b[0:NG, :]).then_inc(lists_out, 16)

            for L in range(4):
                rows = {0: T0[:, :, :], 1: X[:, :, :], 2: T1[:, :, :], 3: X[:, :, :]}[L]
                t = tab[L].rearrange("(b p) f -> p b f", p=P)
                for piece, (b0_, b1_) in enumerate(PIECES):
                    if L == 0:
                        sp.wait_ge(mm0_used, -(-b1_ // KB))
                    elif L == 2:
                        sp.wait_ge(silu2, -(-b1_ // 4))
                    else:
                        norm_wait(sp, L if L == 1 else 4, piece)
                    sp.dma_start(t[:, b0_:b1_, :], rows[:, b0_:b1_, :]).then_inc(table_ready, 16)
                if L == 0:
                    sp.wait_ge(edge_tr_used, 1)
                    for r in range(R):
                        sp.dma_start(idx[:, r * U:(r + 1) * U], srcT[:, r * U:(r + 1) * U]).then_inc(idx_in[r], 16)
                    sp.wait_ge(lists_out, 32)
                    sp.dma_start(winB[:, :], win_d.to_broadcast([P, NCH])).then_inc(lists_in, 16)
                    npass, _ = passes_of(sp)
                with sp.Fori(0, npass) as ps:
                    k = L // 3

                    def row_load(turn, it, r):
                        sp.wait_ge(row_free[k], turn * R + (r + 1))
                        sp.dma_start(rowB[:, r, :], (rel_d, typ_d)[k][:, bass.ds(it * (R * GE) + r * GE, GE)].to_broadcast([P, GE])).then_inc(row_in[k][r], 16)

                    if L == 0:
                        sp.wait_ge(relc_ready, ps + 1)
                        sp.dma_start(rel_d.rearrange("o (g j) -> (o g) j", j=GE), relc[0:NG, :]).then_inc(rel_out, 16)
                        sp.wait_ge(rel_out, ps * 16 + 16)
                        sp.sem_inc(passed, 1)
                    if L in (0, 3):
                        for r in range(AHEAD):
                            row_load(ps * NIT, 0, r)

                    def iteration(it, last):
                        turn = ps * NIT + it
                        for r in range(R):
                            sp.wait_ge(idx_used[L], turn * R + (r + 1))
                            sp.dma_start(idx[:, r * U:(r + 1) * U],
                                         srcT[:, bass.ds(it * (R * U) + (R + r) * U, U)]).then_inc(idx_in[r], 16)
                            if L in (0, 3):
                                if r + AHEAD < R:
                                    row_load(turn, it, r + AHEAD)
                                elif not last:
                                    row_load(turn + 1, it + 1, r + AHEAD - R)

                    with sp.Fori(0, NIT - 1) as it:
                        iteration(it, False)
                    iteration(NIT - 1, True)

            for piece, (b0_, b1_) in enumerate(PIECES):
                norm_wait(sp, 5, piece)
                b1_ = min(b1_, NB - 1)
                sp.dma_start(out[b0_ * P:b1_ * P, :].rearrange("(b p) f -> p b f", p=P), X[:, b0_:b1_, :]).then_inc(out_done, 16)
            sp.dma_start(out[(NB - 1) * P:N, :], X[0:LASTR, NB - 1, :]).then_inc(out_done, 16)
            sp.wait_ge(out_done, 16 * 4)

        @block.gpsimd
        def _(pool):
            nc.gpsimd.iota(iota_i[:, :], pattern=[[1, P]], base=0, channel_multiplier=0).then_inc(iotas, 1)
            nc.gpsimd.iota(m16_i[:, :], pattern=[[0, P // 16], [1, 16]], base=0, channel_multiplier=0).then_inc(iotas, 1)
            nc.gpsimd.iota(pcol_i[:, :], pattern=[[0, 1]], base=0, channel_multiplier=1).then_inc(iotas, 1)
            nc.gpsimd.memset(attr[:, :], 0.0).then_inc(pool_pads, 1)
            nc.gpsimd.memset(nd[:, :, :], 0.0).then_inc(pool_pads, 1)
            nc.gpsimd.memset(wr[:, :, :, :], 1.0).then_inc(pool_pads, 1)
            nc.gpsimd.memset(den[:, :, :], 0.0).then_inc(pool_pads, 1)
            nc.gpsimd.memset(ar[:, :], 1.0).then_inc(pool_pads, 1)
            nc.gpsimd.memset(zeros[:, :], 0.0).then_inc(pool_pads, 1)

            def gather(L, turn, loads):
                width = ROW0 if L == 0 else F
                for r in range(R):
                    pool.wait_ge(slot_free[L], turn * R + (r + 1))
                    pool.wait_ge(idx_in[r], loads * 16 + 16)
                    pool.sem_inc(passed, 1)
                    for u in range(U):
                        s = r * U + u
                        nc.gpsimd.indirect_dma_start(
                            vals[:, s, 0:width], None, tab[L],
                            bass.IndirectOffsetOnAxis(ap=idx[:, s:s + 1], axis=0)).then_inc(got[L][r], 16)

            pool.wait_ge(table_ready, 16 * len(PIECES))
            gather(0, 0, 0)
            npass, general = passes_of(pool)
            with pool.If(general == 1):
                with pool.Fori(0, NB * NCH) as n:
                    pool.wait_ge(g_idx_ready, n + 1)
                    pool.sem_inc(passed, 1)
                    nc.gpsimd.indirect_dma_start(g_row[:, :], None, tab[0],
                                                 bass.IndirectOffsetOnAxis(ap=g_idx[:, 0:1], axis=0)).then_inc(g_got, 16)
            G = nc.gpsimd
            for L in range(4):
                if L == 1:
                    pool.wait_ge(wself_ready, 1)
                    G.tensor_tensor(NX.rearrange("p b (h f) -> p b h f", h=H), T0[:, :, 0:F].rearrange("p b (h f) -> p b h f", h=H),
                                    wself[:, :, :].unsqueeze(3).to_broadcast([P, NB, H, FH]), ALU.mult).then_inc(wk_ready, 1)
                    pool.wait_ge(wk_ready, 1)
                    for i in range(BANKS):
                        pool.wait_ge(div_done, i + 1)
                        G.tensor_tensor(NX[:, nodes(i), :], NX[:, nodes(i), :], X[:, nodes(i), :], ALU.add).then_inc(x_added, 1)
                if L == 2:
                    pool.wait_ge(cnt_ready, 1)
                    G.tensor_tensor(bias3[:, :, :], cnt[:, :].unsqueeze(2).to_broadcast([P, NB, F]),
                                    bmsg[:, :].unsqueeze(1).to_broadcast([P, NB, F]), ALU.mult).then_inc(bias3_step, 1)
                    pool.wait_ge(bias3_step, 1)
                    G.tensor_tensor(bias3[:, :, :], bias3[:, :, :],
                                    bself[:, :].unsqueeze(1).to_broadcast([P, NB, F]), ALU.add).then_inc(bias3_step, 1)
                if L == 3:
                    for i in range(BANKS):
                        norm_wait(pool, 3, piece_of(i))
                        G.tensor_tensor(T1[:, nodes(i), :], T1[:, nodes(i), :],
                                        lng[:, :].unsqueeze(1).to_broadcast([P, len(blocks(i)), F]), ALU.mult).then_inc(g_done, 1)
                pool.wait_ge(table_ready, 16 * len(PIECES) * (L + 1))
                if L == 0:
                    with pool.Fori(1, npass * NIT) as turn:
                        gather(0, turn, turn)
                else:
                    with pool.Fori(0, npass * NIT) as turn:
                        gather(L, turn, pool.snap(npass * (L * NIT) + turn))

        @block.scalar
        def _(act):
            act.wait_ge(w0_tr, 1)
            nc.scalar.copy(W0T, B7[:, 0:F]).then_inc(w0_cp, 1)
            act.wait_ge(w0_tr, 2)
            nc.scalar.copy(W0[:, F:KW], B7[:, 0:2 * H]).then_inc(w0_cp, 1)
            for i in range(BANKS):
                act.wait_ge(xt_tr, i + 1)
                nc.scalar.copy(XT[:, cols(i)], PS[:, cols(i)]).then_inc(xt_ready, 1)

            def columns(i):
                return PS[:, i * 512:i * 512 + U * P].rearrange("p (u g) -> p u g", u=U)[:, :, 0:NG]

            act.wait_ge(edge_tr, 2)
            nc.scalar.copy(dstT[:, :].rearrange("p (g u) -> p u g", u=U), columns(7)).then_inc(dst_cp, 1)
            for k in range(4):
                act.wait_ge(edge_tr, 3 + k)
                nc.scalar.copy(attrE[:, :, :].rearrange("p g (u k) -> p k u g", k=4)[:, k, :, :], columns(k)).then_inc(attr_cols, 1)
            act.wait_ge(wt_tr, 1)
            nc.scalar.copy(WmT[:, :], B7[:, 0:P])
            nc.scalar.copy(WsT[:, :], B7[:, P:2 * P]).then_inc(wt_used, 1)
            act.wait_ge(attr_cols, 4)
            npass, _ = passes_of(act)
            act.wait_ge(node_ready, 1)
            act.wait_ge(pool_pads, 6)
            for k in range(ABANKS):
                a0 = 7 * k + k % 2
                n = len(range(a0, min(7 * k + 7, NWIN), 2))
                if n:
                    o = nc.scalar.copy(nd[:, a0 + k:a0 + k + 2 * n - 1:2, :], nodeE[:, a0 // 2:a0 // 2 + n, :])
            o.then_inc(even_ready, 1)
            act.wait_ge(wself_in, 1)
            nc.scalar.activation(wself[:, :, :], wself[:, :, :], ACT.Exp).then_inc(wself_ready, 1)
            with act.Fori(0, npass) as ps, act.Fori(0, NIT) as it:
                turn = act.snap(ps * NIT + it)
                for r in range(R):
                    g = turn * R + r
                    e = attrE[:, bass.ds(it * R + r, 1), :].rearrange("p o k -> p (o k)")
                    p = attrS[:, bass.ds(it * R + r, 1), :].rearrange("p o k -> p (o k)")
                    nc.scalar.copy(p[:, 0:16], e).then_inc(part_act, 1)
                    act.wait_ge(t_ready, g + 1)
                    nc.scalar.activation(wr[:, r, :, 0:H], tt[:, r, :, :], ACT.Exp).then_inc(w_ready, 1)
                    act.wait_ge(part_dve, g * 2 + 1)
                    nc.scalar.copy(p[:, 16:32], left[:, :]).then_inc(part_act, 1)
                    act.wait_ge(part_act, g * 2 + 2)
                    nc.scalar.copy(p[:, 48:80], p[:, 0:32]).then_inc(dup_done, 1)
                    nc.scalar.copy(p[:, 80:96], p[:, 0:16]).then_inc(dup_done, 1)

            def normalise(n, dst):
                for h, (b0_, b1_) in enumerate(((0, HNB), (HNB, NB))):
                    act.wait_ge(var_ready, 2 * n - 1 + h)
                    nc.scalar.activation(rstd[:, b0_:b1_], mb[:, b0_:b1_], ACT.Sqrt, bias=eps[:, 0:1], scale=1.0 / F).then_inc(std_ready, 1)
                    act.wait_ge(scale_ready, 2 * n - 1 + h)
                    for b in (ACT1, ACT2)[h]:
                        o = nc.scalar.activation(dst[:, b, :], NX[:, b, :], ACT.Identity, bias=shift[:, b:b + 1], scale=rstd[:, b:b + 1])
                        if b == QNB - 1:
                            o.then_inc(norm_act, 1)
                    o.then_inc(norm_act, 1)

            act.wait_ge(joined, 1)
            for k in range(ABANKS):
                to, at = bank_nodes(k)
                nc.scalar.copy(AG[:, to], PS[:, at]).then_inc(acc_read, 1)
            act.wait_ge(cnt_ready, 1)
            for b in range(NB):
                o = nc.scalar.activation(T1[:, b, :], ident[:, :], ACT.Copy, scale=rc[:, b:b + 1])
            o.then_inc(rc_diag, 1)
            def copy_xt(L):
                for i in range(HBANK, BANKS):
                    act.wait_ge(xt_tr, BANKS * L + i + 1)
                    nc.scalar.copy(XT[:, cols(i)], PS[:, cols(i)]).then_inc(xt_rest, 1)

            normalise(1, X)
            copy_xt(1)
            for i in range(BANKS):
                act.wait_ge(rc_bc, i + 1)
                nc.scalar.copy(rcB[:, cols(i)], PS[:, cols(i)]).then_inc(rc_cp, 1)
            act.wait_ge(part_dve, npass * (NIT * R * 2))
            act.wait_ge(dup_done, npass * (NIT * R * 2))
            act.sem_inc(passed, 1)
            with act.Fori(0, npass) as ps, act.Fori(0, NIT) as it:
                turn = act.snap(ps * NIT + it)
                for r in range(R):
                    g = turn * R + r
                    nc.scalar.copy(ar[:, 0:ATT], attrS[:, bass.ds(it * R + r, 1), :].rearrange("p o k -> p (o k)")).then_inc(attr_cp, 1)
                    act.wait_ge(attr_tr, g + 1)
                    nc.scalar.copy(arT[0:ATK, :], B7[0:ATK, 0:HALF].bitcast(bf16)).then_inc(attr_T, 1)
                    act.wait_ge(hid_mm, g + 1)
                    act.wait_ge(hid_free, g + 1)
                    nc.scalar.activation(hid[:, :, :].rearrange("p u f -> p (u f)"), B7, ACT.Silu).then_inc(hid_act, 1)
            act.wait_ge(hid_free, npass * (NIT * R) + 1)
            nc.scalar.activation(ew[:, :], ew[:, :], ACT.Sigmoid, bias=be2[:, 0:1]).then_inc(ew_ready, 1)
            normalise(2, X)
            copy_xt(2)
            for i in range(BANKS):
                act.wait_ge(mm2_used, i + 1)
                b = blocks(i)
                nc.scalar.activation(T1[:, b[0]:b[-1] + 1, :], NX[:, b[0]:b[-1] + 1, :], ACT.Silu).then_inc(silu2, 1)
            act.wait_ge(table_ready, 16 * len(PIECES) * 3)
            for i in range(BANKS):
                act.wait_ge(upx, i + 1)
                nc.scalar.activation(T1f[:, cols(i)], PS[:, cols(i)], ACT.Identity, bias=bu1[:, 0:1]).then_inc(upx_used, 1)
            for i in range(BANKS):
                act.wait_ge(up1_sum, i + 1)
                nc.scalar.activation(T1f[:, cols(i)], T1f[:, cols(i)], ACT.Silu).then_inc(up1_act, 1)
            normalise(3, T1)
            normalise(4, X)
            copy_xt(3)
            normalise(5, X)

        @block.vector
        def _(dve):
            done = [0]
            V = nc.vector

            def link(instr):
                done[0] += 1
                instr.then_inc(dve_order, 1)
                dve.wait_ge(dve_order, done[0])

            def loose(instr):
                done[0] += 1
                instr.then_inc(dve_order, 1)
                return done[0]

            def settle():
                dve.wait_ge(dve_order, done[0])

            for L in range(2):
                dve.sem_inc(row_free[L], R)
            dve.sem_inc(bank7_free, 1)
            dve.sem_inc(vals_ready[1], 1)
            dve.sem_inc(hid_free, 1)
            V.memset(X[:, NB - 1, :], 0.0).then_inc(padded, 1)
            V.memset(edge_raw[:, 0:3:2, :], 0).then_inc(padded, 1)
            V.memset(edge_raw[:, 1, :], PAD_DST).then_inc(padded, 1)
            loose(V.memset(ones[:, :], 1.0))
            loose(V.memset(S[:, :, :], 0.0))
            loose(V.memset(S1[:, :], 0.0))
            loose(V.memset(pb[:, :], 0.0))
            loose(V.memset(eps[:, :], LN_EPS))
            loose(V.memset(viol[:, :], 0.0))
            dve.wait_ge(iotas, 3)
            loose(V.tensor_copy(iota[:, :], iota_i[:, :]))
            loose(V.tensor_copy(m16[:, :], m16_i[:, :]))
            link(V.tensor_copy(pcol[:, :], pcol_i[:, :]))
            loose(V.memset(S1[:, ATT:ATK], 1.0))
            link(V.tensor_scalar(ident[:, :], iota[:, :], pcol[:, 0:1], None, ALU.is_equal))
            for k in range(4):
                loose(V.tensor_copy(ident4[:, k, :], ident[:, :]))
            loose(V.tensor_copy(swap[:, 0:HALF], ident[:, HALF:P]))
            loose(V.tensor_copy(swap[:, HALF:P], ident[:, 0:HALF]))
            loose(V.tensor_copy(identb[:, :], ident[:, :]))
            link(V.tensor_scalar(ptmp[:, :], pcol[:, :], float(NREL), None, ALU.is_ge))
            loose(V.scalar_tensor_tensor(pmod[:, :], ptmp[:, :], -float(NREL), pcol[:, :], ALU.mult, ALU.add))
            settle()
            dve.sem_inc(consts, 1)

            dve.wait_ge(w0_in, 16 * W0_LOADS)
            for half in range(2):
                v = aw[:, :, 1 - half, :]
                loose(V.tensor_tensor(hv[:, half, :].rearrange("p (h f) -> p h f", h=H), ident[:, :].rearrange("p (h f) -> p h f", h=H), v, ALU.mult))
                loose(V.tensor_tensor(hv[:, 2 + half, :].rearrange("p (h f) -> p h f", h=H), b0[:, 0:F].rearrange("p (h f) -> p h f", h=H), v, ALU.mult))
            settle()
            V.tensor_reduce(A[:, :], hv[:, 0:2, :].rearrange("p t (h f) -> p (t h) f", h=H), AX, ALU.add).then_inc(heads_ready, 1)
            link(V.tensor_reduce(b0[:, F:KW], hv[:, 2:4, :].rearrange("p t (h f) -> p (t h) f", h=H), AX, ALU.add))
            link(V.tensor_tensor(b0[:, F + H:KW], b0[:, F + H:KW], ab[:, :], ALU.add))

            dve.wait_ge(edges_in, 16 * 3 * (1 + (REM > 0)))
            V.tensor_copy(edge_f[0:NG, :, :], edge_raw[0:NG, :, :]).then_inc(edge_cast, 1)
            dve.wait_ge(edge_cast, 1)
            V.tensor_scalar(typ_b[0:NG, :], edge_f[0:NG, 2, :], 0.0, float(NREL - 1), ALU.max, ALU.min).then_inc(lists_ready, 1)
            d4 = edge_f[0:NG, 1, :].rearrange("p (u j) -> p u j", u=U)
            link(V.tensor_reduce(cmin[0:NG, :], d4, AX, ALU.min))
            link(V.tensor_scalar(cmin[0:NG, :], cmin[0:NG, :], float(HALF * (NWIN - 1)), None, ALU.min))
            link(V.tensor_copy(cwin_i[0:NG, :], cmin[0:NG, :]))
            link(V.tensor_single_scalar(cwin_i[0:NG, :], cwin_i[0:NG, :], 6, ALU.arith_shift_right))
            V.tensor_copy(cwin[0:NG, :], cwin_i[0:NG, :]).then_inc(lists_ready, 2)
            dve.wait_ge(lists_ready, 3)
            tmp = T1f[0:NG, 0:GE]
            link(V.scalar_tensor_tensor(tmp, edge_f[0:NG, 1, :], 0.5 * PAD_DST, edge_f[0:NG, 1, :], ALU.is_lt, ALU.mult))
            link(V.tensor_reduce(cmax[0:NG, :], tmp.rearrange("p (u j) -> p u j", u=U), AX, ALU.max))
            link(V.scalar_tensor_tensor(cspan[0:NG, :], cwin[0:NG, :], -float(HALF), cmax[0:NG, :], ALU.mult, ALU.add))
            link(V.tensor_scalar(cspan[0:NG, :], cspan[0:NG, :], float(P), None, ALU.is_ge))
            link(V.tensor_reduce(viol[0:NG, :], cspan[0:NG, :], AX, ALU.max))

            def copy_xt(L):
                for i in range(HBANK):
                    dve.wait_ge(xt_tr, BANKS * L + i + 1)
                    V.tensor_copy(XT[:, cols(i)], PS[:, cols(i)]).then_inc(xt_ready, 1)

            for i in range(KGROUPS):
                if i == KGROUPS - 2:
                    dve.wait_ge(edge_tr, 1)
                    link(V.tensor_copy(srcT[:, 0:NCH].rearrange("p (g u) -> p u g", u=U),
                                       B7.rearrange("p (u g) -> p u g", u=U)[:, :, 0:NG]))
                    V.tensor_copy(srcT[:, NCH:NCH + R * U], srcT[:, 0:R * U]).then_inc(edge_tr_used, 1)
                dve.wait_ge(mm0, i + 1)
                b = range(KB * i, min(KB * (i + 1), NB))
                q = PS[:, i % 7 * 512:i % 7 * 512 + KW * len(b)].rearrange("p (b k) -> p b k", k=KW)
                s = slice(b[0], b[-1] + 1)
                loose(V.tensor_tensor(T0[:, s, :], q[:, :, 0:ROW0], b0[:, 0:ROW0].unsqueeze(1).to_broadcast([P, len(b), ROW0]), ALU.add))
                V.tensor_tensor(sd[:, s, :], q[:, :, ROW0:KW], b0[:, ROW0:KW].unsqueeze(1).to_broadcast([P, len(b), H]), ALU.add).then_inc(mm0_used, 1)
            dve.wait_ge(mm0_used, KGROUPS)
            ss = T0[:, :, F:ROW0]
            link(V.tensor_reduce(ext[:, 0:H], ss.rearrange("p b h -> p h b"), AX, ALU.max))
            link(V.tensor_reduce(ext[:, H:2 * H], ss.rearrange("p b h -> p h b"), AX, ALU.min))
            link(V.tensor_scalar(ext[:, H:2 * H], ext[:, H:2 * H], -1.0, None, ALU.mult))
            dve.sem_inc(ext_ready, 1)
            dve.wait_ge(ext_tr, 1)
            link(V.tensor_reduce(exc[:, :], B7[0:2 * H, 0:P], AX, ALU.max))
            V.tensor_scalar(exq[:, :], ident[0:2 * H, 0:2 * H], exc[:, 0:1], None, ALU.mult).then_inc(ext_diag, 1)
            dve.wait_ge(ext_bc, 1)
            loose(V.tensor_scalar(inside[:, :], B7[:, 8:9], 0.5, None, ALU.is_lt))
            link(V.tensor_copy(exB[:, :], B7[:, 0:2 * H]))
            link(V.tensor_tensor(rng[:, :], exB[:, 0:H], exB[:, H:2 * H], ALU.add))
            link(V.tensor_reduce(rng1[:, :], rng[:, :], AX, ALU.max))
            link(V.scalar_tensor_tensor(isfast[:, :], rng1[:, :], SAFE_RANGE, inside[:, :], ALU.is_le, ALU.mult))
            loose(V.tensor_scalar(npass_f[:, 0:1], isfast[:, :], 1.0 - NB, float(NB), ALU.mult, ALU.add))
            loose(V.tensor_scalar(npass_f[:, 1:2], isfast[:, :], -1.0, 1.0, ALU.mult, ALU.add))
            loose(V.tensor_scalar(pstep[:, :], isfast[:, :], -2.0, 2.0, ALU.mult, ALU.add))
            link(V.tensor_copy(mx[:, :, :], exB[:, 0:H].unsqueeze(1).to_broadcast([P, NB, H])))
            V.tensor_copy(npass_i[:, :], npass_f[:, :]).then_inc(npass_ready, 1)

            def places(ps):
                V.tensor_scalar(cwinc[0:NG, :], cwin[0:NG, :], isfast[0:NG, 0:1], pb[0:NG, 0:1], ALU.mult, ALU.add).then_inc(place_step, 1)
                dve.wait_ge(place_step, ps * 2 + 1)
                r3 = T1f[0:NG, 0:GE].rearrange("p (u j) -> p u j", u=U)
                V.scalar_tensor_tensor(r3, cwinc[0:NG, :].unsqueeze(2).to_broadcast([NG, U, P]), -float(HALF),
                                       edge_f[0:NG, 1, :].rearrange("p (u j) -> p u j", u=U), ALU.mult, ALU.add).then_inc(place_step, 1)
                dve.wait_ge(place_step, ps * 2 + 2)
                V.tensor_scalar(relc[0:NG, :], T1f[0:NG, 0:GE], -1.0, float(P), ALU.max, ALU.min).then_inc(relc_ready, 1)

            places(0)
            dve.wait_ge(dst_cp, 1)
            npass, general = passes_of(dve)
            with dve.If(general == 1):
                V.tensor_copy(mx[:, :, :], ss).then_inc(g_ready, 1)
                V.memset(g_base[:, :], 0.0).then_inc(g_ready, 1)
                dve.wait_ge(g_ready, 2)
                mxf = mx[:, :, :].rearrange("p b h -> p (b h)")
                with dve.Fori(0, NB) as w:
                    with dve.Fori(0, NCH) as c:
                        n = dve.snap(w * NCH + c)
                        V.tensor_copy(g_idx[:, :], srcT[:, bass.ds(c, 1)]).then_inc(g_idx_ready, 1)
                        V.tensor_scalar(g_oh[:, :], iota[:, :], g_base[:, 0:1], dstT[:, bass.ds(c, 1)], ALU.add, ALU.is_equal).then_inc(g_ready, 1)
                        dve.wait_ge(g_ready, n * 8 + w + 3)
                        V.tensor_scalar(g_ohm[:, :], g_oh[:, :], BIG, -BIG, ALU.mult, ALU.add).then_inc(g_ready, 1)
                        dve.wait_ge(g_got, n * 16 + 16)
                        for h in range(H):
                            V.tensor_scalar(g_dg[:, h, :], ident[:, :], g_row[:, F + h:F + h + 1], None, ALU.mult).then_inc(g_ready, 1)
                        dve.wait_ge(g_mm, n + 1)
                        V.tensor_reduce(g_m[:, :], B7.rearrange("p (h e) -> p h e", h=H), AX, ALU.max).then_inc(g_ready, 1)
                        dve.wait_ge(g_ready, n * 8 + w + 9)
                        V.tensor_tensor(mxf[:, bass.ds(w * H, H)], mxf[:, bass.ds(w * H, H)], g_m[:, :], ALU.max).then_inc(g_ready, 1)
                        dve.wait_ge(g_ready, n * 8 + w + 10)
                    V.tensor_scalar(g_base[:, :], g_base[:, :], float(P), None, ALU.add).then_inc(g_ready, 1)
                    dve.wait_ge(g_ready, w * (NCH * 8 + 1) + (NCH * 8 + 3))

            def leaky(dst, src):
                link(V.scalar_tensor_tensor(dst, src, SLOPE, src, ALU.mult, ALU.max))

            link(V.tensor_tensor(zz[:, :, :], sd[:, :, :], mx[:, :, :], ALU.add))
            leaky(nodeE[:, :, H:2 * H], zz[:, :, :])
            link(V.tensor_copy(nodeE[:, :, 0:H], sd[:, :, :]))
            dve.sem_inc(node_ready, 1)
            link(V.tensor_tensor(zz[:, :, :], sd[:, :, :], ss, ALU.add))
            leaky(wself[:, :, :], zz[:, :, :])
            V.tensor_tensor(wself[:, :, :], wself[:, :, :], nodeE[:, :, H:2 * H], ALU.subtract).then_inc(wself_in, 1)
            dve.wait_ge(pool_pads, 6)
            dve.wait_ge(node_sw, 1)
            sw = B7[:, 0:NB * 2 * H].rearrange("p (b k) -> p b k", k=2 * H)
            for k in range(ABANKS):
                for odd in range(2):
                    a0 = 7 * k + (k + odd) % 2
                    a1 = min(7 * k + 7, NWIN)
                    n = len(range(a0, a1, 2))
                    if not n:
                        continue
                    to = nd[:, a0 + k:a0 + k + 2 * n - 1:2, :]
                    if a0 % 2:
                        loose(V.tensor_copy(to[0:HALF], sw[0:HALF, a0 // 2:a0 // 2 + n, :]))
                        loose(V.tensor_copy(to[HALF:P], sw[HALF:P, a0 // 2 + 1:a0 // 2 + 1 + n, :]))
            settle()
            dve.wait_ge(even_ready, 1)
            link(V.tensor_copy(nd3[:, :, 0, :], nd[:, :, :]))
            link(V.tensor_tensor(ndr[:, :, :], nd[:, :, :], nd3[:, :, 0, :], ALU.subtract))
            link(V.tensor_copy(nd3[:, :, 1, :], ndr[:, :, :]))
            link(V.tensor_tensor(nd3[:, :, 2, :], ndr[:, :, :], nd3[:, :, 1, :], ALU.subtract))
            dve.sem_inc(nd_ready, 1)
            dve.wait_ge(lists_in, 16)

            def set_pass(L, ps):
                base = ps * PASS_STEPS
                chain = pass_set[L]
                V.tensor_scalar(winc[:, :], winB[:, :], isfast[:, 0:1], pb[:, 0:1], ALU.mult, ALU.add).then_inc(chain, 1)
                dve.wait_ge(chain, base + 1)
                V.scalar_tensor_tensor(relT[:, :], winc[:, :], -float(HALF), dstT[:, :], ALU.mult, ALU.add).then_inc(chain, 1)
                V.tensor_copy(win_i[:, :], winc[0:1, :]).then_inc(chain, 1)
                V.tensor_tensor(pb[:, :], pb[:, :], pstep[:, :], ALU.add).then_inc(chain, 1)
                dve.wait_ge(chain, base + 4)
                V.tensor_scalar(slot_i[:, :], win_i[:, :], 37.0, None, ALU.mult).then_inc(chain, 1)
                dve.wait_ge(chain, base + 5)
                V.tensor_single_scalar(slot_i[:, :], slot_i[:, :], 8, ALU.arith_shift_right).then_inc(chain, 1)
                dve.wait_ge(chain, base + 6)
                V.tensor_tensor(slot_i[:, :], slot_i[:, :], winc[0:1, :], ALU.add).then_inc(chain, 1)
                dve.wait_ge(chain, base + PASS_STEPS)
                dve.sem_inc(passed, 1)

            def one_hot(L, it, r, weighted=False):
                for u in range(U):
                    c = it * (R * U) + (r * U + u)
                    o = V.tensor_scalar(oh[:, r * U + u, :], iota[:, :], relT[:, bass.ds(c, 1)],
                                        ew[:, bass.ds(c, 1)] if weighted else None,
                                        ALU.is_equal, *([ALU.mult] if weighted else []))
                o.then_inc(oh_ready[L], 1)

            with dve.Fori(0, npass) as ps:
                dve.wait_ge(slot_free[0], ps * (NIT * R) + R)
                set_pass(0, ps)
                def masks(it, r):
                    turn = ps * NIT + it
                    dve.wait_ge(slot_free[0], turn * R + (r + 1))
                    dve.wait_ge(row_in[0][r], turn * 16 + 16)
                    V.tensor_scalar(ohT[:, r, :], rowB[:, r, :], pcol[:, 0:1], None, ALU.is_equal).then_inc(ohT_ready[0], 1)
                    one_hot(0, it, r)
                    dve.wait_ge(ohT_ready[0], turn * R + (r + 1))
                    dve.sem_inc(row_free[0], 1)

                def iteration(it, last):
                    turn = ps * NIT + it
                    for r in range(R):
                        g = turn * R + r
                        dve.wait_ge(got[0][r], turn * (16 * U) + 16 * U)
                        dve.sem_inc(idx_used[0], 1)
                        dve.wait_ge(sd_ready, g + 1)
                        sp_ = B7[:, NDP0:512].rearrange("p (u t k) -> p u k t", u=U, t=3)
                        V.tensor_reduce(dn[:, r, :, :], sp_, AX, ALU.add).then_inc(dn_done, 1)
                        dve.wait_ge(dn_done, g + 1)
                        V.memset(B7[:, NDP0:512], 0.0).then_inc(bank7_free, 1)
                        V.tensor_tensor(z[:, r, :, :], dn[:, r, :, 0:H], vals[:, r * U:(r + 1) * U, F:ROW0], ALU.add).then_inc(z_done, 1)
                        dve.wait_ge(z_done, g + 1)
                        V.scalar_tensor_tensor(lz[:, r, :, :], z[:, r, :, :], SLOPE, z[:, r, :, :], ALU.mult, ALU.max).then_inc(lz_done, 1)
                        dve.wait_ge(lz_done, g + 1)
                        V.tensor_tensor(lz[:, r, :, :], lz[:, r, :, :], dn[:, r, :, H:2 * H], ALU.subtract).then_inc(t_sub, 1)
                        dve.wait_ge(t_sub, g + 1)
                        V.tensor_scalar(tt[:, r, :, :], lz[:, r, :, :], 1.0, None, ALU.min).then_inc(t_ready, 1)
                        e = attrE[:, bass.ds(it * R + r, 1), :].rearrange("p o k -> p (o k)")
                        p = attrS[:, bass.ds(it * R + r, 1), :].rearrange("p o k -> p (o k)")
                        dve.wait_ge(part_act, g * 2 + 1)
                        V.tensor_tensor(left[:, :], e, p[:, 0:16], ALU.subtract).then_inc(part_dve, 1)
                        if r + 1 < R:
                            masks(it, r + 1)
                        elif not last:
                            masks(it + 1, 0)
                        dve.wait_ge(w_ready, g + 1)
                        v = vals[:, r * U:(r + 1) * U, 0:F].rearrange("p u (h f) -> p u h f", h=H)
                        V.tensor_tensor(v, v, wr[:, r, :, 0:H].unsqueeze(3).to_broadcast([P, U, H, FH]), ALU.mult).then_inc(vals_ready[0], 1)
                        dve.wait_ge(part_act, g * 2 + 2)
                        dve.wait_ge(part_dve, g * 2 + 1)
                        V.tensor_tensor(p[:, 32:48], left[:, :], p[:, 16:32], ALU.subtract).then_inc(part_dve, 1)

                masks(0, 0)
                with dve.Fori(0, NIT - 1) as it:
                    iteration(it, False)
                places(ps + 1)
                iteration(NIT - 1, True)

            dve.wait_ge(slot_free[0], npass * (NIT * R) + R)
            dve.wait_ge(wself_ready, 1)
            V.tensor_copy(D[:, :, :].rearrange("p w k -> p (w k)"), DENP).then_inc(den_ready, 1)

            def read_sums(L, op, other):
                hi = PS[:, 0:512 * ABANKS].rearrange("p (k n) -> p k n", n=512)
                link(V.tensor_copy(shared[:, 1:ABANKS, :], hi[:, 1:ABANKS, 0:SHARED]))
                link(V.tensor_tensor(hi[:, 0:ABANKS - 1, STRIDE:512], hi[:, 0:ABANKS - 1, STRIDE:512], shared[:, 1:ABANKS, :], ALU.add))
                dve.sem_inc(joined, 1)
                if op is not None:
                    for k in range(ABANKS):
                        to, at = bank_nodes(k)
                        V.tensor_tensor(AG[:, to], PS[:, at], other[:, to], op).then_inc(acc_read, 1)

            read_sums(0, None, None)
            dve.wait_ge(den_sw, 1)
            sdn = B7[:, 0:NSLOT * DW].rearrange("p (w k) -> p w k", k=DW)
            for k in range(ABANKS):
                a0 = 7 * k + k % 2
                n = len(range(a0, min(7 * k + 7, NWIN), 2))
                if n:
                    loose(V.tensor_copy(den[:, a0 // 2:a0 // 2 + n, :], D[:, a0 + k:a0 + k + 2 * n - 1:2, :]))
            settle()
            for k in range(ABANKS):
                a0 = 7 * k + 1 - k % 2
                n = len(range(a0, min(7 * k + 7, NWIN), 2))
                if n:
                    b0_ = a0 // 2
                    f = sdn[:, a0 + k:a0 + k + 2 * n - 1:2, :]
                    lo, hi = den[0:HALF, b0_ + 1:b0_ + 1 + n, :], den[HALF:P, b0_:b0_ + n, :]
                    loose(V.tensor_tensor(lo, lo, f[0:HALF], ALU.add))
                    loose(V.tensor_tensor(hi, hi, f[HALF:P], ALU.add))
            settle()
            link(V.tensor_tensor(rden[:, :, :], den[:, :, 0:H], wself[:, :, :], ALU.add))
            link(V.reciprocal(rden[:, :, :], rden[:, :, :]))
            link(V.tensor_scalar(rc[:, :], den[:, :, H], 1.0, None, ALU.max))
            loose(V.tensor_scalar(cnt[:, :], den[:, :, H], 1.0, None, ALU.min))
            link(V.reciprocal(rc[:, :], rc[:, :]))
            dve.sem_inc(cnt_ready, 1)

            def psum4(i):
                return PS[:, cols(i)].rearrange("p (b f) -> p b f", f=F)

            norms = [0]

            def pipeline(steps, between):
                marks, due = {}, []
                for t in range(BANKS + len(steps) - 1):
                    for k in reversed(range(len(steps))):
                        i = t - k
                        if 0 <= i < BANKS:
                            if k and marks[i, k - 1]:
                                dve.wait_ge(dve_order, marks[i, k - 1])
                            marks[i, k] = steps[k](i)
                            if k == len(steps) - 1:
                                due += between.get(i, [])
                            if due:
                                due.pop(0)()

            def stats(i):
                for b in blocks(i):
                    m = loose(V.bn_stats(st[:, b, :], NX[:, b, :]))
                return m

            def normalise(dst, *steps):
                norms[0] += 1
                n = norms[0]

                def apply(some):
                    for b in some:
                        o = V.tensor_scalar(dst[:, b, :], NX[:, b, :], rstd[:, b:b + 1], shift[:, b:b + 1], ALU.mult, ALU.add)
                    o.then_inc(norm_dve, 1)

                def variance(h):
                    s = slice(HNB * h, (HNB, NB)[h])
                    settle()
                    loose(V.tensor_tensor(ma[:, s], st[:, s, 1], st[:, s, 4], ALU.subtract))
                    loose(V.tensor_tensor(mean2[:, s], st[:, s, 1], st[:, s, 4], ALU.add))
                    loose(V.tensor_tensor(mb[:, s], st[:, s, 2], st[:, s, 5], ALU.add))
                    settle()
                    link(V.tensor_tensor(ma[:, s], ma[:, s], ma[:, s], ALU.mult))
                    V.scalar_tensor_tensor(mb[:, s], ma[:, s], 0.25 * F, mb[:, s], ALU.mult, ALU.add).then_inc(var_ready, 1)

                def scale(h):
                    s = slice(HNB * h, (HNB, NB)[h])
                    dve.wait_ge(std_ready, 2 * n - 1 + h)
                    link(V.reciprocal(rstd[:, s], rstd[:, s]))
                    V.scalar_tensor_tensor(shift[:, s], mean2[:, s], -0.5, rstd[:, s], ALU.mult, ALU.mult).then_inc(scale_ready, 1)

                pipeline(steps, {HBANK - 1: [lambda: variance(0), lambda: scale(0)]})
                variance(1)
                dve.wait_ge(scale_ready, 2 * n - 1)
                apply(range(ACT1[-1] + 1, HNB))
                scale(1)
                dve.wait_ge(scale_ready, 2 * n)
                apply(range(HNB, ACT2[0]))

            def add_own(i):
                dve.wait_ge(back, i + 1)
                return loose(V.tensor_tensor(NX[:, nodes(i), :], psum4(i), NX[:, nodes(i), :], ALU.add))

            def divide(i):
                h4 = NX[:, nodes(i), :].rearrange("p b (h f) -> p b h f", h=H)
                V.tensor_tensor(h4, h4, rden[:, nodes(i), :].unsqueeze(3).to_broadcast([P, len(blocks(i)), H, FH]), ALU.mult).then_inc(div_done, 1)

            def pause(i):
                pass

            def stats_after(sem_):
                def step(i):
                    dve.wait_ge(sem_, i + 1)
                    return stats(i)
                return step

            dve.wait_ge(wk_ready, 1)
            normalise(X, add_own, divide, pause, stats_after(x_added))

            copy_xt(1)

            for u in range(U):
                V.tensor_scalar(S[:, u, 0:ATT], m16[:, 0:ATT], -4.0 * u, pcol[0:4, 0:1], ALU.add, ALU.is_equal).then_inc(sel_ready, 1)
            for k, n in enumerate((48, 80, 96)):
                loose(V.tensor_scalar(psel[:, k:k + 1], pcol[:, :], float(n), None, ALU.is_lt))
            settle()
            link(V.tensor_tensor(psel[:, 2:3], psel[:, 2:3], psel[:, 1:2], ALU.subtract))
            link(V.tensor_tensor(psel[:, 1:2], psel[:, 1:2], psel[:, 0:1], ALU.subtract))
            for k in range(3):
                loose(V.scalar_tensor_tensor(psel[:, k:k + 1], pcol[:, :], float(ATT + k), psel[:, k:k + 1], ALU.is_equal, ALU.add))

            def two_parts(src, p1, p2):
                link(V.tensor_copy(p1, src))
                link(V.tensor_tensor(src, src, p1, ALU.subtract))
                link(V.tensor_copy(p2, src))
                link(V.tensor_tensor(src, src, p2, ALU.subtract))

            dve.wait_ge(we1_mm, 1)
            link(V.tensor_copy(We1, B7))
            two_parts(We1, ohT[:, 0, :], ohT[:, 1, :])
            link(V.tensor_scalar(We1b[:, :], ohT[:, 0, :], psel[:, 0:1], None, ALU.mult))
            link(V.scalar_tensor_tensor(We1b[:, :], ohT[:, 1, :], psel[:, 1:2], We1b[:, :], ALU.mult, ALU.add))
            link(V.scalar_tensor_tensor(We1b[:, :], We1, psel[:, 2:3], We1b[:, :], ALU.mult, ALU.add))
            two_parts(rel[:, :], ohT[:, 0, 0:F], ohT[:, 1, 0:F])
            loose(V.memset(relb[NREL:P, 1, :], 0.0))
            loose(V.tensor_copy(relb[0:NREL, 0, :], ohT[0:NREL, 0, 0:F]))
            loose(V.tensor_copy(relb[NREL:P, 0, :], ohT[NREL:P, 1, 0:F]))
            link(V.tensor_copy(relb[0:NREL, 1, :], rel[0:NREL, :]))
            dve.sem_inc(parts_ready, 1)

            def plain_loop(L):
                with dve.Fori(0, npass) as ps:
                    dve.wait_ge(slot_free[L], ps * (NIT * R) + R)
                    set_pass(L, ps)
                    with dve.Fori(0, NIT) as it:
                        turn = dve.snap(ps * NIT + it)
                        for r in range(R):
                            dve.wait_ge(slot_free[L], turn * R + (r + 1))
                            one_hot(L, it, r, weighted=L == 2)

            def reset_pass():
                link(V.memset(pb[:, :], 0.0))

            reset_pass()
            with dve.Fori(0, npass) as ps:
                dve.wait_ge(slot_free[1], ps * (NIT * R) + R)
                set_pass(1, ps)

                def masks1(it, r):
                    dve.wait_ge(slot_free[1], (ps * NIT + it) * R + (r + 1))
                    one_hot(1, it, r)

                def iteration1(it, last):
                    for r in range(R):
                        g = (ps * NIT + it) * R + r
                        if r + 1 < R:
                            masks1(it, r + 1)
                        elif not last:
                            masks1(it + 1, 0)
                        dve.wait_ge(hid_act, g + 1)
                        V.tensor_tensor(hid[:, :, :], hid[:, :, :], We2[:, :].unsqueeze(1).to_broadcast([P, U, F]), ALU.mult).then_inc(prod_done, 1)
                        dve.wait_ge(prod_done, g + 1)
                        V.tensor_reduce(ew[:, bass.ds(it * (R * U) + r * U, U)], hid[:, :, :], AX, ALU.add).then_inc(hid_free, 1)

                masks1(0, 0)
                with dve.Fori(0, NIT - 1) as it:
                    iteration1(it, False)
                iteration1(NIT - 1, True)
            dve.wait_ge(slot_free[1], npass * (NIT * R) + R)
            read_sums(1, ALU.add, XT)

            def relu_add(i):
                dve.wait_ge(post1, i + 1)
                return loose(V.scalar_tensor_tensor(NX[:, nodes(i), :], psum4(i), 0.0, X[:, nodes(i), :], ALU.max, ALU.add))

            normalise(X, relu_add, stats)

            copy_xt(2)
            for i in range(BANKS):
                b = blocks(i)
                s = slice(b[0], b[-1] + 1)
                dve.wait_ge(mm2, i + 1)
                V.tensor_tensor(NX[:, s, :], psum4(i), bagg[:, :].unsqueeze(1).to_broadcast([P, len(b), F]), ALU.add).then_inc(mm2_used, 1)
            for i in range(BANKS):
                dve.wait_ge(silu2, i + 1)
                dve.wait_ge(xr, i + 1)
                V.tensor_tensor(NX[:, nodes(i), :], psum4(i), bu2[:, :].unsqueeze(1).to_broadcast([P, len(blocks(i)), F]), ALU.add).then_inc(xr_used, 1)
            dve.wait_ge(xr_used, BANKS)
            loose(V.tensor_tensor(X[:, :, :], X[:, :, :], lnb[:, :].unsqueeze(1).to_broadcast([P, NB, F]), ALU.add))
            dve.wait_ge(ew_ready, 1)
            reset_pass()
            plain_loop(2)
            dve.wait_ge(slot_free[2], npass * (NIT * R) + R)
            read_sums(2, ALU.mult, rcB)
            def hidden_sum(i):
                dve.wait_ge(up1, i + 1)
                V.tensor_tensor(T1f[:, cols(i)], PS[:, cols(i)], T1f[:, cols(i)], ALU.add).then_inc(up1_sum, 1)

            def hidden_ahead(i):
                for k in range(i + 2, BANKS if i == HBANK - 1 else i + 3):
                    if i < HBANK:
                        hidden_sum(k)

            def add_update(i):
                dve.wait_ge(up2, i + 1)
                return loose(V.tensor_tensor(NX[:, nodes(i), :], psum4(i), NX[:, nodes(i), :], ALU.add))

            for i in range(2):
                hidden_sum(i)
            normalise(T1, hidden_ahead, add_update, stats)

            def add_xb(i):
                dve.wait_ge(g_done, i + 1)
                return loose(V.tensor_tensor(NX[:, nodes(i), :], T1[:, nodes(i), :], X[:, nodes(i), :], ALU.add))

            normalise(X, add_xb, stats)

            copy_xt(3)
            dve.wait_ge(bias3_step, 2)
            norm_wait(dve, 4)

            def self_part(i):
                dve.wait_ge(xr, BANKS + i + 1)
                V.tensor_tensor(NX[:, nodes(i), :], psum4(i), bias3[:, nodes(i), :], ALU.add).then_inc(xr_used, 1)

            for i in range(BANKS):
                self_part(i)
            dve.wait_ge(xr_used, 2 * BANKS)
            loose(V.tensor_tensor(NX[:, :, :], NX[:, :, :], X[:, :, :], ALU.add))
            reset_pass()
            with dve.Fori(0, npass) as ps:
                dve.wait_ge(slot_free[3], ps * (NIT * R) + R)
                set_pass(3, ps)
                def masks3(it, r):
                    turn = ps * NIT + it
                    dve.wait_ge(slot_free[3], turn * R + (r + 1))
                    dve.wait_ge(row_in[1][r], turn * 16 + 16)
                    V.tensor_scalar(ohT[:, r, :], rowB[:, r, :], pmod[:, 0:1], None, ALU.is_equal).then_inc(ohT_ready[1], 1)
                    one_hot(3, it, r)
                    dve.wait_ge(ohT_ready[1], turn * R + (r + 1))
                    dve.sem_inc(row_free[1], 1)

                def iteration3(it, last):
                    turn = ps * NIT + it
                    for r in range(R):
                        if r + 1 < R:
                            masks3(it, r + 1)
                        elif not last:
                            masks3(it + 1, 0)
                        dve.wait_ge(got[3][r], turn * (16 * U) + 16 * U)
                        dve.sem_inc(idx_used[3], 1)
                        dve.wait_ge(rel_ready, turn * R + (r + 1))
                        v = vals[:, r * U:(r + 1) * U, 0:F]
                        V.tensor_tensor(v, v, B7.rearrange("p (u f) -> p u f", u=U), ALU.add).then_inc(vals_ready[1], 1)

                masks3(0, 0)
                with dve.Fori(0, NIT - 1) as it:
                    iteration3(it, False)
                iteration3(NIT - 1, True)
            dve.wait_ge(slot_free[3], npass * (NIT * R) + R)
            read_sums(3, ALU.mult, rcB)
            def add_message(i):
                dve.wait_ge(post3, i + 1)
                return loose(V.tensor_tensor(NX[:, nodes(i), :], psum4(i), NX[:, nodes(i), :], ALU.add))

            normalise(X, add_message, stats)

        @block.tensor
        def _(pe):
            T = nc.tensor
            for L in range(4):
                pe.sem_inc(slot_free[L], R)
            pe.wait_ge(consts, 1)

            def x_transposed(L):
                n = {0: 0, 1: 1, 2: 2, 3: 4}[L]
                for i in range(BANKS):
                    if n == 0 and i == 0:
                        pe.wait_ge(x_first, 16)
                    elif n == 0 and i == HBANK:
                        pe.wait_ge(x_in, 16 * 2)
                    elif n and i in (0, QBANK, HBANK):
                        norm_wait(pe, n, piece_of(i))
                    for b in blocks(i):
                        o = T.transpose(PS[:, b * P:(b + 1) * P], X[:, b, :], ident[:, :])
                    o.then_inc(xt_tr, 1)

            def sums_wait(L, i):
                pe.wait_ge(acc_read, ABANKS * L + min(i + 2, ABANKS))

            def dense(dst_sem, wait, terms):
                for i in range(BANKS):
                    wait(i)
                    for b in blocks(i):
                        for k, (lhs, rhs) in enumerate(terms):
                            o = T.matmul(PS[:, b * P:(b + 1) * P], lhs[:, b * P:(b + 1) * P], rhs,
                                         start=k == 0, stop=k == len(terms) - 1)
                    o.then_inc(dst_sem, 1)

            def zero_banks(first=0, end=7):
                for i in range(first, end):
                    T.matmul(PS[:, i * 512:(i + 1) * 512], zeros[0:1, 0:P], zeros[0:1, :], start=True, stop=False, skip_group_check=True)

            pe.wait_ge(w0_in, 16 * W0_LOADS)
            T.transpose(B7[:, 0:F], W0[:, 0:F], ident[:, :]).then_inc(w0_tr, 1)
            pe.wait_ge(w0_cp, 1)
            pe.wait_ge(heads_ready, 1)
            T.matmul(B7[:, 0:2 * H], W0T, A[:, :], start=True, stop=True).then_inc(w0_tr, 1)
            x_transposed(0)

            def list_columns(k, bank):
                for u in range(U):
                    o = T.transpose(PS[:, bank * 512 + u * P:bank * 512 + u * P + NG], edge_f[0:NG, k, u * P:(u + 1) * P], ident[0:NG, 0:NG])
                o.then_inc(edge_tr, 1)

            pe.wait_ge(w0_cp, 2)
            for i in range(KGROUPS):
                if i == KGROUPS - 4:
                    pe.wait_ge(edge_cast, 1)
                    list_columns(0, 7)
                b = range(KB * i, min(KB * (i + 1), NB))
                pe.wait_ge(xt_ready, max(b[-1] // 4, min(i, BANKS - 1)) + 1)
                if i >= 7:
                    pe.wait_ge(mm0_used, i - 6)
                for k, n in enumerate(b):
                    o = T.matmul(PS[:, i % 7 * 512 + k * KW:i % 7 * 512 + (k + 1) * KW], XT[:, n * P:(n + 1) * P], W0[:, :], start=True, stop=True)
                o.then_inc(mm0, 1)
            pe.wait_ge(edge_tr_used, 1)
            list_columns(1, 7)
            pe.wait_ge(dst_cp, 1)
            pe.wait_ge(ext_ready, 1)
            T.transpose(B7[0:2 * H, 0:P], ext[:, :], ident[:, :]).then_inc(ext_tr, 1)
            pe.wait_ge(ext_diag, 1)
            T.matmul(B7[:, 0:2 * H], ones[0:2 * H, :], exq[:, :], start=True, stop=True)
            T.matmul(B7[:, 2 * H:2 * H + 1], ones[:, :], viol[:, :], start=True, stop=True).then_inc(ext_bc, 1)
            pe.wait_ge(mm0_used, KGROUPS)
            pe.wait_ge(attr_in, 16 * (1 + (REM > 0)))
            av = attr[:, :].rearrange("p (u j k) -> p u k j", u=U, k=4)
            for k in range(4):
                for u in range(U):
                    o = T.transpose(PS[:, k * 512 + u * P:k * 512 + u * P + NG], av[0:NG, u, k, :], ident[0:NG, 0:NG])
                o.then_inc(edge_tr, 1)
            pe.wait_ge(npass_ready, 1)
            pe.wait_ge(w_in, 16 * W_LOADS)
            T.transpose(B7[:, 0:P], Wmr[:, :], ident[:, :])
            T.transpose(B7[:, P:2 * P], Wsr[:, :], ident[:, :]).then_inc(wt_tr, 1)
            pe.wait_ge(wt_used, 1)
            npass, general = passes_of(pe)
            with pe.If(general == 1):
                with pe.Fori(0, NB) as w, pe.Fori(0, NCH) as c:
                    n = pe.snap(w * NCH + c)
                    pe.wait_ge(g_ready, n * 8 + w + 8)
                    T.matmul(B7, g_oh[:, :], g_dg[:, :, :].rearrange("p h e -> p (h e)"), start=True, stop=False)
                    T.matmul(B7, g_ohm[:, :], ident4[:, :, :].rearrange("p h e -> p (h e)"), start=False, stop=True).then_inc(g_mm, 1)
            pe.wait_ge(node_ready, 1)
            T.matmul(B7[:, 0:NB * 2 * H], swap[:, :], nodeE[:, :, :].rearrange("p b k -> p (b k)"), start=True, stop=True).then_inc(node_sw, 1)
            pe.wait_ge(attr_cols, 4)
            pe.wait_ge(pool_pads, 6)
            zero_banks()
            pe.wait_ge(nd_ready, 1)
            zero_banks(7, 8)
            ndf = nd3[:, :, :, :].rearrange("p w t k -> p (w t k)")

            def slots(it, more=0):
                n = (R + more) * U
                _, v = nc.values_load_multi_w_load_instructions(
                    slot_i[0:1, bass.ds(it * (R * U), n)], engines=[mybir.EngineType.PE], min_val=0, max_val=NSLOT - 1,
                    skip_runtime_bounds_check_because="set_pass() bounds them")
                return [v[r * U:(r + 1) * U] for r in range(R + more)]

            def scatter(r, u, w):
                s = r * U + u
                return T.matmul(PS[:, bass.ds(w * HALF, P)], vals[:, s, 0:F], oh[:, s, :],
                                start=False, stop=False, skip_group_check=True)

            with pe.Fori(0, npass) as ps:
                pe.wait_ge(pass_set[0], ps * PASS_STEPS + PASS_STEPS)
                pe.sem_inc(passed, 1)

                def fetch(it, r, wins):
                    g = (ps * NIT + it) * R + r
                    pe.wait_ge(ohT_ready[0], g + 1)
                    pe.wait_ge(bank7_free, g + 1)
                    for u in range(U):
                        o = T.matmul(B7[:, NDP0 + u * NDP:NDP0 + (u + 1) * NDP], ohT[:, r % R, u * P:(u + 1) * P],
                                     ndf[:, bass.ds(wins[u] * NDP, NDP)], start=False, stop=False, skip_group_check=True)
                    o.then_inc(sd_ready, 1)

                def iteration(it, last):
                    wins = slots(it, 0 if last else 1)
                    for r in range(R):
                        g = (ps * NIT + it) * R + r
                        ahead = r + 1 < R or not last
                        if ahead:
                            fetch(it, r + 1, wins[r + 1])
                        pe.wait_ge(oh_ready[0], g + 1)
                        pe.wait_ge(vals_ready[0], g + 1)
                        for u in range(U):
                            scatter(r, u, wins[r][u])
                        pe.wait_ge(bank7_free, g + (3 if ahead else 2))
                        for u in range(U):
                            o = T.matmul(DENP[:, bass.ds(wins[r][u] * DW, DW)], oh[:, r * U + u, :], wr[:, r, u, :],
                                         start=False, stop=False, skip_group_check=True)
                        o.then_inc(slot_free[0], 1)

                fetch(0, 0, slots(0)[0])
                with pe.Fori(0, NIT - 1) as it:
                    iteration(it, False)
                iteration(NIT - 1, True)
            pe.wait_ge(den_ready, 1)
            pe.wait_ge(t_ready, npass * (NIT * R))
            T.matmul(B7[:, 0:NSLOT * DW], swap[:, :], D[:, :, :].rearrange("p w k -> p (w k)"), start=True, stop=True).then_inc(den_sw, 1)
            for i in range(BANKS):
                sums_wait(0, i)
                for b in blocks(i):
                    o = T.transpose(PS[:, b * P:(b + 1) * P], AG[:, b * P:(b + 1) * P], ident[:, :])
                o.then_inc(back, 1)

            x_transposed(1)
            pe.wait_ge(sel_ready, U)
            for u in range(U):
                T.matmul(B7[:, u * F:(u + 1) * F], S[:, u, :], eW1[:, :], start=True, stop=False)
                o = T.matmul(B7[:, u * F:(u + 1) * F], S1[:, :], eb1[:, :], start=False, stop=True)
            o.then_inc(we1_mm, 1)
            pe.wait_ge(rc_diag, 1)
            xt_wait(pe, 1, HBANK - 1)
            xt_wait(pe, 1, BANKS - 1)
            for i in range(BANKS):
                for b in blocks(i):
                    o = T.matmul(PS[:, b * P:(b + 1) * P], ones[:, :], T1[:, b, :], start=True, stop=True)
                o.then_inc(rc_bc, 1)
            pe.wait_ge(rc_cp, BANKS)
            zero_banks()
            pe.wait_ge(parts_ready, 1)
            with pe.Fori(0, npass) as ps:
                pe.wait_ge(pass_set[1], ps * PASS_STEPS + PASS_STEPS)
                pe.sem_inc(passed, 1)
                with pe.Fori(0, NIT) as it:
                    turn = pe.snap(ps * NIT + it)
                    wins = slots(it)
                    for r in range(R):
                        g = turn * R + r
                        pe.wait_ge(attr_cp, g + 1)
                        T.transpose(B7[:, 0:HALF].bitcast(bf16), ar[:, :], identb[:, :]).then_inc(attr_tr, 1)
                        pe.wait_ge(oh_ready[1], g + 1)
                        pe.wait_ge(got[1][r], turn * (16 * U) + 16 * U)
                        pe.sem_inc(idx_used[1], 1)
                        scatter(r, 0, wins[r][0])
                        pe.wait_ge(attr_T, g + 1)
                        T.matmul(B7, arT[0:ATK, :], We1b[0:ATK, :], start=True, stop=True).then_inc(hid_mm, 1)
                        for u in range(1, U):
                            o = scatter(r, u, wins[r][u])
                        o.then_inc(slot_free[1], 1)
            dense(post1, lambda i: sums_wait(1, i), [(AG, W1[:, :])])

            x_transposed(2)
            dense(mm2, lambda i: xt_wait(pe, 2, i), [(XT, Wagg[:, :])])
            dense(xr, lambda i: pe.wait_ge(mm2_used, i + 1), [(XT, Wres[:, :])])
            for i in range(BANKS):
                pe.wait_ge(xr_used, i + 1)
                T.matmul(PS[:, cols(i)], Wu1[:, 0, :], XT[:, cols(i)], start=True, stop=True).then_inc(upx, 1)
            pe.wait_ge(upx_used, BANKS)
            zero_banks()

            with pe.Fori(0, npass) as ps:
                pe.wait_ge(pass_set[2], ps * PASS_STEPS + PASS_STEPS)
                pe.sem_inc(passed, 1)
                with pe.Fori(0, NIT) as it:
                    turn = pe.snap(ps * NIT + it)
                    wins = slots(it)
                    for r in range(R):
                        pe.wait_ge(oh_ready[2], turn * R + (r + 1))
                        pe.wait_ge(got[2][r], turn * (16 * U) + 16 * U)
                        pe.sem_inc(idx_used[2], 1)
                        for u in range(U):
                            o = scatter(r, u, wins[r][u])
                        o.then_inc(slot_free[2], 1)
            def hidden(i):
                sums_wait(2, i)
                T.matmul(PS[:, cols(i)], Wu1[:, 1, :], AG[:, cols(i)], start=True, stop=True).then_inc(up1, 1)

            for i in range(2):
                hidden(i)
            for i in range(BANKS):
                if i + 2 < BANKS:
                    hidden(i + 2)
                pe.wait_ge(up1_act, i + 1)
                for b in blocks(i):
                    o = T.matmul(PS[:, b * P:(b + 1) * P], T1f[:, b * P:(b + 1) * P], Wu2[:, :], start=True, stop=True)
                o.then_inc(up2, 1)

            x_transposed(3)
            dense(xr, lambda i: xt_wait(pe, 3, i), [(XT, WsT[:, :])])
            pe.wait_ge(xr_used, 2 * BANKS)
            zero_banks()
            pe.wait_ge(ew_ready, 1)
            pe.sem_inc(passed, 1)
            with pe.Fori(0, npass) as ps:
                pe.wait_ge(pass_set[3], ps * PASS_STEPS + PASS_STEPS)
                pe.sem_inc(passed, 1)
                def relations(turn, r):
                    pe.wait_ge(ohT_ready[1], turn * R + (r + 1))
                    pe.wait_ge(vals_ready[1], turn * R + (r + 1))
                    for u in range(U):
                        for k in range(2):
                            o = T.matmul(B7[:, u * F:(u + 1) * F], ohT[:, r % R, u * P:(u + 1) * P], relb[:, k, :], start=k == 0, stop=k == 1)
                    o.then_inc(rel_ready, 1)

                def iteration3(it, last):
                    turn = pe.snap(ps * NIT + it)
                    wins = slots(it)
                    for r in range(R):
                        if r + 1 < R or not last:
                            relations(turn, r + 1)
                        else:
                            pe.wait_ge(vals_ready[1], turn * R + (r + 2))
                        pe.wait_ge(oh_ready[3], turn * R + (r + 1))
                        for u in range(U):
                            o = scatter(r, u, wins[r][u])
                        o.then_inc(slot_free[3], 1)

                relations(pe.snap(ps * NIT), 0)
                with pe.Fori(0, NIT - 1) as it:
                    iteration3(it, False)
                iteration3(NIT - 1, True)
            dense(post3, lambda i: sums_wait(3, i), [(AG, WmT[:, :])])


_INS = {'x': 'x', 'src': 'src', 'dst': 'dst', 'attr': 'edge_attr_4', 'typ': 'edge_type_64',
        'W_w': 'L0_gnn_W_w', 'W_b': 'L0_gnn_W_b', 'a_w': 'L0_gnn_a_w', 'a_b': 'L0_gnn_a_b', 'W1': 'L1_gnn_W',
        'agg_W': 'L2_gnn_agg_W', 'agg_b': 'L2_gnn_agg_b', 'edge_W1': 'L2_gnn_edge_W1', 'edge_b1': 'L2_gnn_edge_b1',
        'edge_W2': 'L2_gnn_edge_W2', 'edge_b2': 'L2_gnn_edge_b2', 'upd_W1': 'L2_gnn_upd_W1',
        'upd_b1': 'L2_gnn_upd_b1', 'upd_W2': 'L2_gnn_upd_W2', 'upd_b2': 'L2_gnn_upd_b2', 'ln_g': 'L2_gnn_ln_g',
        'ln_b': 'L2_gnn_ln_b', 'res_W': 'L2_gnn_res_W', 'W_self': 'L3_gnn_W_self', 'b_self': 'L3_gnn_b_self',
        'W_msg': 'L3_gnn_W_msg', 'b_msg': 'L3_gnn_b_msg', 'rel_emb': 'L3_gnn_rel_emb'}


def kernel(**inputs):
    import numpy as _np
    import concourse.bacc as _bacc
    from concourse import mybir as _mybir
    from concourse.bass_utils import run_bass_kernel_spmd as _run

    nc = _bacc.Bacc("TRN2", target_bir_lowering=False, num_devices=1)
    arrays, args = {}, {}
    for short, name in _INS.items():
        a = _np.ascontiguousarray(inputs[name])
        arrays[f"in_{name}"] = a
        args[short] = nc.dram_tensor(f"in_{name}", a.shape, _mybir.dt.from_np(a.dtype), kind="ExternalInput").ap()
    shape = inputs["x"].shape
    out = nc.dram_tensor("out", shape, _mybir.dt.float32, kind="ExternalOutput").ap()
    gnn_kernel(nc, args, out)
    return _run(nc, [arrays], core_ids=[0]).results[0]["out"]
```
